# Optimizing a Trainium2 kernel written in Bass

```python
import numpy as np
import jax
import jax.numpy as jnp

def _softmax(x, axis=-1):
    return jax.nn.softmax(x, axis=axis)

def _gelu(x):
    return jax.nn.gelu(x, approximate=True)

def _silu(x):
    return jax.nn.silu(x)

def _sigmoid(x):
    return jax.nn.sigmoid(x)

def _layernorm(x, axis=-1, eps=1e-05):
    m = jnp.mean(x, axis=axis, keepdims=True)
    v = jnp.var(x, axis=axis, keepdims=True)
    return (x - m) / jnp.sqrt(v + eps)

def _scatter_add(tgt, idx, src, axis=0):
    return tgt.at[idx].add(src)

def _segment_sum(src, seg, n):
    return jax.ops.segment_sum(src, seg, n)
kernel_name = 'mk_audio_tower_d2_tok_audfeat256_r4_0c0dd4'

def setup_inputs(seed: int=0):
    np.random.seed(seed)
    _w = jnp.asarray

    def _rec_inputs():
        import jax
        import jax.numpy as jnp
        _rk = jax.random.key(seed)
        x = -0.000392918 + 0.999932 * jax.random.normal(jax.random.fold_in(_rk, 1), (64, 375, 16), jnp.float32)
        return x
    x = _rec_inputs()

    def _L0_tok_setup():
        import jax, jax.numpy as jnp
        import numpy as np
        PATCH = 16
        STRIDE = 8
        EPS = 1e-05
        key = jax.random.key(seed)
        k1, k2, k3 = jax.random.split(key, 3)
        B, S, F, D = (128, 2048, 16, 64)
        in_dim = F * PATCH
        x = jax.random.normal(k1, (B, S, F), dtype=jnp.float32)
        bound = 1.0 / np.sqrt(in_dim)
        W = jax.random.uniform(k2, (D, in_dim), minval=-bound, maxval=bound, dtype=jnp.float32)
        b = jax.random.uniform(k3, (D,), minval=-bound, maxval=bound, dtype=jnp.float32)
        gamma = jnp.ones((D,), dtype=jnp.float32)
        beta = jnp.zeros((D,), dtype=jnp.float32)
        return {'x': x, 'W': W, 'b': b, 'gamma': gamma, 'beta': beta}
    _L0_tok_all = _L0_tok_setup()
    _L0_tok_in = {k: v for k, v in _L0_tok_all.items() if k in ('W', 'b', 'gamma', 'beta')}
    del _L0_tok_all

    def _L0_attn_setup():
        import jax, jax.numpy as jnp
        import numpy as np
        B, S, H = (2, 1024, 64)
        NH, NKV = (8, 4)
        HD = H // NH
        GROUPS = NH // NKV
        ROPE_BASE = 10000.0

        def _rope_cos_sin(seq_len, dim, dtype):
            inv_freq = 1.0 / ROPE_BASE ** (jnp.arange(0, dim, 2, dtype=jnp.float32) / dim)
            t = jnp.arange(seq_len, dtype=jnp.float32)
            freqs = jnp.outer(t, inv_freq)
            emb = jnp.concatenate([freqs, freqs], -1)
            return (jnp.cos(emb).astype(dtype), jnp.sin(emb).astype(dtype))

        def _rotate_half(x):
            x1, x2 = jnp.split(x, 2, axis=-1)
            return jnp.concatenate([-x2, x1], axis=-1)
        key = jax.random.key(seed)
        k0, k1, k2, k3, k4 = jax.random.split(key, 5)
        return {'hidden_states': jax.random.normal(k0, (B, S, H), jnp.float32), 'Wq': jax.random.normal(k1, (H, H), jnp.float32) * 0.02, 'Wk': jax.random.normal(k2, (NKV * HD, H), jnp.float32) * 0.02, 'Wv': jax.random.normal(k3, (NKV * HD, H), jnp.float32) * 0.02, 'Wo': jax.random.normal(k4, (H, H), jnp.float32) * 0.02}
    _L0_attn_all = _L0_attn_setup()
    _L0_attn_in = {k: v for k, v in _L0_attn_all.items() if k in ('Wq', 'Wk', 'Wv', 'Wo')}
    del _L0_attn_all

    def _L0_ffn_setup():
        import jax, jax.numpy as jnp
        import numpy as np
        B, T, D, H, E = (16, 1024, 64, 128, 8)
        key = jax.random.key(seed)
        ks = jax.random.split(key, 5)
        x = jax.random.normal(ks[0], (B, T, D), dtype=jnp.float32)
        gate_w = jax.random.normal(ks[1], (D, E), dtype=jnp.float32) * 0.02
        gate_b = jnp.zeros((E,), dtype=jnp.float32)
        W1 = jax.random.normal(ks[2], (E, D, H), dtype=jnp.float32) * 0.02
        b1 = jnp.zeros((E, H), dtype=jnp.float32)
        W2 = jax.random.normal(ks[3], (E, H, D), dtype=jnp.float32) * 0.02
        b2 = jnp.zeros((E, D), dtype=jnp.float32)
        return {'x': x, 'gate_w': gate_w, 'gate_b': gate_b, 'W1': W1, 'b1': b1, 'W2': W2, 'b2': b2}
    _L0_ffn_all = _L0_ffn_setup()
    _L0_ffn_in = {k: v for k, v in _L0_ffn_all.items() if k in ('gate_w', 'gate_b', 'W1', 'b1', 'W2', 'b2')}
    del _L0_ffn_all

    def _L1_attn_setup():
        import jax, jax.numpy as jnp
        import numpy as np
        B, T, D = (4, 512, 64)
        W_LORA, A_LORA, G_LORA = (64, 64, 128)
        DECAY_SCALE = -0.6065306597126334
        EPS = D * 1e-05

        def _forward(x, x_mix, W_r, W_k, W_v, W_o, A_w, B_w, b_w, A_a, B_a, b_a, A_g, B_g, k_k, k_a, r_k, gn_w, gn_b):
            b, t, d = x.shape
            shifted = jnp.pad(x, ((0, 0), (1, 0), (0, 0)))[:, :-1]
            delta = shifted - x
            xr, xw, xk, xv, xa, xg = [x + delta * x_mix[i] for i in range(6)]
            r = xr @ W_r
            w = DECAY_SCALE * jax.nn.sigmoid(jnp.tanh(xw @ A_w) @ B_w + b_w)
            k = xk @ W_k
            v = xv @ W_v
            a = jax.nn.sigmoid(xa @ A_a @ B_a + b_a)
            g = jax.nn.sigmoid(xg @ A_g) @ B_g
            kk = k * k_k
            kk = kk / jnp.maximum(jnp.linalg.norm(kk, axis=-1, keepdims=True), 1e-12)
            k = k * (1.0 + (a - 1.0) * k_a)
            decay = jnp.exp(w)

            def step(S, inp):
                r_t, dec_t, k_t, v_t, kk_t, a_t = inp
                b_t = kk_t * a_t
                sa = jnp.einsum('bvk,bk->bv', S, -kk_t)
                S = S * dec_t[:, None, :] + sa[:, :, None] * b_t[:, None, :] + v_t[:, :, None] * k_t[:, None, :]
                o_t = jnp.einsum('bvk,bk->bv', S, r_t)
                return (S, o_t)
            tm = lambda z: jnp.swapaxes(z, 0, 1)
            S0 = jnp.zeros((b, d, d), x.dtype)
            _, o = jax.lax.scan(step, S0, (tm(r), tm(decay), tm(k), tm(v), tm(kk), tm(a)))
            o = jnp.swapaxes(o, 0, 1)
            mu = jnp.mean(o, axis=-1, keepdims=True)
            var = jnp.var(o, axis=-1, keepdims=True)
            o = (o - mu) * jax.lax.rsqrt(var + EPS) * gn_w + gn_b
            o = o + jnp.sum(r * k * r_k, axis=-1, keepdims=True) * v
            return o * g @ W_o
        key = jax.random.key(seed)
        ks = jax.random.split(key, 20)
        n = jax.random.normal
        p = {}
        p['x'] = n(ks[0], (B, T, D), jnp.float32)
        p['x_mix'] = n(ks[1], (6, D), jnp.float32) * 0.1
        s = 1.0 / np.sqrt(D).astype(np.float32)
        p['W_r'] = n(ks[2], (D, D), jnp.float32) * s
        p['W_k'] = n(ks[3], (D, D), jnp.float32) * s
        p['W_v'] = n(ks[4], (D, D), jnp.float32) * s
        p['W_o'] = n(ks[5], (D, D), jnp.float32) * s
        p['A_w'] = n(ks[6], (D, W_LORA), jnp.float32) * s
        p['B_w'] = n(ks[7], (W_LORA, D), jnp.float32) / np.sqrt(W_LORA).astype(np.float32)
        p['b_w'] = n(ks[8], (D,), jnp.float32) * 0.5
        p['A_a'] = n(ks[9], (D, A_LORA), jnp.float32) * s
        p['B_a'] = n(ks[10], (A_LORA, D), jnp.float32) / np.sqrt(A_LORA).astype(np.float32)
        p['b_a'] = n(ks[11], (D,), jnp.float32) * 0.1
        p['A_g'] = n(ks[12], (D, G_LORA), jnp.float32) * s
        p['B_g'] = n(ks[13], (G_LORA, D), jnp.float32) / np.sqrt(G_LORA).astype(np.float32)
        p['k_k'] = n(ks[14], (D,), jnp.float32) * 0.5 + 0.85
        p['k_a'] = n(ks[15], (D,), jnp.float32) * 0.1 + 1.0
        p['r_k'] = n(ks[16], (D,), jnp.float32) * 0.1
        p['gn_w'] = jnp.ones((D,), jnp.float32)
        p['gn_b'] = jnp.zeros((D,), jnp.float32)
        return p
    _L1_attn_all = _L1_attn_setup()
    _L1_attn_in = {k: v for k, v in _L1_attn_all.items() if k in ('x_mix', 'W_r', 'W_k', 'W_v', 'W_o', 'A_w', 'B_w', 'b_w', 'A_a', 'B_a', 'b_a', 'A_g', 'B_g', 'k_k', 'k_a', 'r_k', 'gn_w', 'gn_b')}
    del _L1_attn_all

    def _L1_ffn_setup():
        import jax, jax.numpy as jnp
        import numpy as np
        B, T, IN_DIM = (64, 64, 64)
        HID, OUT_DIM = (128, 64)
        N_LAYERS, N_EXPERTS, N_SHARED = (2, 16, 1)
        key = jax.random.key(seed)
        ks = jax.random.split(key, 10)
        s = 0.02
        x = jax.random.normal(ks[0], (B, T, IN_DIM), dtype=jnp.float32)
        route_id = jax.random.randint(ks[1], (B,), 0, N_EXPERTS)
        Wi = jax.random.normal(ks[2], (HID, IN_DIM), dtype=jnp.float32) * s
        bi = jnp.zeros((HID,), dtype=jnp.float32)
        Wr = jax.random.normal(ks[3], (N_LAYERS, N_EXPERTS, HID, HID), dtype=jnp.float32) * s
        br = jax.random.normal(ks[4], (N_LAYERS, N_EXPERTS, HID), dtype=jnp.float32) * s
        Ws = jax.random.normal(ks[5], (N_LAYERS, N_SHARED, HID, HID), dtype=jnp.float32) * s
        bs = jax.random.normal(ks[6], (N_LAYERS, N_SHARED, HID), dtype=jnp.float32) * s
        Wo = jax.random.normal(ks[7], (OUT_DIM, HID), dtype=jnp.float32) * s
        bo = jnp.zeros((OUT_DIM,), dtype=jnp.float32)
        return {'x': x, 'route_id': route_id, 'Wi': Wi, 'bi': bi, 'Wr': Wr, 'br': br, 'Ws': Ws, 'bs': bs, 'Wo': Wo, 'bo': bo}
    _L1_ffn_all = _L1_ffn_setup()
    _L1_ffn_in = {k: v for k, v in _L1_ffn_all.items() if k in ('route_id', 'Wi', 'bi', 'Wr', 'br', 'Ws', 'bs', 'Wo', 'bo')}
    del _L1_ffn_all
    return {'x': x, 'L0_tok_W': _L0_tok_in['W'], 'L0_tok_b': _L0_tok_in['b'], 'L0_tok_gamma': _L0_tok_in['gamma'], 'L0_tok_beta': _L0_tok_in['beta'], 'L0_attn_Wq': _L0_attn_in['Wq'], 'L0_attn_Wk': _L0_attn_in['Wk'], 'L0_attn_Wv': _L0_attn_in['Wv'], 'L0_attn_Wo': _L0_attn_in['Wo'], 'L0_ffn_gate_w': _L0_ffn_in['gate_w'], 'L0_ffn_gate_b': _L0_ffn_in['gate_b'], 'L0_ffn_W1': _L0_ffn_in['W1'], 'L0_ffn_b1': _L0_ffn_in['b1'], 'L0_ffn_W2': _L0_ffn_in['W2'], 'L0_ffn_b2': _L0_ffn_in['b2'], 'L1_attn_x_mix': _L1_attn_in['x_mix'], 'L1_attn_W_r': _L1_attn_in['W_r'], 'L1_attn_W_k': _L1_attn_in['W_k'], 'L1_attn_W_v': _L1_attn_in['W_v'], 'L1_attn_W_o': _L1_attn_in['W_o'], 'L1_attn_A_w': _L1_attn_in['A_w'], 'L1_attn_B_w': _L1_attn_in['B_w'], 'L1_attn_b_w': _L1_attn_in['b_w'], 'L1_attn_A_a': _L1_attn_in['A_a'], 'L1_attn_B_a': _L1_attn_in['B_a'], 'L1_attn_b_a': _L1_attn_in['b_a'], 'L1_attn_A_g': _L1_attn_in['A_g'], 'L1_attn_B_g': _L1_attn_in['B_g'], 'L1_attn_k_k': _L1_attn_in['k_k'], 'L1_attn_k_a': _L1_attn_in['k_a'], 'L1_attn_r_k': _L1_attn_in['r_k'], 'L1_attn_gn_w': _L1_attn_in['gn_w'], 'L1_attn_gn_b': _L1_attn_in['gn_b'], 'L1_ffn_route_id': _L1_ffn_in['route_id'], 'L1_ffn_Wi': _L1_ffn_in['Wi'], 'L1_ffn_bi': _L1_ffn_in['bi'], 'L1_ffn_Wr': _L1_ffn_in['Wr'], 'L1_ffn_br': _L1_ffn_in['br'], 'L1_ffn_Ws': _L1_ffn_in['Ws'], 'L1_ffn_bs': _L1_ffn_in['bs'], 'L1_ffn_Wo': _L1_ffn_in['Wo'], 'L1_ffn_bo': _L1_ffn_in['bo']}

def reference(x, L0_tok_W, L0_tok_b, L0_tok_gamma, L0_tok_beta, L0_attn_Wq, L0_attn_Wk, L0_attn_Wv, L0_attn_Wo, L0_ffn_gate_w, L0_ffn_gate_b, L0_ffn_W1, L0_ffn_b1, L0_ffn_W2, L0_ffn_b2, L1_attn_x_mix, L1_attn_W_r, L1_attn_W_k, L1_attn_W_v, L1_attn_W_o, L1_attn_A_w, L1_attn_B_w, L1_attn_b_w, L1_attn_A_a, L1_attn_B_a, L1_attn_b_a, L1_attn_A_g, L1_attn_B_g, L1_attn_k_k, L1_attn_k_a, L1_attn_r_k, L1_attn_gn_w, L1_attn_gn_b, L1_ffn_route_id, L1_ffn_Wi, L1_ffn_bi, L1_ffn_Wr, L1_ffn_br, L1_ffn_Ws, L1_ffn_bs, L1_ffn_Wo, L1_ffn_bo):
    import jax
    import jax.numpy as jnp

    def _L0_tok_ref(x, W, b, gamma, beta):
        import jax, jax.numpy as jnp
        import numpy as np
        PATCH = 16
        STRIDE = 8
        EPS = 1e-05
        B, S, F = x.shape
        starts = jnp.arange(0, S - PATCH + 1, STRIDE)
        idx = starts[:, None] + jnp.arange(PATCH)[None, :]
        patches = x[:, idx, :].reshape(B, idx.shape[0], PATCH * F)
        y = jnp.einsum('bpi,di->bpd', patches, W) + b
        mu = jnp.mean(y, axis=-1, keepdims=True)
        var = jnp.mean(jnp.square(y - mu), axis=-1, keepdims=True)
        return (y - mu) * jax.lax.rsqrt(var + EPS) * gamma + beta

    def _L0_attn_ref(hidden_states, Wq, Wk, Wv, Wo):
        import jax, jax.numpy as jnp
        import numpy as np
        B, S, H = (2, 1024, 64)
        NH, NKV = (8, 4)
        HD = H // NH
        GROUPS = NH // NKV
        ROPE_BASE = 10000.0

        def _rope_cos_sin(seq_len, dim, dtype):
            inv_freq = 1.0 / ROPE_BASE ** (jnp.arange(0, dim, 2, dtype=jnp.float32) / dim)
            t = jnp.arange(seq_len, dtype=jnp.float32)
            freqs = jnp.outer(t, inv_freq)
            emb = jnp.concatenate([freqs, freqs], -1)
            return (jnp.cos(emb).astype(dtype), jnp.sin(emb).astype(dtype))

        def _rotate_half(x):
            x1, x2 = jnp.split(x, 2, axis=-1)
            return jnp.concatenate([-x2, x1], axis=-1)
        b, s, _ = hidden_states.shape
        q = (hidden_states @ Wq.T).reshape(b, s, NH, HD).transpose(0, 2, 1, 3)
        k = (hidden_states @ Wk.T).reshape(b, s, NKV, HD).transpose(0, 2, 1, 3)
        v = (hidden_states @ Wv.T).reshape(b, s, NKV, HD).transpose(0, 2, 1, 3)
        cos, sin = _rope_cos_sin(s, HD, hidden_states.dtype)
        q = q * cos + _rotate_half(q) * sin
        k = k * cos + _rotate_half(k) * sin
        k = jnp.repeat(k, GROUPS, axis=1)
        v = jnp.repeat(v, GROUPS, axis=1)
        scores = jnp.einsum('bhqd,bhkd->bhqk', q, k) / jnp.sqrt(jnp.float32(HD)).astype(q.dtype)
        causal = jnp.triu(jnp.full((s, s), -jnp.inf, dtype=scores.dtype), k=1)
        scores = scores + causal
        attn = jax.nn.softmax(scores.astype(jnp.float32), axis=-1).astype(q.dtype)
        out = jnp.einsum('bhqk,bhkd->bhqd', attn, v)
        out = out.transpose(0, 2, 1, 3).reshape(b, s, NH * HD)
        return out @ Wo.T

    def _L0_ffn_ref(x, gate_w, gate_b, W1, b1, W2, b2):
        import jax, jax.numpy as jnp
        import numpy as np
        B, T, D, H, E = (16, 1024, 64, 128, 8)
        Bb, Tt, Dd = x.shape
        Ee = gate_w.shape[1]
        xf = x.reshape(-1, Dd)
        N = xf.shape[0]
        logits = xf @ gate_w + gate_b
        probs = jax.nn.softmax(logits, axis=-1)
        top2_vals, top2_idx = jax.lax.top_k(probs, 2)
        cw = jnp.zeros((N, Ee), dtype=xf.dtype).at[jnp.arange(N)[:, None], top2_idx].add(top2_vals)

        def step(acc, params):
            w1, bb1, w2, bb2, we = params
            h = jax.nn.gelu(xf @ w1 + bb1, approximate=False)
            y = h @ w2 + bb2
            return (acc + we[:, None] * y, None)
        out, _ = jax.lax.scan(step, jnp.zeros_like(xf), (W1, b1, W2, b2, cw.T))
        return out.reshape(Bb, Tt, Dd)

    def _L1_attn_ref(x, x_mix, W_r, W_k, W_v, W_o, A_w, B_w, b_w, A_a, B_a, b_a, A_g, B_g, k_k, k_a, r_k, gn_w, gn_b):
        import jax, jax.numpy as jnp
        import numpy as np
        B, T, D = (4, 512, 64)
        W_LORA, A_LORA, G_LORA = (64, 64, 128)
        DECAY_SCALE = -0.6065306597126334
        EPS = D * 1e-05

        def _forward(x, x_mix, W_r, W_k, W_v, W_o, A_w, B_w, b_w, A_a, B_a, b_a, A_g, B_g, k_k, k_a, r_k, gn_w, gn_b):
            b, t, d = x.shape
            shifted = jnp.pad(x, ((0, 0), (1, 0), (0, 0)))[:, :-1]
            delta = shifted - x
            xr, xw, xk, xv, xa, xg = [x + delta * x_mix[i] for i in range(6)]
            r = xr @ W_r
            w = DECAY_SCALE * jax.nn.sigmoid(jnp.tanh(xw @ A_w) @ B_w + b_w)
            k = xk @ W_k
            v = xv @ W_v
            a = jax.nn.sigmoid(xa @ A_a @ B_a + b_a)
            g = jax.nn.sigmoid(xg @ A_g) @ B_g
            kk = k * k_k
            kk = kk / jnp.maximum(jnp.linalg.norm(kk, axis=-1, keepdims=True), 1e-12)
            k = k * (1.0 + (a - 1.0) * k_a)
            decay = jnp.exp(w)

            def step(S, inp):
                r_t, dec_t, k_t, v_t, kk_t, a_t = inp
                b_t = kk_t * a_t
                sa = jnp.einsum('bvk,bk->bv', S, -kk_t)
                S = S * dec_t[:, None, :] + sa[:, :, None] * b_t[:, None, :] + v_t[:, :, None] * k_t[:, None, :]
                o_t = jnp.einsum('bvk,bk->bv', S, r_t)
                return (S, o_t)
            tm = lambda z: jnp.swapaxes(z, 0, 1)
            S0 = jnp.zeros((b, d, d), x.dtype)
            _, o = jax.lax.scan(step, S0, (tm(r), tm(decay), tm(k), tm(v), tm(kk), tm(a)))
            o = jnp.swapaxes(o, 0, 1)
            mu = jnp.mean(o, axis=-1, keepdims=True)
            var = jnp.var(o, axis=-1, keepdims=True)
            o = (o - mu) * jax.lax.rsqrt(var + EPS) * gn_w + gn_b
            o = o + jnp.sum(r * k * r_k, axis=-1, keepdims=True) * v
            return o * g @ W_o
        return _forward(x, x_mix, W_r, W_k, W_v, W_o, A_w, B_w, b_w, A_a, B_a, b_a, A_g, B_g, k_k, k_a, r_k, gn_w, gn_b)

    def _L1_ffn_ref(x, route_id, Wi, bi, Wr, br, Ws, bs, Wo, bo):
        import jax, jax.numpy as jnp
        import numpy as np
        B, T, IN_DIM = (64, 64, 64)
        HID, OUT_DIM = (128, 64)
        N_LAYERS, N_EXPERTS, N_SHARED = (2, 16, 1)
        flat = x.reshape(-1, x.shape[-1])
        n_tok = flat.shape[0]
        route = jnp.repeat(route_id, n_tok // route_id.shape[0])
        h = jax.nn.relu(flat @ Wi.T + bi)
        n_layers, n_experts = (Wr.shape[0], Wr.shape[1])
        for l in range(n_layers):
            shared = (jnp.einsum('nd,shd->snh', h, Ws[l]) + bs[l][:, None, :]).mean(axis=0)
            routed = jnp.zeros_like(h)
            for e in range(n_experts):
                ye = h @ Wr[l, e].T + br[l, e]
                routed = routed + jnp.where((route == e)[:, None], ye, 0.0)
            h = jax.nn.relu(shared + routed + h)
        out = h @ Wo.T + bo
        return out.reshape(*x.shape[:-1], out.shape[-1])
    h = _L0_tok_ref(x, L0_tok_W, L0_tok_b, L0_tok_gamma, L0_tok_beta)
    h = h + _L0_attn_ref(_layernorm(h, axis=-1), L0_attn_Wq, L0_attn_Wk, L0_attn_Wv, L0_attn_Wo)
    h = h + _L0_ffn_ref(_layernorm(h, axis=-1), L0_ffn_gate_w, L0_ffn_gate_b, L0_ffn_W1, L0_ffn_b1, L0_ffn_W2, L0_ffn_b2)
    h = h + _L1_attn_ref(_layernorm(h, axis=-1), L1_attn_x_mix, L1_attn_W_r, L1_attn_W_k, L1_attn_W_v, L1_attn_W_o, L1_attn_A_w, L1_attn_B_w, L1_attn_b_w, L1_attn_A_a, L1_attn_B_a, L1_attn_b_a, L1_attn_A_g, L1_attn_B_g, L1_attn_k_k, L1_attn_k_a, L1_attn_r_k, L1_attn_gn_w, L1_attn_gn_b)
    h = h + _L1_ffn_ref(_layernorm(h, axis=-1), L1_ffn_route_id, L1_ffn_Wi, L1_ffn_bi, L1_ffn_Wr, L1_ffn_br, L1_ffn_Ws, L1_ffn_bs, L1_ffn_Wo, L1_ffn_bo)
    return h

_drawn_inputs = setup_inputs


def setup_inputs(seed=0):
    import zlib

    import numpy as np

    out = dict(_drawn_inputs(seed))
    spreads = {'L0_tok_gamma': (1.0, 0.2),
     'L0_tok_beta': (0.0, 0.1),
     'L0_ffn_gate_b': (0.0, 0.274),
     'L0_ffn_b1': (0.0, 0.8),
     'L0_ffn_b2': (0.0, 0.297),
     'L1_attn_gn_w': (1.0, 0.2),
     'L1_attn_gn_b': (0.0, 0.278),
     'L1_ffn_bi': (0.0, 0.709),
     'L1_ffn_bo': (0.0, 0.1)}
    factors = {'L0_attn_Wq': 8.0,
     'L0_attn_Wk': 8.0,
     'L0_attn_Wv': 3.326,
     'L0_attn_Wo': 3.065,
     'L0_ffn_gate_w': 2.708,
     'L0_ffn_W1': 8.0,
     'L0_ffn_W2': 4.976,
     'L1_ffn_Wi': 3.266,
     'L1_ffn_Wr': 8.0,
     'L1_ffn_br': 8.0,
     'L1_ffn_Ws': 7.823,
     'L1_ffn_bs': 8.0,
     'L1_attn_b_a': 2.746}
    for name, (base, spread) in spreads.items():
        noise = np.random.default_rng([zlib.crc32(name.encode()), seed]).standard_normal(out[name].shape)
        drawn = base * np.exp(spread * noise) if base else spread * noise
        out[name] = jnp.asarray(drawn.astype(out[name].dtype))
    for name, factor in factors.items():
        out[name] = (out[name] * factor).astype(out[name].dtype)
    return out
```

```python
import numpy as np
import concourse.bass as bass
from concourse import mybir
from contextlib import ExitStack

B, S_IN, F_IN = 64, 375, 16
PATCH, STRIDE, D = 16, 8, 64
T = (S_IN - PATCH) // STRIDE + 1
NH, NKV, HD = 8, 4, 8
E, HID = 8, 128
NR = 16
NL = 2
C = 4
PP = B // 2 // C
W = PP * T
LEVELS = (2, 4, 8, 16)
DECAY = -0.6065306597126334
SS_SCALE = 2.0 ** 20
NEG = -1.0e30

GROUPS = [
    [("tokA", 64), ("tokB", 64), ("mean", 128), ("vecs", 32)],
    [("wq", 128), ("wqr", 128), ("wk", 128), ("wkr", 128), ("wv", NKV * HD), ("cosq", T), ("sinq", T),
     ("cosk", T), ("sink", T), ("headmask", NH), ("identf", 128), ("identd", T), ("wo", 128)],
    [("gw", E), ("gb", E), ("tri", E * E), ("b1", E), ("w1", E * HID), ("w2", E * D), ("b2", 128),
     ("sel", E * 128)],
    [("Wr", 128), ("Wk", 128), ("Wvf", 128), ("Wvt", 64), ("Aw", 128), ("Bw", 128), ("Aa", 128), ("Ba", 128),
     ("Ag", 128), ("Bg", 64), ("Wo", 128), ("reset", W), ("mask4", 4 * T), ("maskL", T), ("negm1", T),
     ("negm1T", T), ("eye2", 2 * T), ("levels", len(LEVELS) * T), ("row32", 1)],
    [("Wi", 128), ("Ws", NL * 128), ("WoT", 64), ("Rb", NL * 128)],
]
COL, GROUP_OF, N_CONST = {}, {}, 0
GROUP_RANGE = []
for _g, _names in enumerate(GROUPS):
    _start = N_CONST
    for _n, _w in _names:
        COL[_n] = (N_CONST, _w)
        GROUP_OF[_n] = _g
        N_CONST += _w
    GROUP_RANGE.append((_start, N_CONST))
VECS = ["tok_b", "gamma", "beta", "b_w", "b_a", "k_k", "k_a", "r_k", "gn_w", "gn_b", "bi", "bo",
        "eps_ln", "eps_gn", "zero", "ten_ln2", "mix0", "mix1", "mix2", "mix3", "mix4", "mix5", "eidx", "shared"]

ARENA = 25 * W
H_, N_ = 0, W
def slot(i):
    return i * W
QBD_, KX_, VD_ = 5 * W, 8 * W, 16 * W
PB_ = VD_ + PP * 2 * NKV * 18
PT_ = PB_ + 512
XT_ = PT_ + 512
CH = T // 1 + 1
M4_, L_, TT_, X_, VT_ = slot(11), slot(2), slot(15), slot(17), slot(21)
U_, Y_ = slot(3), slot(5)
WG1_ = slot(19)

SEMS = """cst0 cst1 cst2 cst3 cst4 cst_bf ids psum0 init
tok_mm tok_y tok_n h0
q_mm q_mul q_sum q_bd k_mm k_mul k_sum kx v_mm vd s_mm s_max s_sub s_exp pt_mm pt_ev pv_mm o_rec att
attT_mm attT wo_mm h1
gate_mm g_lg g_mx g_sub g_exp g_sum g_rec g_pr g_cmp g_tri g_add g_cnt cw cwT_mm cwT b2_mm b2_add
hid_mm gelu y_mm cwb y_mul acc
delta xi rk_mm rk vw_mm vw aw_mm aw_aa aw_sg ab_mm ab g_hid g_sig gg_mm gg cs ep em kk0 kk_sq kk_mm kk_cl kk_ln kk_rs
kk bt0 bt tk kp kt kr1 krr bon0 bon_mm bon oneka vt_mm vt
m_mm m_ev l_ev lv1 tt1 x_mm x_ev t_mm t_ev u_mm u_ev y_mm2 y_ev z_mm z_ev w_mm sa o_mm o_ev
gn_n gn_a gn_b2 gn_g ro_mm h3
r_ge r_le r_in r_off r_mul r_id r_oh wsI f_mm f_relu r_mm r_relu fo_mm fo out_done""".split()
LNS = ["lt", "l1", "l2", "l3", "gn", "l4"]
SEMS += ["ln_mean", "ln_xc", "ln_sq", "ln_var", "ln_log", "ln_rs", "ln_out"]
SEMS += [f"x{c}" for c in range(C)] + [f"wg{l}_{c}" for l in range(NL) for c in range(C)]


def audio_tower(nc, xT, consts, masks_bf, route, wr, out):
    fp32, bf16, i32 = mybir.dt.float32, mybir.dt.bfloat16, mybir.dt.int32
    ALU, ACT, AX = mybir.AluOpType, mybir.ActivationFunctionType, mybir.AxisListType
    ctx = ExitStack()
    with ctx:
        def sb(name, shape, dt):
            return ctx.enter_context(nc.sbuf_tensor(name, shape, dt))

        sem = {n: ctx.enter_context(nc.semaphore(n)) for n in SEMS}
        K = sb("K", [128, N_CONST], fp32)
        KB = sb("KB", [128, 128 + T], bf16)
        arena = sb("arena", [128, C, ARENA], fp32)
        WG0 = sb("WG0", [128, B, 128], fp32)
        rid = sb("rid", [1, B], i32)
        rtmp = sb("rtmp", [1, 4, B], fp32)
        ride = sb("ride", [1, B], i32)
        ridb = sb("ridb", [NR + 1, B], i32)
        oneh = sb("oneh", [NR + 1, B], fp32)
        smax = sb("smax", [128, C, NH], fp32)
        orec = sb("orec", [128, C, 2 * NH], fp32)
        oneka = sb("oneka", [128, 1], fp32)
        WsI = sb("WsI", [128, NL * 128], fp32)
        PS = ctx.enter_context(nc.psum_tensor("PS", [128, 2 * C, 512], fp32))

        def k(name, lo=0, hi=None, p0=0, p1=128):
            o, w = COL[name]
            return K[p0:p1, o + lo:o + (w if hi is None else hi)]

        def vec(name):
            o = COL["vecs"][0] + VECS.index(name)
            return K[:, o:o + 1]

        def a(c, off, n=W, p0=0, p1=128):
            return arena[p0:p1, c, off:off + n]

        def norm(p, c):
            return LNS.index(p) * C + c + 1

        def normed(p, c):
            return ["l1", "l2", "l3", "l4"].index(p) * C + c + 1

        def pair(ap, t=T):
            return ap.rearrange("q (p t) -> q p t", t=t)

        def bank(c, b, n=W, lo=0, p0=0, p1=128):
            return PS[p0:p1, 2 * c + b, lo:lo + n]

        def both(c, n=W):
            return PS[:, 2 * c:2 * c + 2, 0:n]

        def over_pairs(ap, n=PP):
            return ap.unsqueeze(1).broadcast_to([ap.shape[0], n, ap.shape[1]])

        def half(c, off, j, lo, n, rows=T):
            return arena[64 * j:64 * j + rows, c, off + lo:off + lo + n]

        identb, maskb = KB[:, 0:128], KB[:, 128:128 + T]
        block = ctx.enter_context(nc.Block())

        @block.sync
        def _(sp):
            def load_consts(g):
                lo, hi = GROUP_RANGE[g]
                sp.dma_start(K[:, lo:hi], consts[:, lo:hi]).then_inc(sem[f"cst{g}"], 16)

            load_consts(0)
            for c in range(C):
                sp.dma_start(a(c, XT_, 2 * PP * CH), xT[:, c, :]).then_inc(sem[f"x{c}"], 16)
            load_consts(1)
            sp.dma_start(KB[:], masks_bf).then_inc(sem["cst_bf"], 16)
            sp.dma_start(rid[:], route[0:1, :]).then_inc(sem["ids"], 16)
            sp.dma_start(ridb[:], route[0:1, :].broadcast_to([NR + 1, B])).then_inc(sem["ids"], 16)
            for g in (2, 3, 4):
                load_consts(g)
            sp.wait_ge(sem["r_id"], 1)
            for l in range(NL):
                for c in range(C):
                    if l == 1:
                        sp.wait_ge(sem["o_mm"], c + 1)
                    for j in range(2):
                        for i in range(PP):
                            b = 32 * j + PP * c + i
                            e = sp.value_load(ride[0:1, b:b + 1], min_val=0, max_val=NR)
                            n = PP * j + i
                            dst = WG0[:, 2 * PP * c + n, :] if l == 0 else a(c, WG1_ + 128 * n, 128)
                            sp.dma_start(dst, wr[:, bass.ds(e * 128 + l * (NR + 1) * 128, 128)]).then_inc(
                                sem[f"wg{l}_{c}"], 16)
            for c in range(C):
                sp.wait_ge(sem["fo"], c + 1)
                sp.dma_start(out[:, c * W:(c + 1) * W], a(c, slot(6))).then_inc(sem["out_done"], 16)
            sp.wait_ge(sem["out_done"], 16 * C)

        @block.gpsimd
        def _(pool):
            g = nc.gpsimd
            for c in range(C):
                g.memset(a(c, QBD_, 3 * W), 0.0)
                g.memset(a(c, VD_, PP * 2 * NKV * 18 + 512), 0.0).then_inc(sem["init"], 1)
            pool.wait_ge(sem["cst1"], 16)
            for c in range(C):
                pool.wait_ge(sem["q_mul"], c + 1)
                g.tensor_tensor(a(c, slot(2)), a(c, slot(2)), a(c, slot(3)), ALU.add).then_inc(sem["q_sum"], 1)
            for c in range(C):
                pool.wait_ge(sem["k_mul"], c + 1)
                g.tensor_tensor(a(c, slot(4)), a(c, slot(4)), a(c, PT_), ALU.add).then_inc(sem["k_sum"], 1)
                pool.wait_ge(sem["k_sum"], c + 1)
                g.tensor_tensor(
                    a(c, KX_, NH * W).rearrange("q (p h t) -> q p h t", h=NH, t=T),
                    pair(a(c, slot(4))).unsqueeze(2).broadcast_to([128, PP, NH, T]),
                    k("headmask").unsqueeze(1).unsqueeze(3).broadcast_to([128, PP, NH, T]),
                    ALU.mult).then_inc(sem["kx"], 1)
            for e in range(E):
                for c in range(C):
                    n = e * C + c + 1
                    pool.wait_ge(sem["y_mul"], n)
                    if e:
                        pool.wait_ge(sem["acc"], n - C)
                    else:
                        pool.wait_ge(sem["b2_add"], c + 1)
                    g.tensor_tensor(a(c, H_), a(c, H_), a(c, slot(3 + e % 2)), ALU.add).then_inc(sem["acc"], 1)
            pool.wait_ge(sem["cst4"], 16)
            for l in range(NL):
                g.tensor_tensor(WsI[:, 128 * l:128 * l + 128], k("Ws", 128 * l, 128 * l + 128), k("identf"),
                                ALU.add).then_inc(sem["wsI"], 1)
            for c in range(C):
                pool.wait_ge(sem["kk"], c + 1)
                pool.wait_ge(sem["ab"], c + 1)
                g.tensor_tensor(a(c, slot(5)), a(c, slot(3)), a(c, slot(15)), ALU.mult).then_inc(sem["bt0"], 1)
                pool.wait_ge(sem["bt0"], c + 1)
                pool.wait_ge(sem["em"], c + 1)
                g.tensor_tensor(a(c, slot(5)), a(c, slot(5)), a(c, slot(14)), ALU.mult).then_inc(sem["bt"], 1)
                pool.wait_ge(sem["kp"], c + 1)
                g.tensor_tensor(a(c, slot(7)), a(c, slot(10)), a(c, slot(14)), ALU.mult).then_inc(sem["kt"], 1)
                pool.wait_ge(sem["ep"], c + 1)
                kr = a(c, slot(19), 2 * W).rearrange("q (p u t) -> q p u t", u=2, t=T)
                g.tensor_tensor(kr[:, :, 1, :], pair(a(c, slot(9))), pair(a(c, slot(13))),
                                ALU.mult).then_inc(sem["krr"], 1)
            for c in range(C):
                pool.wait_ge(sem["l_ev"], C + c + 1)
                pool.wait_ge(sem["m_ev"], C + c + 1)
                tt = a(c, TT_, 2 * W).rearrange("q (p u t) -> q p u t", u=2, t=T)
                m4 = a(c, M4_, 4 * W).rearrange("q (p u t) -> q p u t", u=4, t=T)
                g.tensor_tensor(tt[:, :, 0, :], pair(a(c, L_)), over_pairs(k("negm1")), ALU.mult)
                g.tensor_tensor(tt[:, :, 1, :], m4[:, :, 2, :], over_pairs(k("negm1T")),
                                ALU.mult).then_inc(sem["lv1"], 1)
                pool.wait_ge(sem["lv1"], c + 1)
                tt2 = a(c, TT_, 2 * W).rearrange("q (p t) -> q p t", t=2 * T)
                g.tensor_tensor(tt2, tt2, over_pairs(k("eye2")), ALU.add).then_inc(sem["tt1"], 1)
            for c in range(C):
                pool.wait_ge(sem["gn_a"], c + 1)
                pool.wait_ge(sem["bon"], c + 1)
                g.tensor_tensor(a(c, slot(10)), a(c, slot(10)), a(c, slot(8)), ALU.add).then_inc(sem["gn_b2"], 1)
                pool.wait_ge(sem["gn_b2"], c + 1)
                pool.wait_ge(sem["gg"], c + 1)
                g.tensor_tensor(a(c, slot(10)), a(c, slot(10)), a(c, slot(18)), ALU.mult).then_inc(sem["gn_g"], 1)

        @block.scalar
        def _(act):
            s = nc.scalar

            def norm_stats(p, xc, sq, eps):
                for c in range(C):
                    act.wait_ge(sem["ln_xc"], norm(p, c))
                    s.activation(a(c, sq), a(c, xc), ACT.Square).then_inc(sem["ln_sq"], 1)
                for c in range(C):
                    act.wait_ge(sem["ln_var"], norm(p, c))
                    s.activation(a(c, sq), bank(c, 1), ACT.Ln, bias=vec(eps)).then_inc(sem["ln_log"], 1)
                    act.wait_ge(sem["ln_log"], norm(p, c))
                    s.activation(a(c, sq), a(c, sq), ACT.Exp, scale=-0.5).then_inc(sem["ln_rs"], 1)

            act.wait_ge(sem["cst0"], 16)
            for c in range(C):
                act.wait_ge(sem["tok_mm"], c + 1)
                s.activation(a(c, H_), bank(c, 0), ACT.Identity, bias=vec("tok_b")).then_inc(sem["tok_y"], 1)
            norm_stats("lt", slot(2), slot(3), "eps_ln")
            norm_stats("l1", slot(2), slot(3), "eps_ln")
            act.wait_ge(sem["init"], C)
            for c in range(C):
                act.wait_ge(sem["q_sum"], c + 1)
                for j in range(2):
                    r0, r1 = 64 * j, 64 * j + 64
                    last = s.copy(a(c, QBD_, PP * 128, r0, r1).rearrange("q (p t) -> q p t", t=128)[:, :, 64 * j:64 * j + T],
                                  pair(a(c, slot(2), W, r0, r1)))
                last.then_inc(sem["q_bd"], 1)
            for i in range(PP):
                for c in range(C):
                    n = i * C + c + 1
                    pb = a(c, PB_, 512).rearrange("q (h t) -> q h t", t=64)[:, :, 0:T]
                    act.wait_ge(sem["s_sub"], n)
                    s.activation(pb, pb, ACT.Exp).then_inc(sem["s_exp"], 1)
                for c in range(C):
                    n = i * C + c + 1
                    act.wait_ge(sem["pt_mm"], n)
                    s.copy(a(c, PT_, 512).rearrange("q (r t) -> q r t", t=64)[:, :, 0:T],
                           bank(c, 1, 512).rearrange("q (r t) -> q r t", t=64)[:, :, 0:T]).then_inc(sem["pt_ev"], 1)
            for c in range(C):
                act.wait_ge(sem["attT_mm"], c + 1)
                s.copy(a(c, slot(4)), bank(c, 0)).then_inc(sem["attT"], 1)
            norm_stats("l2", slot(2), slot(3), "eps_ln")
            for c in range(C):
                act.wait_ge(sem["g_sub"], c + 1)
                s.activation(a(c, slot(9), PP * E), a(c, slot(9), PP * E), ACT.Exp).then_inc(sem["g_exp"], 1)
            for c in range(C):
                act.wait_ge(sem["cwT_mm"], c + 1)
                s.copy(a(c, slot(5)), bank(c, 1)).then_inc(sem["cwT"], 1)
            act.wait_ge(sem["cst2"], 16)
            for e in range(E):
                for c in range(C):
                    act.wait_ge(sem["hid_mm"], e * C + c + 1)
                    s.activation(a(c, slot(6), 2 * W).rearrange("q (b w) -> q b w", b=2), both(c), ACT.Gelu,
                                 bias=k("b1", e, e + 1)).then_inc(sem["gelu"], 1)
                for c in range(C):
                    act.wait_ge(sem["y_mm"], e * C + c + 1)
                    s.copy(a(c, slot(8)), bank(c, 1)).then_inc(sem["cwb"], 1)
            norm_stats("l3", slot(2), slot(3), "eps_ln")
            for c in range(C):
                act.wait_ge(sem["rk_mm"], c + 1)
                s.copy(a(c, slot(9), 2 * W).rearrange("q (b w) -> q b w", b=2), both(c)).then_inc(sem["rk"], 1)
            for c in range(C):
                act.wait_ge(sem["vw_mm"], c + 1)
                s.copy(a(c, slot(11)), bank(c, 0))
                s.activation(a(c, slot(12)), bank(c, 1), ACT.Tanh).then_inc(sem["vw"], 1)
            for c in range(C):
                act.wait_ge(sem["aw_mm"], c + 1)
                s.activation(a(c, slot(14)), bank(c, 1), ACT.Sigmoid, bias=vec("b_w")).then_inc(sem["aw_sg"], 1)
            for c in range(C):
                act.wait_ge(sem["ab_mm"], c + 1)
                s.activation(a(c, slot(15)), bank(c, 0), ACT.Sigmoid, bias=vec("b_a")).then_inc(sem["ab"], 1)
            for c in range(C):
                act.wait_ge(sem["g_hid"], c + 1)
                s.activation(a(c, slot(16), 2 * W).rearrange("q (b w) -> q b w", b=2), both(c),
                             ACT.Sigmoid).then_inc(sem["g_sig"], 1)
            for c in range(C):
                act.wait_ge(sem["gg_mm"], c + 1)
                s.copy(a(c, slot(18)), bank(c, 0)).then_inc(sem["gg"], 1)
            for c in range(C):
                act.wait_ge(sem["kk0"], c + 1)
                s.activation(a(c, slot(4)), a(c, slot(3)), ACT.Square).then_inc(sem["kk_sq"], 1)
            for c in range(C):
                act.wait_ge(sem["cs"], c + 1)
                s.activation(a(c, slot(13)), a(c, slot(12)), ACT.Exp, scale=DECAY).then_inc(sem["ep"], 1)
                s.activation(a(c, slot(14)), a(c, slot(12)), ACT.Exp, scale=-DECAY).then_inc(sem["em"], 1)
            for c in range(C):
                act.wait_ge(sem["kk_cl"], c + 1)
                s.activation(a(c, slot(4)), a(c, slot(4)), ACT.Ln, scale=SS_SCALE).then_inc(sem["kk_ln"], 1)
                act.wait_ge(sem["kk_ln"], c + 1)
                s.activation(a(c, slot(4)), a(c, slot(4)), ACT.Exp, scale=-0.5,
                             bias=vec("ten_ln2")).then_inc(sem["kk_rs"], 1)
            for c in range(C):
                act.wait_ge(sem["vt_mm"], c + 1)
                s.copy(a(c, VT_, 512), bank(c, 0, 512)).then_inc(sem["vt"], 1)
            for c in range(C):
                act.wait_ge(sem["u_mm"], c + 1)
                s.copy(a(c, U_, 512), bank(c, 0, 512)).then_inc(sem["u_ev"], 1)
            for c in range(C):
                act.wait_ge(sem["y_mm2"], c + 1)
                s.copy(a(c, Y_, 512), bank(c, 1, 512)).then_inc(sem["y_ev"], 1)
            for c in range(C):
                act.wait_ge(sem["z_mm"], c + 1)
                s.activation(a(c, U_, 512), bank(c, 0, 512), ACT.Copy, scale=k("row32")).then_inc(sem["z_ev"], 1)
            for c in range(C):
                act.wait_ge(sem["o_mm"], c + 1)
                s.copy(a(c, slot(9)), bank(c, 0)).then_inc(sem["o_ev"], 1)
            norm_stats("gn", slot(10), slot(17), "eps_gn")
            norm_stats("l4", slot(2), slot(3), "eps_ln")
            for c in range(C):
                act.wait_ge(sem["f_mm"], c + 1)
                s.activation(a(c, slot(2), 2 * W).rearrange("q (b w) -> q b w", b=2), both(c), ACT.Relu,
                             bias=vec("bi")).then_inc(sem["f_relu"], 1)
            for l in range(NL):
                for c in range(C):
                    act.wait_ge(sem["r_mm"], l * C + c + 1)
                    s.activation(a(c, slot(4 if l == 0 else 2), 2 * W).rearrange("q (b w) -> q b w", b=2), both(c),
                                 ACT.Relu).then_inc(sem["r_relu"], 1)

        @block.vector
        def _(dve):
            v = nc.vector

            def center(p, src, xc):
                for c in range(C):
                    dve.wait_ge(sem["ln_mean"], norm(p, c))
                    v.tensor_tensor(a(c, xc), a(c, src), bank(c, 0), ALU.subtract).then_inc(sem["ln_xc"], 1)

            def scale_norm(p, xc, sq, dst):
                for c in range(C):
                    dve.wait_ge(sem["ln_rs"], norm(p, c))
                    v.tensor_tensor(a(c, dst), a(c, xc), a(c, sq), ALU.mult).then_inc(sem["ln_out"], 1)

            for b in range(2 * C):
                last = v.memset(PS[:, b, :], 1.0)
            last.then_inc(sem["psum0"], 1)
            dve.wait_ge(sem["cst0"], 16)
            v.tensor_scalar(oneka[:], vec("k_a"), -1.0, 1.0, ALU.mult, ALU.add).then_inc(sem["oneka"], 1)
            center("lt", H_, slot(2))
            for c in range(C):
                dve.wait_ge(sem["ln_rs"], norm("lt", c))
                v.tensor_tensor(a(c, slot(2)), a(c, slot(2)), a(c, slot(3)), ALU.mult).then_inc(sem["tok_n"], 1)
                dve.wait_ge(sem["tok_n"], c + 1)
                v.tensor_scalar(a(c, H_), a(c, slot(2)), vec("gamma"), vec("beta"), ALU.mult,
                                ALU.add).then_inc(sem["h0"], 1)
            center("l1", H_, slot(2))
            scale_norm("l1", slot(2), slot(3), N_)
            dve.wait_ge(sem["cst1"], 16)

            def rope(name, done, d0, d1, cos, sin):
                for c in range(C):
                    dve.wait_ge(sem[name], c + 1)
                    v.tensor_tensor(pair(a(c, d0)), pair(bank(c, 0)), over_pairs(k(cos)), ALU.mult)
                    v.tensor_tensor(pair(a(c, d1)), pair(bank(c, 1)), over_pairs(k(sin)),
                                    ALU.mult).then_inc(sem[done], 1)

            rope("q_mm", "q_mul", slot(2), slot(3), "cosq", "sinq")
            rope("k_mm", "k_mul", slot(4), PT_, "cosk", "sink")
            dve.wait_ge(sem["init"], C)
            for c in range(C):
                for hh in range(2):
                    vd = a(c, VD_, PP * 2 * NKV * 18, 64 * hh, 64 * hh + 64).rearrange("q (r u) -> q r u", u=18)
                    v.memset(vd[:, :, 9 * hh + 8:9 * hh + 9], 1.0)
            for c in range(C):
                dve.wait_ge(sem["v_mm"], c + 1)
                for hh in range(2):
                    for j in range(2):
                        r0, r1 = 64 * hh, 64 * hh + 64
                        vd = a(c, VD_, PP * 2 * NKV * 18, r0, r1).rearrange("q (p j g u) -> q p j g u", j=2, g=NKV, u=18)
                        last = v.tensor_copy(vd[:, :, j, :, 9 * hh:9 * hh + HD],
                                             bank(c, j, PP * NKV * HD, 0, r0, r1).rearrange(
                                                 "q (p g d) -> q p g d", g=NKV, d=HD))
                last.then_inc(sem["vd"], 1)
            dve.wait_ge(sem["ids"], 32)
            v.tensor_scalar(rtmp[:, 0, :], rid[:], 0.0, None, ALU.is_ge).then_inc(sem["r_ge"], 1)
            v.tensor_scalar(rtmp[:, 1, :], rid[:], float(NR - 1), None, ALU.is_le).then_inc(sem["r_le"], 1)
            v.tensor_scalar(rtmp[:, 2, :], rid[:], float(-NR), None, ALU.add).then_inc(sem["r_off"], 1)
            v.tensor_scalar(oneh[:], ridb[:], vec("eidx")[0:NR + 1, :], vec("shared")[0:NR + 1, :],
                            ALU.is_equal, ALU.max).then_inc(sem["r_oh"], 1)
            dve.wait_ge(sem["r_le"], 1)
            v.tensor_tensor(rtmp[:, 3, :], rtmp[:, 0, :], rtmp[:, 1, :], ALU.mult).then_inc(sem["r_in"], 1)
            dve.wait_ge(sem["r_in"], 1)
            dve.wait_ge(sem["r_off"], 1)
            v.tensor_tensor(rtmp[:, 0, :], rtmp[:, 3, :], rtmp[:, 2, :], ALU.mult).then_inc(sem["r_mul"], 1)
            dve.wait_ge(sem["r_mul"], 1)
            v.tensor_scalar(ride[:], rtmp[:, 0, :], float(NR), None, ALU.add).then_inc(sem["r_id"], 1)

            def attn_out(i):
                for c in range(C):
                    dve.wait_ge(sem["pv_mm"], i * C + c + 1)
                    o = bank(c, 0, 2 * NH * 9, W).rearrange("q (r u) -> q r u", u=9)
                    v.reciprocal(orec[:, c, :].unsqueeze(2), o[:, :, HD:HD + 1]).then_inc(sem["o_rec"], 1)
                    dve.wait_ge(sem["o_rec"], (i // 2) * C + c + 1)
                    v.tensor_tensor(a(c, slot(2) + (i - 1) * D, 2 * D).rearrange("q (r d) -> q r d", d=HD),
                                    o[:, :, 0:HD], orec[:, c, :].unsqueeze(2).broadcast_to([128, 2 * NH, HD]),
                                    ALU.mult).then_inc(sem["att"], 1)

            for i in range(PP):
                for c in range(C):
                    n = i * C + c + 1
                    sc = bank(c, 0).rearrange("q (h t) -> q h t", t=T)
                    dve.wait_ge(sem["s_mm"], n)
                    v.tensor_reduce(smax[:, c, :], sc, AX.X, ALU.max).then_inc(sem["s_max"], 1)
                    dve.wait_ge(sem["s_max"], n)
                    v.tensor_tensor(a(c, PB_, 512).rearrange("q (h t) -> q h t", t=64)[:, :, 0:T], sc,
                                    smax[:, c, :].unsqueeze(2).broadcast_to([128, NH, T]),
                                    ALU.subtract).then_inc(sem["s_sub"], 1)
                if i % 2:
                    attn_out(i)
            for c in range(C):
                dve.wait_ge(sem["wo_mm"], c + 1)
                v.tensor_tensor(a(c, H_), a(c, H_), bank(c, 1), ALU.add).then_inc(sem["h1"], 1)
            center("l2", H_, slot(2))
            scale_norm("l2", slot(2), slot(3), N_)
            dve.wait_ge(sem["cst2"], 16)
            small = PP * E
            for c in range(C):
                lg = a(c, slot(9), small).rearrange("q (p e) -> q p e", e=E)
                mx = a(c, slot(9) + small, PP)
                dve.wait_ge(sem["gate_mm"], c + 1)
                v.tensor_tensor(lg, bank(c, 0, small).rearrange("q (p e) -> q p e", e=E), over_pairs(k("gb")),
                                ALU.add).then_inc(sem["g_lg"], 1)
                dve.wait_ge(sem["g_lg"], c + 1)
                v.tensor_reduce(mx, lg, AX.X, ALU.max).then_inc(sem["g_mx"], 1)
                dve.wait_ge(sem["g_mx"], c + 1)
                v.tensor_tensor(lg, lg, mx.unsqueeze(2).broadcast_to([128, PP, E]),
                                ALU.subtract).then_inc(sem["g_sub"], 1)
            for c in range(C):
                lg = a(c, slot(9), small).rearrange("q (p e) -> q p e", e=E)
                sm, cnt, cw = a(c, slot(9) + 2 * small, PP), a(c, slot(9) + 3 * small, small), a(c, slot(9) + 4 * small, small)
                gt = a(c, slot(10), PP * E * E).rearrange("q (p e f) -> q p e f", e=E, f=E)
                eq = a(c, slot(12), PP * E * E).rearrange("q (p e f) -> q p e f", e=E, f=E)
                other = lg.unsqueeze(2).broadcast_to([128, PP, E, E])
                self_ = lg.unsqueeze(3).broadcast_to([128, PP, E, E])
                dve.wait_ge(sem["g_exp"], c + 1)
                v.tensor_reduce(sm, lg, AX.X, ALU.add).then_inc(sem["g_sum"], 1)
                dve.wait_ge(sem["g_sum"], c + 1)
                v.reciprocal(sm, sm).then_inc(sem["g_rec"], 1)
                dve.wait_ge(sem["g_rec"], c + 1)
                v.tensor_tensor(lg, lg, sm.unsqueeze(2).broadcast_to([128, PP, E]), ALU.mult).then_inc(sem["g_pr"], 1)
                dve.wait_ge(sem["g_pr"], c + 1)
                v.tensor_tensor(eq, other, self_, ALU.is_equal).then_inc(sem["g_cmp"], 1)
                v.tensor_tensor(gt, other, self_, ALU.is_gt).then_inc(sem["g_cmp"], 1)
                dve.wait_ge(sem["g_cmp"], 2 * (c + 1))
                eqf = a(c, slot(12), PP * E * E).rearrange("q (p r) -> q p r", r=E * E)
                v.tensor_tensor(eqf, eqf, over_pairs(k("tri")), ALU.mult).then_inc(sem["g_tri"], 1)
                dve.wait_ge(sem["g_tri"], c + 1)
                v.tensor_tensor(a(c, slot(10), PP * E * E), a(c, slot(10), PP * E * E), a(c, slot(12), PP * E * E),
                                ALU.add).then_inc(sem["g_add"], 1)
                dve.wait_ge(sem["g_add"], c + 1)
                v.tensor_reduce(cnt, a(c, slot(10), PP * E * E).rearrange("q (r f) -> q r f", f=E), AX.X,
                                ALU.add).then_inc(sem["g_cnt"], 1)
                dve.wait_ge(sem["g_cnt"], c + 1)
                v.scalar_tensor_tensor(out=cw, in0=cnt, scalar=2.0, in1=a(c, slot(9), small), op0=ALU.is_lt,
                                       op1=ALU.mult).then_inc(sem["cw"], 1)
            for c in range(C):
                dve.wait_ge(sem["b2_mm"], c + 1)
                v.tensor_tensor(a(c, H_), a(c, H_), bank(c, 0), ALU.add).then_inc(sem["b2_add"], 1)
            for e in range(E):
                for c in range(C):
                    n = e * C + c + 1
                    dve.wait_ge(sem["cwb"], n)
                    if e >= 2:
                        dve.wait_ge(sem["acc"], n - 2 * C)
                    v.tensor_tensor(a(c, slot(3 + e % 2)), bank(c, 0), a(c, slot(8)), ALU.mult).then_inc(sem["y_mul"], 1)
            center("l3", H_, slot(2))
            scale_norm("l3", slot(2), slot(3), N_)
            for c in range(C):
                d, x = pair(a(c, slot(2))), pair(a(c, N_))
                dve.wait_ge(sem["ln_out"], normed("l3", c))
                v.tensor_tensor(d[:, :, 1:T], x[:, :, 0:T - 1], x[:, :, 1:T], ALU.subtract)
                v.tensor_scalar(d[:, :, 0:1], x[:, :, 0:1], -1.0, None, ALU.mult).then_inc(sem["delta"], 1)
                dve.wait_ge(sem["delta"], c + 1)
                for i in range(6):
                    v.scalar_tensor_tensor(out=a(c, slot(3 + i)), in0=a(c, slot(2)), scalar=vec(f"mix{i}"),
                                           in1=a(c, N_), op0=ALU.mult, op1=ALU.add).then_inc(sem["xi"], 1)
            for c in range(C):
                dve.wait_ge(sem["aw_mm"], c + 1)
                v.tensor_copy(a(c, slot(13)), bank(c, 0)).then_inc(sem["aw_aa"], 1)
            dve.wait_ge(sem["cst3"], 16)
            for c in range(C):
                dve.wait_ge(sem["rk"], c + 1)
                v.tensor_scalar(a(c, slot(3)), a(c, slot(10)), vec("k_k"), None, ALU.mult).then_inc(sem["kk0"], 1)
            for c in range(C):
                dve.wait_ge(sem["aw_sg"], c + 1)
                v.tensor_tensor_scan(a(c, slot(12)), k("reset"), a(c, slot(14)), 0.0, ALU.mult,
                                     ALU.add).then_inc(sem["cs"], 1)
            for c in range(C):
                dve.wait_ge(sem["kk_mm"], c + 1)
                v.tensor_scalar(a(c, slot(4)), bank(c, 1), float(D), 1e-24, ALU.mult, ALU.max).then_inc(sem["kk_cl"], 1)
            dve.wait_ge(sem["oneka"], 1)
            for c in range(C):
                dve.wait_ge(sem["kk_rs"], c + 1)
                v.tensor_tensor(a(c, slot(3)), a(c, slot(3)), a(c, slot(4)), ALU.mult).then_inc(sem["kk"], 1)
                dve.wait_ge(sem["ab"], c + 1)
                v.tensor_scalar(a(c, slot(16)), a(c, slot(15)), vec("k_a"), oneka[:], ALU.mult,
                                ALU.add).then_inc(sem["tk"], 1)
                dve.wait_ge(sem["tk"], c + 1)
                v.tensor_tensor(a(c, slot(10)), a(c, slot(10)), a(c, slot(16)), ALU.mult).then_inc(sem["kp"], 1)
                kr = a(c, slot(19), 2 * W).rearrange("q (p u t) -> q p u t", u=2, t=T)
                dve.wait_ge(sem["kk"], c + 1)
                dve.wait_ge(sem["ep"], c + 1)
                v.tensor_tensor(kr[:, :, 0, 1:T], pair(a(c, slot(3)))[:, :, 1:T], pair(a(c, slot(13)))[:, :, 0:T - 1],
                                ALU.mult)
                v.tensor_copy(kr[:, :, 0, 0:1], pair(a(c, slot(3)))[:, :, 0:1]).then_inc(sem["kr1"], 1)
                dve.wait_ge(sem["kp"], c + 1)
                v.scalar_tensor_tensor(out=a(c, slot(8)), in0=a(c, slot(9)), scalar=vec("r_k"), in1=a(c, slot(10)),
                                       op0=ALU.mult, op1=ALU.mult).then_inc(sem["bon0"], 1)
            for c in range(C):
                dve.wait_ge(sem["bon_mm"], c + 1)
                v.scalar_tensor_tensor(out=a(c, slot(8)), in0=bank(c, 1), scalar=float(D), in1=a(c, slot(11)),
                                       op0=ALU.mult, op1=ALU.mult).then_inc(sem["bon"], 1)
            for hf in range(2):
                for c in range(C):
                    dve.wait_ge(sem["m_mm"], hf * C + c + 1)
                    if hf == 0:
                        dve.wait_ge(sem["bon"], c + 1)
                    src = PS[:, 2 * c:2 * c + 2, 0:10 * T].rearrange("q b (i u) -> q b i u", u=5 * T)
                    m4 = a(c, M4_ + hf * 2 * W, 2 * W).rearrange("q (b i u) -> q b i u", b=2, u=4 * T)
                    lm = a(c, L_ + hf * (W // 2), W // 2).rearrange("q (b i u) -> q b i u", b=2, u=T)
                    v.tensor_tensor(m4, src[:, :, :, 0:4 * T],
                                    k("mask4").unsqueeze(1).unsqueeze(1).broadcast_to([128, 2, 2, 4 * T]),
                                    ALU.mult).then_inc(sem["m_ev"], 1)
                    v.tensor_tensor(lm, src[:, :, :, 4 * T:5 * T],
                                    k("maskL").unsqueeze(1).unsqueeze(1).broadcast_to([128, 2, 2, T]),
                                    ALU.mult).then_inc(sem["l_ev"], 1)
            for n in range(len(LEVELS)):
                for c in range(C):
                    dve.wait_ge(sem["x_mm"], n * C + c + 1)
                    v.tensor_tensor(pair(a(c, X_)), pair(bank(c, 0)), over_pairs(k("levels", n * T, n * T + T)),
                                    ALU.mult).then_inc(sem["x_ev"], 1)
                for c in range(C):
                    dve.wait_ge(sem["t_mm"], n * C + c + 1)
                    if n < len(LEVELS) - 1:
                        tt = a(c, TT_, 2 * W).rearrange("q (b w) -> q b w", b=2)
                        v.tensor_tensor(tt, tt, both(c), ALU.subtract).then_inc(sem["t_ev"], 1)
                    else:
                        tt = a(c, TT_, 2 * W).rearrange("q (p u t) -> q p u t", u=2, t=T)[:, :, 1, :]
                        v.tensor_tensor(tt, tt, pair(bank(c, 1)), ALU.subtract).then_inc(sem["t_ev"], 1)
            for c in range(C):
                dve.wait_ge(sem["w_mm"], c + 1)
                v.tensor_tensor(a(c, Y_, 512), a(c, Y_, 512), bank(c, 1, 512), ALU.subtract).then_inc(sem["sa"], 1)
            center("gn", slot(9), slot(10))
            for c in range(C):
                dve.wait_ge(sem["ln_rs"], norm("gn", c))
                v.tensor_tensor(a(c, slot(10)), a(c, slot(10)), a(c, slot(17)), ALU.mult).then_inc(sem["gn_n"], 1)
                dve.wait_ge(sem["gn_n"], c + 1)
                v.tensor_scalar(a(c, slot(10)), a(c, slot(10)), vec("gn_w"), vec("gn_b"), ALU.mult,
                                ALU.add).then_inc(sem["gn_a"], 1)
            for c in range(C):
                dve.wait_ge(sem["ro_mm"], c + 1)
                v.tensor_tensor(a(c, H_), a(c, H_), bank(c, 0), ALU.add).then_inc(sem["h3"], 1)
            center("l4", H_, slot(2))
            scale_norm("l4", slot(2), slot(3), N_)
            for c in range(C):
                dve.wait_ge(sem["fo_mm"], c + 1)
                v.scalar_tensor_tensor(out=a(c, slot(6)), in0=bank(c, 0), scalar=vec("bo"), in1=a(c, H_), op0=ALU.add,
                                       op1=ALU.add).then_inc(sem["fo"], 1)

        @block.tensor
        def _(pe):
            def mm(o, l, r, start=True, stop=True, **kw):
                return nc.tensor.matmul(o, l, r, start=start, stop=stop, **kw)

            def mean_var(p, ready, src, sq):
                for c in range(C):
                    pe.wait_ge(sem[ready], c + 1)
                    mm(bank(c, 0), k("mean"), a(c, src)).then_inc(sem["ln_mean"], 1)
                for c in range(C):
                    pe.wait_ge(sem["ln_sq"], norm(p, c))
                    mm(bank(c, 1), k("mean"), a(c, sq)).then_inc(sem["ln_var"], 1)

            pe.wait_ge(sem["psum0"], 1)
            pe.wait_ge(sem["cst0"], 16)
            for c in range(C):
                pe.wait_ge(sem[f"x{c}"], 16)
                xt = a(c, XT_, 2 * PP * CH).rearrange("q (j p t) -> q j p t", j=2, t=CH)
                for j in range(2):
                    o = bank(c, 0, W, 0, 64 * j, 64 * j + 64)
                    mm(o, k("tokA"), xt[:, j, :, 0:T], stop=False)
                    last = mm(o, k("tokB"), xt[:, j, :, 1:T + 1], start=False)
                last.then_inc(sem["tok_mm"], 1)
            mean_var("lt", "tok_y", H_, slot(3))
            mean_var("l1", "h0", H_, slot(3))
            pe.wait_ge(sem["cst1"], 16)
            for c in range(C):
                pe.wait_ge(sem["ln_out"], normed("l1", c))
                mm(bank(c, 0), k("wq"), a(c, N_))
                mm(bank(c, 1), k("wqr"), a(c, N_)).then_inc(sem["q_mm"], 1)
            for c in range(C):
                pe.wait_ge(sem["q_mul"], c + 1)
                mm(bank(c, 0), k("wk"), a(c, N_))
                mm(bank(c, 1), k("wkr"), a(c, N_)).then_inc(sem["k_mm"], 1)
            for c in range(C):
                pe.wait_ge(sem["k_mul"], c + 1)
                for j in range(2):
                    for hh in range(2):
                        for i in range(PP):
                            last = mm(PS[64 * hh:64 * hh + T, 2 * c + j, 32 * i:32 * i + 32],
                                      half(c, N_, j, i * T, T, 64), k("wv", 0, 32, 64 * j, 64 * j + 64))
                last.then_inc(sem["v_mm"], 1)
            pe.wait_ge(sem["cst_bf"], 16)

            def scores(i):
                for c in range(C):
                    if i == 0:
                        pe.wait_ge(sem["kx"], c + 1)
                        pe.wait_ge(sem["q_bd"], c + 1)
                        pe.wait_ge(sem["vd"], c + 1)
                    elif i % 2 == 0:
                        pe.wait_ge(sem["att"], (i // 2 - 1) * C + c + 1)
                    mm(bank(c, 0).rearrange("q (h t) -> q h t", t=T), identb,
                       maskb.unsqueeze(1).broadcast_to([128, NH, T]), stop=False)
                    mm(bank(c, 0), a(c, QBD_ + 128 * i, 128), a(c, KX_ + i * W), start=False).then_inc(sem["s_mm"], 1)

            for i in range(PP):
                scores(i)
                for c in range(C):
                    n = i * C + c + 1
                    pe.wait_ge(sem["s_exp"], n)
                    for g in range(NKV):
                        last = nc.tensor.transpose(bank(c, 1, 128, 128 * g), a(c, PB_ + 128 * g, 128), k("identf"))
                    last.then_inc(sem["pt_mm"], 1)
                for c in range(C):
                    n = i * C + c + 1
                    pe.wait_ge(sem["pt_ev"], n)
                    for j in range(2):
                        for g in range(NKV):
                            last = mm(PS[64 * j:64 * j + T, 2 * c, W + (i % 2) * NH * 9 + 18 * g:
                                         W + (i % 2) * NH * 9 + 18 * g + 18],
                                      a(c, PT_ + 128 * g + 64 * j, T, 0, 64 + T),
                                      a(c, VD_ + ((i * 2 + j) * NKV + g) * 18, 18, 0, 64 + T))
                    last.then_inc(sem["pv_mm"], 1)
            for c in range(C):
                pe.wait_ge(sem["att"], (PP // 2 - 1) * C + c + 1)
                for i in range(PP):
                    for j in range(2):
                        last = mm(bank(c, 0, T, i * T, 64 * j, 64 * j + 64), half(c, slot(2), j, i * D, D),
                                  k("identd", 0, T, 64 * j, 64 * j + T))
                last.then_inc(sem["attT_mm"], 1)
            for c in range(C):
                pe.wait_ge(sem["attT"], c + 1)
                mm(bank(c, 1), k("wo"), a(c, slot(4))).then_inc(sem["wo_mm"], 1)
            mean_var("l2", "h1", H_, slot(3))
            pe.wait_ge(sem["cst2"], 16)
            for c in range(C):
                pe.wait_ge(sem["ln_out"], normed("l2", c))
                for i in range(PP):
                    for j in range(2):
                        last = mm(PS[64 * j:64 * j + T, 2 * c, E * i:E * i + E], half(c, N_, j, i * T, T, 64),
                                  k("gw", 0, E, 64 * j, 64 * j + 64))
                last.then_inc(sem["gate_mm"], 1)
            for c in range(C):
                pe.wait_ge(sem["cw"], c + 1)
                for i in range(PP):
                    for j in range(2):
                        last = mm(PS[64 * j:64 * j + E, 2 * c + 1, i * T:i * T + T],
                                  half(c, slot(9) + 4 * PP * E, j, i * E, E), k("identd", 0, T, 64 * j, 64 * j + T))
                last.then_inc(sem["cwT_mm"], 1)
            for c in range(C):
                pe.wait_ge(sem["cwT"], c + 1)
                mm(bank(c, 0), k("b2"), a(c, slot(5))).then_inc(sem["b2_mm"], 1)
            for e in range(E):
                for c in range(C):
                    if e == 0:
                        pe.wait_ge(sem["b2_add"], c + 1)
                    else:
                        pe.wait_ge(sem["y_mul"], (e - 1) * C + c + 1)
                    for j in range(2):
                        last = mm(bank(c, j), k("w1", e * HID, e * HID + HID, 64 * j, 64 * j + 64),
                                  half(c, N_, j, 0, W, 64))
                    last.then_inc(sem["hid_mm"], 1)
                for c in range(C):
                    pe.wait_ge(sem["gelu"], e * C + c + 1)
                    for j in range(2):
                        mm(bank(c, 0, W, 0, 64 * j, 64 * j + 64), k("w2", e * D, e * D + D), a(c, slot(6 + j)))
                    mm(bank(c, 1), k("sel", e * 128, e * 128 + 128), a(c, slot(5))).then_inc(sem["y_mm"], 1)
            for c in range(C):
                pe.wait_ge(sem["acc"], (E - 1) * C + c + 1)
                mm(bank(c, 0), k("mean"), a(c, H_)).then_inc(sem["ln_mean"], 1)
            for c in range(C):
                pe.wait_ge(sem["ln_sq"], norm("l3", c))
                mm(bank(c, 1), k("mean"), a(c, slot(3))).then_inc(sem["ln_var"], 1)
            pe.wait_ge(sem["cst3"], 16)
            for c in range(C):
                pe.wait_ge(sem["xi"], 6 * c + 6)
                mm(bank(c, 0), k("Wr"), a(c, slot(3)))
                mm(bank(c, 1), k("Wk"), a(c, slot(5))).then_inc(sem["rk_mm"], 1)
            for c in range(C):
                pe.wait_ge(sem["rk"], c + 1)
                mm(bank(c, 0), k("Wvf"), a(c, slot(6)))
                mm(bank(c, 1), k("Aw"), a(c, slot(4))).then_inc(sem["vw_mm"], 1)
            for c in range(C):
                pe.wait_ge(sem["vw"], c + 1)
                mm(bank(c, 0), k("Aa"), a(c, slot(7)))
                mm(bank(c, 1), k("Bw"), a(c, slot(12))).then_inc(sem["aw_mm"], 1)
            for c in range(C):
                pe.wait_ge(sem["aw_aa"], c + 1)
                mm(bank(c, 0), k("Ba"), a(c, slot(13))).then_inc(sem["ab_mm"], 1)
            for c in range(C):
                pe.wait_ge(sem["ab"], c + 1)
                pe.wait_ge(sem["aw_sg"], c + 1)
                for j in range(2):
                    last = mm(bank(c, j), k("Ag", 0, 128, 64 * j, 64 * j + 64), half(c, slot(8), j, 0, W, 64))
                last.then_inc(sem["g_hid"], 1)
            for c in range(C):
                pe.wait_ge(sem["g_sig"], c + 1)
                for j in range(2):
                    last = mm(bank(c, 0, W, 0, 64 * j, 64 * j + 64), k("Bg"), a(c, slot(16 + j)))
                last.then_inc(sem["gg_mm"], 1)
            for c in range(C):
                pe.wait_ge(sem["kk_sq"], c + 1)
                mm(bank(c, 1), k("mean"), a(c, slot(4))).then_inc(sem["kk_mm"], 1)
            for c in range(C):
                pe.wait_ge(sem["gg"], c + 1)
                for i in range(PP):
                    for j in range(2):
                        last = mm(PS[64 * j:64 * j + T, 2 * c, D * i:D * i + D], half(c, slot(6), j, i * T, T, 64),
                                  k("Wvt", 0, D, 64 * j, 64 * j + 64))
                last.then_inc(sem["vt_mm"], 1)
            for c in range(C):
                pe.wait_ge(sem["bon0"], c + 1)
                pe.wait_ge(sem["kk_cl"], c + 1)
                mm(bank(c, 1), k("mean"), a(c, slot(8))).then_inc(sem["bon_mm"], 1)
            for hf in range(2):
                for c in range(C):
                    if hf == 0:
                        for name in ("bt", "kt", "krr", "kr1", "bon", "vt"):
                            pe.wait_ge(sem[name], c + 1)
                    else:
                        pe.wait_ge(sem["l_ev"], c + 1)
                        pe.wait_ge(sem["m_ev"], c + 1)
                    for q in range(PP // 2):
                        i = hf * PP // 2 + q
                        col = (q % 2) * 5 * T
                        for j in range(2):
                            o = PS[64 * j:64 * j + T, 2 * c + q // 2, col:col + 5 * T]
                            mm(o[:, 0:2 * T], half(c, slot(7), j, i * T, T, 64), half(c, slot(19), j, 2 * i * T, 2 * T, 64))
                            mm(o[:, 2 * T:4 * T], half(c, slot(5), j, i * T, T, 64), half(c, slot(19), j, 2 * i * T, 2 * T, 64))
                            last = mm(o[:, 4 * T:5 * T], half(c, slot(19), j, 2 * i * T, T, 64), half(c, slot(5), j, i * T, T, 64))
                    last.then_inc(sem["m_mm"], 1)

            def m4(c, i, j, u, rows=T):
                return half(c, M4_, j, (4 * i + u) * T, T, rows)

            def tt(c, i, j, u):
                return half(c, TT_, j, (2 * i + u) * T, T)

            for n in range(len(LEVELS)):
                for c in range(C):
                    if n == 0:
                        pe.wait_ge(sem["tt1"], c + 1)
                    else:
                        pe.wait_ge(sem["t_ev"], (n - 1) * C + c + 1)
                    for i in range(PP):
                        for j in range(2):
                            last = mm(bank(c, 0, T, i * T, 64 * j, 64 * j + T), m4(c, i, j, 2), tt(c, i, j, 0))
                    last.then_inc(sem["x_mm"], 1)
                for c in range(C):
                    pe.wait_ge(sem["x_ev"], n * C + c + 1)
                    for i in range(PP):
                        for j in range(2):
                            x = half(c, X_, j, i * T, T)
                            if n < len(LEVELS) - 1:
                                o = PS[64 * j:64 * j + T, 2 * c + i // 4, (i % 4) * 2 * T:(i % 4) * 2 * T + 2 * T]
                                mm(o[:, 0:T], tt(c, i, j, 1), x)
                                last = mm(o[:, T:2 * T], x, tt(c, i, j, 1))
                            else:
                                last = mm(bank(c, 1, T, i * T, 64 * j, 64 * j + T), x, tt(c, i, j, 1))
                    last.then_inc(sem["t_mm"], 1)

            def solve(name, ready, b, lhs, rhs, rows=T):
                for c in range(C):
                    for r in ready:
                        pe.wait_ge(sem[r[0]], r[1] + c + 1)
                    for i in range(PP):
                        for j in range(2):
                            last = mm(PS[64 * j:64 * j + T, 2 * c + b, D * i:D * i + D], lhs(c, i, j),
                                      half(c, rhs, j, i * D, D, rows))
                    last.then_inc(sem[name], 1)

            solve("u_mm", [("t_ev", (len(LEVELS) - 1) * C)], 0, lambda c, i, j: m4(c, i, j, 0), VT_)
            solve("y_mm2", [("u_ev", 0)], 1, lambda c, i, j: tt(c, i, j, 1), U_)
            solve("z_mm", [("y_ev", 0)], 0, lambda c, i, j: m4(c, i, j, 2, 32), Y_, 32)
            solve("w_mm", [("z_ev", 0)], 1, lambda c, i, j: tt(c, i, j, 1), U_)
            for c in range(C):
                pe.wait_ge(sem["sa"], c + 1)
                for i in range(PP):
                    for j in range(2):
                        o = bank(c, 0, T, i * T, 64 * j, 64 * j + 64)
                        mm(o, half(c, Y_, j, i * D, D), m4(c, i, j, 3), stop=False)
                        last = mm(o, half(c, VT_, j, i * D, D), m4(c, i, j, 1), start=False)
                last.then_inc(sem["o_mm"], 1)
            mean_var("gn", "o_ev", slot(9), slot(17))
            for c in range(C):
                pe.wait_ge(sem["gn_g"], c + 1)
                mm(bank(c, 0), k("Wo"), a(c, slot(10))).then_inc(sem["ro_mm"], 1)
            mean_var("l4", "h3", H_, slot(3))
            pe.wait_ge(sem["cst4"], 16)
            pe.wait_ge(sem["r_oh"], 1)
            pe.wait_ge(sem["wsI"], NL)
            for c in range(C):
                pe.wait_ge(sem["ln_out"], normed("l4", c))
                for j in range(2):
                    last = mm(bank(c, j), k("Wi", 0, 128, 64 * j, 64 * j + 64), half(c, N_, j, 0, W, 64))
                last.then_inc(sem["f_mm"], 1)
            for l in range(NL):
                for c in range(C):
                    if l == 0:
                        pe.wait_ge(sem["f_relu"], c + 1)
                    else:
                        pe.wait_ge(sem["r_relu"], c + 1)
                    pe.wait_ge(sem[f"wg{l}_{c}"], 16 * 2 * PP)
                    src = slot(2 if l == 0 else 4)
                    for j in range(2):
                        mm(pair(bank(c, j)), k("Rb", 128 * l, 128 * l + 128, 0, NR + 1),
                           oneh[:, 32 * j + PP * c:32 * j + PP * c + PP].unsqueeze(2).broadcast_to([NR + 1, PP, T]),
                           stop=False)
                        for i in range(PP):
                            n = PP * j + i
                            w = WG0[:, 2 * PP * c + n, :] if l == 0 else a(c, WG1_ + 128 * n, 128)
                            mm(bank(c, j, T, i * T), w, a(c, src + j * W + i * T, T), start=False, stop=False)
                        last = mm(bank(c, j), WsI[:, 128 * l:128 * l + 128], a(c, src + j * W), start=False)
                    last.then_inc(sem["r_mm"], 1)
            for c in range(C):
                pe.wait_ge(sem["r_relu"], C + c + 1)
                for j in range(2):
                    last = mm(bank(c, 0, W, 0, 64 * j, 64 * j + 64), k("WoT"), a(c, slot(2 + j)))
                last.then_inc(sem["fo_mm"], 1)


def shape_constants():
    z = {}
    pos = np.arange(T, dtype=np.float32)
    inv = (1.0 / 10000.0 ** (np.arange(0, HD, 2, dtype=np.float32) / HD)).astype(np.float32)
    fr = np.outer(pos, inv).astype(np.float32)
    emb = np.concatenate([fr, fr], -1)
    cos = np.tile(np.cos(emb).T, (2 * NH, 1)).astype(np.float32)
    sin = np.tile(np.sin(emb).T, (2 * NH, 1)).astype(np.float32)
    sign = np.tile(np.where(np.arange(HD) < HD // 2, -1.0, 1.0), 2 * NH)[:, None].astype(np.float32)
    sc = np.float32(1.0 / np.sqrt(HD))
    z["cosq"], z["sinq"], z["cosk"], z["sink"] = cos * sc, sin * sign * sc, cos, sin * sign
    q = np.arange(128)
    z["headmask"] = ((q % 64) // HD)[:, None] == np.arange(NH)[None, :]
    z["identf"] = np.eye(128)
    r = (q % 64)[:, None]
    t = np.arange(T)[None, :]
    z["identd"] = r == t
    z["mean"] = ((q[:, None] // 64) == (q[None, :] // 64)) / float(D)
    z["tri"] = np.tile((np.arange(E)[None, :] < np.arange(E)[:, None]).reshape(1, -1), (128, 1))
    sel = np.zeros((128, E, 128))
    for e in range(E):
        for j in range(2):
            sel[64 * j + e, e, 64 * j:64 * j + 64] = 1
    z["sel"] = sel.reshape(128, -1)
    z["reset"] = np.tile((np.arange(W) % T != 0)[None, :], (128, 1))
    z["mask4"] = np.concatenate([r < t, r <= t, r < t, -1.0 * (r <= t)], 1)
    z["maskL"] = r > t
    z["negm1"] = -1.0 * ((r // 2 == t // 2) & (r > t))
    z["negm1T"] = -1.0 * ((r // 2 == t // 2) & (r < t))
    z["eye2"] = np.concatenate([r == t, r == t], 1)
    z["levels"] = np.concatenate([(r // (2 * b) == t // (2 * b)) & (r // b > t // b) for b in LEVELS], 1)
    z["row32"] = r >= 32
    out = {n: np.asarray(x, np.float32) for n, x in z.items()}
    causal = np.where((r < T) & (t > r), NEG, 0.0)
    return out, np.concatenate([np.eye(128), causal], 1)


def kernel(**inputs):
    import ml_dtypes
    import concourse.bacc as _bacc
    from concourse import mybir as _mybir
    from concourse.bass_utils import run_bass_kernel_spmd as _run

    inp = {n: np.asarray(x) for n, x in inputs.items()}
    cst, bf = shape_constants()

    def bd(m):
        o = np.zeros((128, 2 * m.shape[1]), np.float32)
        o[:64, :m.shape[1]] = m
        o[64:, m.shape[1]:] = m
        return o

    def dup(m):
        return np.concatenate([m, m], 0)

    wt = inp["L0_tok_W"]
    rot = np.concatenate([(np.arange(HD) + HD // 2) % HD + h * HD for h in range(NH)])
    kvrow = np.concatenate([np.arange(HD) + (h // (NH // NKV)) * HD for h in range(NH)])
    wq, wk = inp["L0_attn_Wq"], inp["L0_attn_Wk"][kvrow]
    cst.update(
        tokA=wt[:, :128].T, tokB=wt[:, 128:].T, wq=bd(wq.T), wqr=bd(wq[rot].T), wk=bd(wk.T), wkr=bd(wk[rot].T),
        wv=dup(inp["L0_attn_Wv"].T), wo=bd(inp["L0_attn_Wo"].T), gw=dup(inp["L0_ffn_gate_w"]),
        gb=np.tile(inp["L0_ffn_gate_b"][None], (128, 1)), b1=inp["L0_ffn_b1"].T,
        w1=dup(inp["L0_ffn_W1"].transpose(1, 0, 2).reshape(D, -1)),
        w2=inp["L0_ffn_W2"].transpose(1, 0, 2).reshape(HID, -1),
        Wr=bd(inp["L1_attn_W_r"]), Wk=bd(inp["L1_attn_W_k"]), Wvf=bd(inp["L1_attn_W_v"]), Wvt=dup(inp["L1_attn_W_v"]),
        Aw=bd(inp["L1_attn_A_w"]), Bw=bd(inp["L1_attn_B_w"]), Aa=bd(inp["L1_attn_A_a"]), Ba=bd(inp["L1_attn_B_a"]),
        Ag=dup(inp["L1_attn_A_g"]), Bg=inp["L1_attn_B_g"], Wo=bd(inp["L1_attn_W_o"]),
        Wi=dup(inp["L1_ffn_Wi"].T), Ws=inp["L1_ffn_Ws"][:, 0].transpose(2, 0, 1).reshape(128, -1),
        WoT=inp["L1_ffn_Wo"].T)
    b2 = np.zeros((128, 128), np.float32)
    b2[0:E, 0:64] = inp["L0_ffn_b2"]
    b2[64:64 + E, 64:128] = inp["L0_ffn_b2"]
    rb = np.zeros((128, NL * 128), np.float32)
    rb[0:NR] = inp["L1_ffn_br"].transpose(1, 0, 2).reshape(NR, -1)
    rb[NR] = inp["L1_ffn_bs"][:, 0].reshape(-1)
    cst["b2"], cst["Rb"] = b2, rb
    vecs = np.zeros((128, 32), np.float32)
    cols = dict(tok_b=inp["L0_tok_b"], gamma=inp["L0_tok_gamma"], beta=inp["L0_tok_beta"], b_w=inp["L1_attn_b_w"],
                b_a=inp["L1_attn_b_a"], k_k=inp["L1_attn_k_k"], k_a=inp["L1_attn_k_a"], r_k=inp["L1_attn_r_k"],
                gn_w=inp["L1_attn_gn_w"], gn_b=inp["L1_attn_gn_b"], bo=inp["L1_ffn_bo"])
    for i in range(6):
        cols[f"mix{i}"] = inp["L1_attn_x_mix"][i]
    for n, x in cols.items():
        vecs[:, VECS.index(n)] = np.concatenate([x, x])
    vecs[:, VECS.index("bi")] = inp["L1_ffn_bi"]
    vecs[:, VECS.index("eps_ln")] = 1e-5
    vecs[:, VECS.index("eps_gn")] = D * 1e-5
    vecs[:, VECS.index("ten_ln2")] = 10.0 * np.log(2.0)
    vecs[:, VECS.index("eidx")] = np.arange(128)
    vecs[NR, VECS.index("shared")] = 1.0
    cst["vecs"] = vecs
    packed = np.zeros((128, N_CONST), np.float32)
    for n, (o, w) in COL.items():
        packed[:cst[n].shape[0], o:o + w] = cst[n]
    x = inp["x"][:, :CH * STRIDE].reshape(2, C, PP, CH, STRIDE * F_IN)
    xT = np.ascontiguousarray(x.transpose(4, 1, 0, 2, 3).reshape(128, C, 2 * PP * CH))
    wr = np.zeros((128, NL, NR + 1, 128), np.float32)
    wr[:, :, :NR] = inp["L1_ffn_Wr"].transpose(3, 0, 1, 2)
    arrays = {
        "xT": xT, "consts": packed, "masks_bf": np.ascontiguousarray(bf.astype(ml_dtypes.bfloat16)),
        "route": np.ascontiguousarray(inp["L1_ffn_route_id"].reshape(1, B)), "wr": wr.reshape(128, -1),
    }
    nc = _bacc.Bacc("TRN2", target_bir_lowering=False, num_devices=1)
    args = [nc.dram_tensor(n, v.shape, _mybir.dt.from_np(v.dtype), kind="ExternalInput").ap() for n, v in arrays.items()]
    args.append(nc.dram_tensor("out", (128, C * W), _mybir.dt.float32, kind="ExternalOutput").ap())
    audio_tower(nc, *args)
    r = _run(nc, [arrays], core_ids=[0])
    o = r.results[0]["out"]
    return np.ascontiguousarray(o.reshape(2, D, B // 2, T).transpose(0, 2, 3, 1).reshape(B, T, D))
```

```python
import numpy as np
import concourse.bass as bass
from concourse import mybir
from contextlib import ExitStack

B, S_IN, F_IN = 64, 375, 16
PATCH, STRIDE, D = 16, 8, 64
T = (S_IN - PATCH) // STRIDE + 1
NH, NKV, HD = 8, 4, 8
E, HID = 8, 128
NR = 16
NL = 2
C = 4
PP = B // 2 // C
W = PP * T
LEVELS = (2, 4, 8, 16)
DECAY = -0.6065306597126334
SS_SCALE = 2.0 ** 20
NEG = -1.0e30

GROUPS = [
    [("tokA", 64), ("tokB", 64), ("mean", 128), ("vecs", 36)],
    [("wq", 128), ("wqr", 128), ("wk", 128), ("wkr", 128), ("wv", NKV * HD), ("cosq", T), ("sinq", T),
     ("cosk", T), ("sink", T), ("headmask", NH), ("identf", 128), ("identd", T), ("wo", 128)],
    [("gw", E), ("gb", E), ("tri", E * E), ("b1", E), ("w1", E * HID), ("w2", E * D), ("b2", 128)],
    [("Wr", 128), ("Wk", 128), ("Wvf", 128), ("Wvt", 64), ("Aw", 128), ("Bw", 128), ("Aa", 128), ("Ba", 128),
     ("Ag", 128), ("Bg", 64), ("Wo", 128), ("reset", W), ("mask4", 4 * T), ("maskL", T), ("negm1", T),
     ("negm1T", T), ("eye2", 2 * T), ("levels", len(LEVELS) * 2 * T), ("row32", 1)],
    [("Wi", 128), ("Ws", NL * 128), ("WoT", 64), ("Rb", NL * 128)],
]
COL, GROUP_OF, N_CONST = {}, {}, 0
GROUP_RANGE = []
for _g, _names in enumerate(GROUPS):
    _start = N_CONST
    for _n, _w in _names:
        COL[_n] = (N_CONST, _w)
        GROUP_OF[_n] = _g
        N_CONST += _w
    GROUP_RANGE.append((_start, N_CONST))
VECS = ["tok_b", "gamma", "beta", "b_w", "b_a", "k_k", "k_a", "r_k", "gn_w", "gn_b", "bi", "bo",
        "eps_ln", "eps_gn", "zero", "ten_ln2", "mix0", "mix1", "mix2", "mix3", "mix4", "mix5", "eidx", "shared",
        "cw_mid", "cw_low", "rb_mid", "rb_low", "feat0", "feat1", "tok0", "tok1", "early0", "early1"]

H_, N_ = 0, W
def slot(i):
    return i * W
QBD_, KX_, VD_ = 5 * W, 8 * W, 16 * W
PB_ = VD_ + PP * 2 * NKV * 18
PT_ = PB_ + 512
XT_ = PT_ + 512
CH = T // 1 + 1
M4_, L_, TT_, U_, Y_ = slot(11), slot(9), slot(3), slot(19), slot(3)
KR_, X_, VT_, LT_, TB_, SA_ = ((slot(1), slot(17)), (slot(5), slot(7)), (slot(1), slot(17)), (slot(10), slot(15)),
                               (slot(5), slot(7)), (slot(5), slot(19)))
WG1_ = slot(19) + PP * D
ARENA = WG1_ + 2 * PP * 128
CW_ = slot(13) + 160

SEMS = """rb_steps r_steps g_steps cst0 cst1 cst2 cst3 cst4 cst_bf ids psum0 init oneka rb_split
r_id r_oh wsI
tok_mm tok_y h0 ln_mean ln_xc ln_sq ln_var ln_log ln_rs ln_out
q_mm q_mul q_sum q_bd k_mm k_mul k_sum kx v_mm vd s_mm s_max s_sub s_exp pt_mm pt_ev pv_mm o_rec att
attT_mm attT wo_mm h1
gate_mm g_sub g_exp g_cmp cw cwT_mm c_hi c_r c_mid cwT b2_mm b2_add
hid_mm gelu y_mm cwb y_mul acc
delta xi rk_mm rk vw_mm vw aw_mm aw_aa aw_sg ab_mm ab g_hid g_sig gg_mm gg cs ep em kk0 kk_sq kk_mm kk_cl kk_ln kk_rs
kk bt0 bt tk kp kt kr1 krr krb bon0 bon_mm bon vt_mm vt
m_mm m_ev lv1 tt1 ltb ttb lt32 sab x_mm x_ev t_mm t_ev u_mm u_ev y_mm2 y_ev z_mm z_ev w_mm sa o_mm o_ev
gn_a gn_b2 gn_g ro_mm h3 f_mm f_relu r_mm r_relu fo_mm fo out_done""".split()
LNS = ["lt", "l1", "l2", "l3", "gn", "l4"]
SEMS += [f"x{c}" for c in range(C)] + [f"wg{l}_{c}" for l in range(NL) for c in range(C)]

def norm_steps(k):
    return [("mean", k, 0.6), ("var", k, 0.6)]


STEPS = [("tok", 0, 1.3)] + norm_steps(0) + norm_steps(1) + [("q", 0, 1.2), ("k", 0, 1.2), ("v", 0, 1.6)]
for _i in range(PP):
    STEPS += [("s", _i, 0.8), ("t", _i, 0.4), ("pvb" if _i % 2 else "pva", _i, 0.3)]
STEPS += [("attT", 0, 0.8), ("wo", 0, 0.6)] + norm_steps(2) + [("gate", 0, 0.4), ("cwT", 0, 0.8), ("b2", 0, 0.6)]
for _i in range(E):
    STEPS += [("hid", _i, 1.2), ("y", _i, 0.8)]
STEPS += norm_steps(3) + [("rk", 0, 1.2), ("vw", 0, 1.2), ("aw", 0, 1.2), ("ab", 0, 0.6), ("gh", 0, 1.2), ("gg", 0, 0.6),
                          ("kk", 0, 0.6), ("bon", 0, 0.6), ("m", 0, 2.5), ("m", 1, 2.5),
                          ("vt", 0, 1.2)]
for _i in range(len(LEVELS)):
    STEPS += [("lx", _i, 1.3), ("lt", _i, 2.4)]
STEPS += [("u", 0, 1.8), ("y2", 0, 1.8), ("z", 0, 1.8), ("w", 0, 1.8), ("o", 0, 2.6)] + norm_steps(4)
STEPS += [("ro", 0, 0.6)] + norm_steps(5) + [("f", 0, 1.2), ("r", 0, 4.5), ("r", 1, 4.5), ("fo", 0, 0.6)]


def schedule():
    keyed, at = [], 0.0
    for n, (name, i, us) in enumerate(STEPS):
        for c in range(C):
            keyed.append((at + SKEW[c], n, c, name, i))
        at += us
    return [(name, i, c) for _, _, c, name, i in sorted(keyed)]


SKEW = (0.0, 0.0, 0.0, 0.0)
ORDER = schedule()
COUNT = {}
for _name, _i, _c in ORDER:
    COUNT[_name, _i, _c] = 1 + sum(1 for key in COUNT if key[0] == _name)


def audio_tower(nc, xT, consts, masks_bf, route, wr, out):
    fp32, bf16, i32 = mybir.dt.float32, mybir.dt.bfloat16, mybir.dt.int32
    ALU, ACT, AX = mybir.AluOpType, mybir.ActivationFunctionType, mybir.AxisListType
    ctx = ExitStack()
    with ctx:
        def sb(name, shape, dt):
            return ctx.enter_context(nc.sbuf_tensor(name, shape, dt))

        sem = {n: ctx.enter_context(nc.semaphore(n)) for n in SEMS}
        K = sb("K", [128, N_CONST], fp32)
        KB = sb("KB", [128, 128 + T + E * 128], bf16)
        arena = sb("arena", [128, C, ARENA], fp32)
        WG0 = sb("WG0", [128, B, 128], fp32)
        rid = sb("rid", [1, B], i32)
        ride = sb("ride", [1, B], i32)
        ridb = sb("ridb", [3 * (NR + 1), B], i32)
        oneh = sb("oneh", [3 * (NR + 1), B], bf16)
        rb_split = sb("rb_split", [3 * (NR + 1), 2, NL * 128], bf16)
        smax = sb("smax", [128, C, NH], fp32)
        orec = sb("orec", [128, C, 2 * NH], fp32)
        oneka = sb("oneka", [128, 1], fp32)
        PS = ctx.enter_context(nc.psum_tensor("PS", [128, 2 * C, 512], fp32))

        def k(name, lo=0, hi=None, p0=0, p1=128):
            o, w = COL[name]
            return K[p0:p1, o + lo:o + (w if hi is None else hi)]

        def vec(name):
            o = COL["vecs"][0] + VECS.index(name)
            return K[:, o:o + 1]

        def a(c, off, n=W, p0=0, p1=128):
            return arena[p0:p1, c, off:off + n]

        def pair(ap, t=T):
            return ap.rearrange("q (p t) -> q p t", t=t)

        def bank(c, b, n=W, lo=0, p0=0, p1=128):
            return PS[p0:p1, 2 * c + b, lo:lo + n]

        def both(c, n=W):
            return PS[:, 2 * c:2 * c + 2, 0:n]

        def over_pairs(ap, n=PP):
            return ap.unsqueeze(1).broadcast_to([ap.shape[0], n, ap.shape[1]])

        def half(c, off, j, lo, n, rows=T):
            return arena[64 * j:64 * j + rows, c, off + lo:off + lo + n]

        def halves(ap):
            return ap.rearrange("q (b w) -> q b w", b=2)

        def to_bank(c, b, n, j, i, rows):
            return PS[64 * j:64 * j + rows, 2 * c + b, n * i:n * i + n]

        def m2(c):
            return a(c, M4_, 4 * W).rearrange("q (p u t) -> q p u t", u=4, t=T)[:, :, 2, :]

        def part_bf(c, i):
            return a(c, slot(i), W // 2).bitcast(bf16)

        rtmp = a(0, ARENA - 4 * B, 4 * B, 0, 1).rearrange("q (r b) -> q r b", b=B)
        identb, maskb, selb = KB[:, 0:128], KB[:, 128:128 + T], KB[:, 128 + T:]
        LN_EXP = "natural_log_exp_and_others"
        NORM_SLOTS = {p: (slot(2), slot(3)) for p in LNS}
        NORM_SLOTS["gn"] = (slot(10), slot(17))
        block = ctx.enter_context(nc.Block())

        @block.sync
        def _(sp):
            def load_consts(g):
                lo, hi = GROUP_RANGE[g]
                sp.dma_start(K[:, lo:hi], consts[:, lo:hi]).then_inc(sem[f"cst{g}"], 16)

            load_consts(0)
            for c in range(C):
                sp.dma_start(a(c, XT_, 2 * PP * CH), xT[:, c, :]).then_inc(sem[f"x{c}"], 16)
                if c == 0:
                    load_consts(1)
                    sp.dma_start(KB[:], masks_bf).then_inc(sem["cst_bf"], 16)
            sp.dma_start(rid[:], route[0:1, :]).then_inc(sem["ids"], 16)
            sp.dma_start(ridb[:], route[0:1, :].broadcast_to([3 * (NR + 1), B])).then_inc(sem["ids"], 16)
            for g in (2, 3, 4):
                load_consts(g)
            sp.wait_ge(sem["r_id"], 1)
            for l in range(NL):
                for c in range(C):
                    if l == 1:
                        sp.wait_ge(sem["h1"], c + 1)
                    for j in range(2):
                        for i in range(PP):
                            b = 32 * j + PP * c + i
                            e = sp.value_load(ride[0:1, b:b + 1], min_val=0, max_val=NR)
                            n = PP * j + i
                            dst = WG0[:, 2 * PP * c + n, :] if l == 0 else a(c, WG1_ + 128 * n, 128)
                            sp.dma_start(dst, wr[:, bass.ds(e * 128 + l * (NR + 1) * 128, 128)]).then_inc(
                                sem[f"wg{l}_{c}"], 16)
            for c in range(C):
                sp.wait_ge(sem["fo"], c + 1)
                sp.dma_start(out[:, c * W:(c + 1) * W], a(c, slot(6))).then_inc(sem["out_done"], 16)
            sp.wait_ge(sem["out_done"], 16 * C)

        @block.gpsimd
        def _(pool):
            g = nc.gpsimd
            for c in range(C):
                g.memset(a(c, QBD_, 3 * W), 0.0)
                g.memset(a(c, VD_, PP * 2 * NKV * 18 + 512), 0.0).then_inc(sem["init"], 1)
            pool.wait_ge(sem["cst4"], 16)
            pool.wait_ge(sem["cst1"], 16)
            for l in range(NL):
                ws = k("Ws", 128 * l, 128 * l + 128)
                g.tensor_tensor(ws, ws, k("identf"), ALU.add).then_inc(sem["wsI"], 1)
            for name, i, c in ORDER:
                n = COUNT[name, i, c]
                if name == "q":
                    pool.wait_ge(sem["q_mul"], n)
                    g.tensor_tensor(a(c, slot(2)), a(c, slot(2)), a(c, slot(3)), ALU.add).then_inc(sem["q_sum"], 1)
                elif name == "k":
                    pool.wait_ge(sem["k_mul"], n)
                    g.tensor_tensor(a(c, slot(4)), a(c, slot(4)), a(c, PT_), ALU.add).then_inc(sem["k_sum"], 1)
                    pool.wait_ge(sem["k_sum"], n)
                    g.tensor_tensor(
                        a(c, KX_, NH * W).rearrange("q (p h t) -> q p h t", h=NH, t=T),
                        pair(a(c, slot(4))).unsqueeze(2).broadcast_to([128, PP, NH, T]),
                        k("headmask").unsqueeze(1).unsqueeze(3).broadcast_to([128, PP, NH, T]),
                        ALU.mult).then_inc(sem["kx"], 1)
                elif name == "y":
                    pool.wait_ge(sem["y_mul"], n)
                    if i:
                        pool.wait_ge(sem["acc"], COUNT["y", i - 1, c])
                    g.tensor_tensor(a(c, H_), a(c, H_), a(c, slot(3 + i % 2)), ALU.add).then_inc(sem["acc"], 1)
                elif name == "kk":
                    pool.wait_ge(sem["kk"], n)
                    g.tensor_tensor(a(c, slot(5)), a(c, slot(3)), a(c, slot(15)), ALU.mult).then_inc(sem["bt0"], 1)
                    pool.wait_ge(sem["bt0"], n)
                    g.tensor_tensor(a(c, slot(5)), a(c, slot(5)), a(c, slot(14)), ALU.mult).then_inc(sem["bt"], 1)
                    pool.wait_ge(sem["kp"], n)
                    g.tensor_tensor(a(c, slot(7)), a(c, slot(10)), a(c, slot(14)), ALU.mult).then_inc(sem["kt"], 1)
                    g.tensor_tensor(a(c, slot(12)), a(c, slot(9)), a(c, slot(13)), ALU.mult).then_inc(sem["krr"], 1)
                elif name == "m":
                    pool.wait_ge(sem["m_ev"], n)
                    p0, p1 = i * PP // 2, (i + 1) * PP // 2
                    tt = a(c, TT_, 2 * W).rearrange("q (p u t) -> q p u t", u=2, t=T)[:, p0:p1]
                    m4 = a(c, M4_, 4 * W).rearrange("q (p u t) -> q p u t", u=4, t=T)[:, p0:p1]
                    g.tensor_tensor(tt[:, :, 0, :], pair(a(c, L_))[:, p0:p1], over_pairs(k("negm1"), PP // 2), ALU.mult)
                    g.tensor_tensor(tt[:, :, 1, :], m4[:, :, 2, :], over_pairs(k("negm1T"), PP // 2),
                                    ALU.mult).then_inc(sem["lv1"], 1)
                    pool.wait_ge(sem["lv1"], n)
                    tt2 = a(c, TT_ + 2 * p0 * T, W).rearrange("q (p t) -> q p t", t=2 * T)
                    g.tensor_tensor(tt2, tt2, over_pairs(k("eye2"), PP // 2), ALU.add).then_inc(sem["tt1"], 1)
                elif name == "var" and LNS[i] == "gn":
                    pool.wait_ge(sem["gn_a"], c + 1)
                    g.tensor_tensor(a(c, slot(10)), a(c, slot(10)), a(c, slot(8)), ALU.add).then_inc(sem["gn_b2"], 1)
                    pool.wait_ge(sem["gn_b2"], c + 1)
                    g.tensor_tensor(a(c, slot(10)), a(c, slot(10)), a(c, slot(16)), ALU.mult).then_inc(sem["gn_g"], 1)

        @block.scalar
        def _(act):
            s = nc.scalar
            loaded = [None]

            def tables(name):
                if loaded[0] != name:
                    s.preload_act_table_set(name)
                    loaded[0] = name

            tables(LN_EXP)
            act.wait_ge(sem["cst0"], 16)
            for name, i, c in ORDER:
                n = COUNT[name, i, c]
                if name == "tok":
                    act.wait_ge(sem["tok_mm"], n)
                    s.activation(a(c, H_), bank(c, 0), ACT.Identity, bias=vec("tok_b")).then_inc(sem["tok_y"], 1)
                elif name == "mean":
                    xc, sq = NORM_SLOTS[LNS[i]]
                    act.wait_ge(sem["ln_xc"], n)
                    s.activation(a(c, sq), a(c, xc), ACT.Square).then_inc(sem["ln_sq"], 1)
                elif name == "var":
                    sq = NORM_SLOTS[LNS[i]][1]
                    tables(LN_EXP)
                    act.wait_ge(sem["ln_var"], n)
                    s.activation(a(c, sq), bank(c, 1), ACT.Ln,
                                 bias=vec("eps_gn" if LNS[i] == "gn" else "eps_ln")).then_inc(sem["ln_log"], 1)
                    act.wait_ge(sem["ln_log"], n)
                    s.activation(a(c, sq), a(c, sq), ACT.Exp, scale=-0.5).then_inc(sem["ln_rs"], 1)
                elif name == "q":
                    if c == 0:
                        act.wait_ge(sem["init"], C)
                    act.wait_ge(sem["q_sum"], n)
                    for j in range(2):
                        r0, r1 = 64 * j, 64 * j + 64
                        qb = a(c, QBD_, PP * 128, r0, r1).rearrange("q (p t) -> q p t", t=128)
                        last = s.copy(qb[:, :, 64 * j:64 * j + T], pair(a(c, slot(2), W, r0, r1)))
                    last.then_inc(sem["q_bd"], 1)
                elif name == "s":
                    pb = a(c, PB_, 512).rearrange("q (h t) -> q h t", t=64)[:, :, 0:T]
                    tables(LN_EXP)
                    act.wait_ge(sem["s_sub"], n)
                    s.activation(pb, pb, ACT.Exp).then_inc(sem["s_exp"], 1)
                elif name == "t":
                    act.wait_ge(sem["pt_mm"], n)
                    s.copy(a(c, PT_, 512).rearrange("q (r t) -> q r t", t=64)[:, :, 0:T],
                           bank(c, 1, 512).rearrange("q (r t) -> q r t", t=64)[:, :, 0:T]).then_inc(sem["pt_ev"], 1)
                elif name == "attT":
                    act.wait_ge(sem["attT_mm"], n)
                    s.copy(a(c, slot(4)), bank(c, 0)).then_inc(sem["attT"], 1)
                elif name == "gate":
                    tables(LN_EXP)
                    act.wait_ge(sem["g_sub"], n)
                    s.activation(a(c, slot(9), PP * E), a(c, slot(9), PP * E), ACT.Exp).then_inc(sem["g_exp"], 1)
                elif name == "cwT":
                    act.wait_ge(sem["cwT_mm"], n)
                    s.copy(part_bf(c, 10), bank(c, 1)).then_inc(sem["c_hi"], 1)
                    act.wait_ge(sem["c_r"], n)
                    s.copy(part_bf(c, 11), a(c, slot(5))).then_inc(sem["c_mid"], 1)
                elif name == "hid":
                    tables("gelu_and_others")
                    act.wait_ge(sem["hid_mm"], n)
                    s.activation(halves(a(c, slot(6), 2 * W)), both(c), ACT.Gelu,
                                 bias=k("b1", i, i + 1)).then_inc(sem["gelu"], 1)
                elif name == "y":
                    act.wait_ge(sem["y_mm"], n)
                    s.copy(a(c, slot(8)), bank(c, 1)).then_inc(sem["cwb"], 1)
                elif name == "rk":
                    act.wait_ge(sem["rk_mm"], n)
                    s.copy(halves(a(c, slot(9), 2 * W)), both(c)).then_inc(sem["rk"], 1)
                elif name == "vw":
                    tables("sigmoid_and_others")
                    act.wait_ge(sem["vw_mm"], n)
                    s.copy(a(c, slot(11)), bank(c, 0))
                    s.activation(a(c, slot(12)), bank(c, 1), ACT.Tanh).then_inc(sem["vw"], 1)
                    act.wait_ge(sem["kk0"], n)
                    s.activation(a(c, slot(4)), a(c, slot(3)), ACT.Square).then_inc(sem["kk_sq"], 1)
                elif name == "aw":
                    tables("sigmoid_and_others")
                    act.wait_ge(sem["aw_mm"], n)
                    s.activation(a(c, slot(14)), bank(c, 1), ACT.Sigmoid, bias=vec("b_w")).then_inc(sem["aw_sg"], 1)
                elif name == "ab":
                    tables("sigmoid_and_others")
                    act.wait_ge(sem["ab_mm"], n)
                    s.activation(a(c, slot(15)), bank(c, 0), ACT.Sigmoid, bias=vec("b_a")).then_inc(sem["ab"], 1)
                elif name == "gh":
                    tables("sigmoid_and_others")
                    act.wait_ge(sem["g_hid"], n)
                    s.activation(halves(a(c, slot(16), 2 * W)), both(c), ACT.Sigmoid).then_inc(sem["g_sig"], 1)
                elif name == "gg":
                    act.wait_ge(sem["gg_mm"], n)
                    s.copy(a(c, slot(16)), bank(c, 0)).then_inc(sem["gg"], 1)
                elif name == "kk":
                    tables(LN_EXP)
                    act.wait_ge(sem["cs"], n)
                    s.activation(a(c, slot(13)), a(c, slot(12)), ACT.Exp, scale=DECAY).then_inc(sem["ep"], 1)
                    s.activation(a(c, slot(14)), a(c, slot(12)), ACT.Exp, scale=-DECAY).then_inc(sem["em"], 1)
                    act.wait_ge(sem["kk_cl"], n)
                    s.activation(a(c, slot(4)), a(c, slot(4)), ACT.Ln, scale=SS_SCALE).then_inc(sem["kk_ln"], 1)
                    act.wait_ge(sem["kk_ln"], n)
                    s.activation(a(c, slot(4)), a(c, slot(4)), ACT.Exp, scale=-0.5,
                                 bias=vec("ten_ln2")).then_inc(sem["kk_rs"], 1)
                elif name == "bon":
                    act.wait_ge(sem["krr"], n)
                    for j in range(2):
                        kr = a(c, KR_[j], 2 * W).rearrange("q (p u t) -> q p u t", u=2, t=T)
                        last = s.activation(kr[:, :, 1, :], pair(a(c, slot(12))), ACT.Copy, scale=vec(f"feat{j}"))
                    last.then_inc(sem["krb"], 1)
                elif name == "m":
                    act.wait_ge(sem["m_ev"], n)
                    p0, p1 = i * PP // 2, (i + 1) * PP // 2
                    for j in range(2):
                        last = s.activation(pair(a(c, LT_[j]))[:, p0:p1], m2(c)[:, p0:p1], ACT.Copy, scale=vec(f"tok{j}"))
                    last.then_inc(sem["ltb"], 1)
                elif name == "vt":
                    act.wait_ge(sem["vt_mm"], n)
                    for j in range(2):
                        last = s.activation(a(c, VT_[j], 512), bank(c, 0, 512), ACT.Copy, scale=vec(f"tok{j}"))
                    last.then_inc(sem["vt"], 1)
                elif name == "lt" and i == len(LEVELS) - 1:
                    act.wait_ge(sem["t_ev"], n)
                    for j in range(2):
                        last = s.activation(pair(a(c, TB_[j])), a(c, TT_, 2 * W).rearrange(
                            "q (p u t) -> q p u t", u=2, t=T)[:, :, 1, :], ACT.Copy, scale=vec(f"tok{j}"))
                    last.then_inc(sem["ttb"], 1)
                    for j in range(2):
                        last = s.activation(pair(a(c, LT_[j])), m2(c), ACT.Copy, scale=vec(f"early{j}"))
                    last.then_inc(sem["lt32"], 1)
                elif name == "u":
                    act.wait_ge(sem["u_mm"], n)
                    s.copy(a(c, U_, 512), bank(c, 0, 512)).then_inc(sem["u_ev"], 1)
                elif name == "y2":
                    act.wait_ge(sem["ttb"], n)
                    act.wait_ge(sem["y_mm2"], n)
                    s.copy(a(c, Y_, 512), bank(c, 1, 512)).then_inc(sem["y_ev"], 1)
                elif name == "z":
                    act.wait_ge(sem["z_mm"], n)
                    s.activation(a(c, U_, 512), bank(c, 0, 512), ACT.Copy, scale=k("row32")).then_inc(sem["z_ev"], 1)
                elif name == "w":
                    act.wait_ge(sem["sa"], 2 * n - 1)
                    s.activation(a(c, SA_[0], 512), a(c, Y_, 512), ACT.Copy, scale=vec("tok0")).then_inc(sem["sab"], 1)
                elif name == "o":
                    act.wait_ge(sem["o_mm"], n)
                    s.copy(a(c, slot(9)), bank(c, 0)).then_inc(sem["o_ev"], 1)
                elif name == "f":
                    act.wait_ge(sem["f_mm"], n)
                    s.activation(halves(a(c, slot(2), 2 * W)), both(c), ACT.Relu, bias=vec("bi")).then_inc(sem["f_relu"], 1)
                elif name == "r":
                    act.wait_ge(sem["r_mm"], n)
                    s.activation(halves(a(c, slot(4 if i == 0 else 2), 2 * W)), both(c), ACT.Relu).then_inc(
                        sem["r_relu"], 1)

        @block.vector
        def _(dve):
            v = nc.vector
            for b in range(2 * C):
                last = v.memset(PS[:, b, :], 1.0)
            last.then_inc(sem["psum0"], 1)
            dve.wait_ge(sem["cst0"], 16)
            v.tensor_scalar(oneka[:], vec("k_a"), -1.0, 1.0, ALU.mult, ALU.add).then_inc(sem["oneka"], 1)

            def route_ids():
                rows = 3 * (NR + 1)
                dve.wait_ge(sem["ids"], 32)
                v.tensor_scalar(rtmp[:, 0, :], rid[:], 0.0, None, ALU.is_ge).then_inc(sem["r_steps"], 1)
                v.tensor_scalar(rtmp[:, 1, :], rid[:], float(NR - 1), None, ALU.is_le).then_inc(sem["r_steps"], 1)
                v.tensor_scalar(rtmp[:, 2, :], rid[:], float(-NR), None, ALU.add).then_inc(sem["r_steps"], 1)
                v.tensor_scalar(oneh[:], ridb[:], vec("eidx")[0:rows, :], vec("shared")[0:rows, :],
                                ALU.is_equal, ALU.max).then_inc(sem["r_oh"], 1)
                dve.wait_ge(sem["r_steps"], 2)
                v.tensor_tensor(rtmp[:, 3, :], rtmp[:, 0, :], rtmp[:, 1, :], ALU.mult).then_inc(sem["r_steps"], 1)
                dve.wait_ge(sem["r_steps"], 4)
                v.tensor_tensor(rtmp[:, 0, :], rtmp[:, 3, :], rtmp[:, 2, :], ALU.mult).then_inc(sem["r_steps"], 1)
                dve.wait_ge(sem["r_steps"], 5)
                v.tensor_scalar(ride[:], rtmp[:, 0, :], float(NR), None, ALU.add).then_inc(sem["r_id"], 1)
                dve.wait_ge(sem["cst4"], 16)
                rb = k("Rb", 0, NL * 128, 0, rows)
                hi, out_ = rb_split[:, 0, :], rb_split[:, 1, :]
                v.tensor_copy(hi, rb).then_inc(sem["rb_steps"], 1)
                dve.wait_ge(sem["rb_steps"], 1)
                v.scalar_tensor_tensor(out=rb, in0=hi, scalar=vec("rb_mid")[0:rows, :], in1=rb, op0=ALU.mult,
                                       op1=ALU.add).then_inc(sem["rb_steps"], 1)
                dve.wait_ge(sem["rb_steps"], 2)
                v.tensor_copy(hi, rb).then_inc(sem["rb_steps"], 1)
                dve.wait_ge(sem["rb_steps"], 3)
                v.scalar_tensor_tensor(out=out_, in0=hi, scalar=vec("rb_low")[0:rows, :], in1=rb, op0=ALU.mult,
                                       op1=ALU.add).then_inc(sem["rb_split"], 1)

            small = PP * E
            for name, i, c in ORDER:
                n = COUNT[name, i, c]
                if name == "mean":
                    src = slot(9) if LNS[i] == "gn" else H_
                    dve.wait_ge(sem["ln_mean"], n)
                    v.tensor_tensor(a(c, NORM_SLOTS[LNS[i]][0]), a(c, src), bank(c, 0),
                                    ALU.subtract).then_inc(sem["ln_xc"], 1)
                elif name == "var":
                    xc, sq = NORM_SLOTS[LNS[i]]
                    dst = xc if LNS[i] in ("lt", "gn") else N_
                    dve.wait_ge(sem["ln_rs"], n)
                    v.tensor_tensor(a(c, dst), a(c, xc), a(c, sq), ALU.mult).then_inc(sem["ln_out"], 1)
                    if LNS[i] == "lt":
                        dve.wait_ge(sem["ln_out"], n)
                        v.tensor_scalar(a(c, H_), a(c, dst), vec("gamma"), vec("beta"), ALU.mult,
                                        ALU.add).then_inc(sem["h0"], 1)
                    if LNS[i] == "gn":
                        dve.wait_ge(sem["ln_out"], n)
                        v.tensor_scalar(a(c, dst), a(c, dst), vec("gn_w"), vec("gn_b"), ALU.mult,
                                        ALU.add).then_inc(sem["gn_a"], 1)
                    if LNS[i] == "l3":
                        d, x = pair(a(c, slot(2))), pair(a(c, N_))
                        dve.wait_ge(sem["ln_out"], n)
                        v.tensor_tensor(d[:, :, 1:T], x[:, :, 0:T - 1], x[:, :, 1:T], ALU.subtract)
                        v.tensor_scalar(d[:, :, 0:1], x[:, :, 0:1], -1.0, None, ALU.mult).then_inc(sem["delta"], 1)
                        dve.wait_ge(sem["delta"], c + 1)
                        for u in range(6):
                            last = v.scalar_tensor_tensor(out=a(c, slot(3 + u)), in0=a(c, slot(2)),
                                                          scalar=vec(f"mix{u}"), in1=a(c, N_), op0=ALU.mult, op1=ALU.add)
                            last.then_inc(sem["xi"], 1)
                elif name in ("q", "k"):
                    if c == 0:
                        dve.wait_ge(sem["cst1"], 16)
                    d0, d1 = (slot(2), slot(3)) if name == "q" else (slot(4), PT_)
                    dve.wait_ge(sem[f"{name}_mm"], n)
                    v.tensor_tensor(pair(a(c, d0)), pair(bank(c, 0)), over_pairs(k(f"cos{name}")), ALU.mult)
                    v.tensor_tensor(pair(a(c, d1)), pair(bank(c, 1)), over_pairs(k(f"sin{name}")),
                                    ALU.mult).then_inc(sem[f"{name}_mul"], 1)
                elif name == "v":
                    if c == 0:
                        dve.wait_ge(sem["init"], C)
                    dve.wait_ge(sem["v_mm"], n)
                    for hh in range(2):
                        r0, r1 = 64 * hh, 64 * hh + 64
                        ones = a(c, VD_, PP * 2 * NKV * 18, r0, r1).rearrange("q (r u) -> q r u", u=18)
                        v.memset(ones[:, :, 9 * hh + 8:9 * hh + 9], 1.0)
                        for j in range(2):
                            vd = a(c, VD_, PP * 2 * NKV * 18, r0, r1).rearrange("q (p j g u) -> q p j g u", j=2, g=NKV,
                                                                                u=18)
                            last = v.tensor_copy(vd[:, :, j, :, 9 * hh:9 * hh + HD],
                                                 bank(c, j, PP * NKV * HD, 0, r0, r1).rearrange(
                                                     "q (p g d) -> q p g d", g=NKV, d=HD))
                    last.then_inc(sem["vd"], 1)
                    if c == 0:
                        route_ids()
                elif name == "s":
                    sc = bank(c, 0).rearrange("q (h t) -> q h t", t=T)
                    dve.wait_ge(sem["s_mm"], n)
                    v.tensor_reduce(smax[:, c, :], sc, AX.X, ALU.max).then_inc(sem["s_max"], 1)
                    dve.wait_ge(sem["s_max"], n)
                    v.tensor_tensor(a(c, PB_, 512).rearrange("q (h t) -> q h t", t=64)[:, :, 0:T], sc,
                                    smax[:, c, :].unsqueeze(2).broadcast_to([128, NH, T]),
                                    ALU.subtract).then_inc(sem["s_sub"], 1)
                elif name == "pvb":
                    o = bank(c, 0, 2 * NH * 9, W).rearrange("q (r u) -> q r u", u=9)
                    dve.wait_ge(sem["pv_mm"], n)
                    v.reciprocal(orec[:, c, :].unsqueeze(2), o[:, :, HD:HD + 1]).then_inc(sem["o_rec"], 1)
                    dve.wait_ge(sem["o_rec"], n)
                    v.tensor_tensor(a(c, slot(2) + (i - 1) * D, 2 * D).rearrange("q (r d) -> q r d", d=HD),
                                    o[:, :, 0:HD], orec[:, c, :].unsqueeze(2).broadcast_to([128, 2 * NH, HD]),
                                    ALU.mult).then_inc(sem["att"], 1)
                elif name == "wo":
                    dve.wait_ge(sem["wo_mm"], n)
                    v.tensor_tensor(a(c, H_), a(c, H_), bank(c, 1), ALU.add).then_inc(sem["h1"], 1)
                elif name == "gate":
                    if c == 0:
                        dve.wait_ge(sem["cst2"], 16)
                    lg = a(c, slot(9), small).rearrange("q (p e) -> q p e", e=E)
                    mx, sm = a(c, slot(9) + small, PP), a(c, slot(9) + 2 * small, PP)
                    cnt, cw = a(c, slot(9) + 3 * small, small), a(c, slot(9) + 4 * small, small)
                    gt, eq = a(c, slot(10), small * E), a(c, slot(12), small * E)
                    other = lg.unsqueeze(2).broadcast_to([128, PP, E, E])
                    self_ = lg.unsqueeze(3).broadcast_to([128, PP, E, E])
                    dve.wait_ge(sem["gate_mm"], n)
                    v.tensor_tensor(lg, bank(c, 0, small).rearrange("q (p e) -> q p e", e=E), over_pairs(k("gb")),
                                    ALU.add).then_inc(sem["g_steps"], 1)
                    dve.wait_ge(sem["g_steps"], 9 * (n - 1) + 1)
                    v.tensor_reduce(mx, lg, AX.X, ALU.max).then_inc(sem["g_steps"], 1)
                    dve.wait_ge(sem["g_steps"], 9 * (n - 1) + 2)
                    v.tensor_tensor(lg, lg, mx.unsqueeze(2).broadcast_to([128, PP, E]),
                                    ALU.subtract).then_inc(sem["g_sub"], 1)
                    dve.wait_ge(sem["g_exp"], n)
                    v.tensor_reduce(sm, lg, AX.X, ALU.add).then_inc(sem["g_steps"], 1)
                    dve.wait_ge(sem["g_steps"], 9 * (n - 1) + 3)
                    v.reciprocal(sm, sm).then_inc(sem["g_steps"], 1)
                    dve.wait_ge(sem["g_steps"], 9 * (n - 1) + 4)
                    v.tensor_tensor(lg, lg, sm.unsqueeze(2).broadcast_to([128, PP, E]), ALU.mult).then_inc(sem["g_steps"], 1)
                    dve.wait_ge(sem["g_steps"], 9 * (n - 1) + 5)
                    v.tensor_tensor(eq.rearrange("q (p e f) -> q p e f", e=E, f=E), other, self_,
                                    ALU.is_equal).then_inc(sem["g_cmp"], 1)
                    v.tensor_tensor(gt.rearrange("q (p e f) -> q p e f", e=E, f=E), other, self_,
                                    ALU.is_gt).then_inc(sem["g_cmp"], 1)
                    dve.wait_ge(sem["g_cmp"], 2 * n)
                    eqp = eq.rearrange("q (p r) -> q p r", r=E * E)
                    v.tensor_tensor(eqp, eqp, over_pairs(k("tri")), ALU.mult).then_inc(sem["g_steps"], 1)
                    dve.wait_ge(sem["g_steps"], 9 * (n - 1) + 6)
                    v.tensor_tensor(gt, gt, eq, ALU.add).then_inc(sem["g_steps"], 1)
                    dve.wait_ge(sem["g_steps"], 9 * (n - 1) + 7)
                    v.tensor_reduce(cnt, gt.rearrange("q (r f) -> q r f", f=E), AX.X, ALU.add).then_inc(sem["g_steps"], 1)
                    dve.wait_ge(sem["g_steps"], 9 * (n - 1) + 8)
                    v.scalar_tensor_tensor(out=cw, in0=cnt, scalar=2.0, in1=a(c, slot(9), small), op0=ALU.is_lt,
                                           op1=ALU.mult).then_inc(sem["g_steps"], 1)
                    dve.wait_ge(sem["g_steps"], 9 * n)
                    v.tensor_copy(a(c, CW_, 3 * small).rearrange("q (p r e) -> q p r e", r=3, e=E),
                                  cw.rearrange("q (p e) -> q p e", e=E).unsqueeze(2).broadcast_to(
                                      [128, PP, 3, E])).then_inc(sem["cw"], 1)
                elif name == "cwT":
                    dve.wait_ge(sem["c_hi"], n)
                    v.scalar_tensor_tensor(out=a(c, slot(5)), in0=part_bf(c, 10), scalar=vec("cw_mid"), in1=bank(c, 1),
                                           op0=ALU.mult, op1=ALU.add).then_inc(sem["c_r"], 1)
                    dve.wait_ge(sem["c_mid"], n)
                    v.scalar_tensor_tensor(out=part_bf(c, 12), in0=part_bf(c, 11), scalar=vec("cw_low"),
                                           in1=a(c, slot(5)), op0=ALU.mult, op1=ALU.add).then_inc(sem["cwT"], 1)
                elif name == "b2":
                    dve.wait_ge(sem["b2_mm"], n)
                    v.tensor_tensor(a(c, H_), a(c, H_), bank(c, 0), ALU.add).then_inc(sem["b2_add"], 1)
                elif name == "y":
                    dve.wait_ge(sem["cwb"], n)
                    if i >= 2:
                        dve.wait_ge(sem["acc"], COUNT["y", i - 2, c])
                    v.tensor_tensor(a(c, slot(3 + i % 2)), bank(c, 0), a(c, slot(8)), ALU.mult).then_inc(sem["y_mul"], 1)
                elif name == "rk":
                    if c == 0:
                        dve.wait_ge(sem["cst3"], 16)
                        dve.wait_ge(sem["oneka"], 1)
                    dve.wait_ge(sem["rk"], n)
                    v.tensor_scalar(a(c, slot(3)), a(c, slot(10)), vec("k_k"), None, ALU.mult).then_inc(sem["kk0"], 1)
                elif name == "aw":
                    dve.wait_ge(sem["aw_mm"], n)
                    v.tensor_copy(a(c, slot(13)), bank(c, 0)).then_inc(sem["aw_aa"], 1)
                    dve.wait_ge(sem["aw_sg"], n)
                    v.tensor_tensor_scan(a(c, slot(12)), k("reset"), a(c, slot(14)), 0.0, ALU.mult,
                                         ALU.add).then_inc(sem["cs"], 1)
                elif name == "kk":
                    dve.wait_ge(sem["kk_mm"], n)
                    v.tensor_scalar(a(c, slot(4)), bank(c, 1), float(D), 1e-24, ALU.mult,
                                    ALU.max).then_inc(sem["kk_cl"], 1)
                    dve.wait_ge(sem["em"], n)
                    v.tensor_scalar(a(c, slot(12)), a(c, slot(15)), vec("k_a"), oneka[:], ALU.mult,
                                    ALU.add).then_inc(sem["tk"], 1)
                    dve.wait_ge(sem["tk"], n)
                    v.tensor_tensor(a(c, slot(10)), a(c, slot(10)), a(c, slot(12)), ALU.mult).then_inc(sem["kp"], 1)
                    dve.wait_ge(sem["kp"], n)
                    v.scalar_tensor_tensor(out=a(c, slot(8)), in0=a(c, slot(9)), scalar=vec("r_k"), in1=a(c, slot(10)),
                                           op0=ALU.mult, op1=ALU.mult).then_inc(sem["bon0"], 1)
                    dve.wait_ge(sem["kk_rs"], n)
                    v.tensor_tensor(a(c, slot(3)), a(c, slot(3)), a(c, slot(4)), ALU.mult).then_inc(sem["kk"], 1)
                    dve.wait_ge(sem["kk"], n)
                    for j in range(2):
                        kr = a(c, KR_[j], 2 * W).rearrange("q (p u t) -> q p u t", u=2, t=T)
                        v.scalar_tensor_tensor(out=kr[:, :, 0, 1:T], in0=pair(a(c, slot(3)))[:, :, 1:T],
                                               scalar=vec(f"feat{j}"), in1=pair(a(c, slot(13)))[:, :, 0:T - 1],
                                               op0=ALU.mult, op1=ALU.mult)
                        last = v.tensor_scalar(kr[:, :, 0, 0:1], pair(a(c, slot(3)))[:, :, 0:1], vec(f"feat{j}"), None,
                                               ALU.mult)
                    last.then_inc(sem["kr1"], 1)
                elif name == "bon":
                    dve.wait_ge(sem["bon_mm"], n)
                    v.scalar_tensor_tensor(out=a(c, slot(8)), in0=bank(c, 1), scalar=float(D), in1=a(c, slot(11)),
                                           op0=ALU.mult, op1=ALU.mult).then_inc(sem["bon"], 1)
                elif name == "m":
                    dve.wait_ge(sem["m_mm"], n)
                    src = PS[:, 2 * c:2 * c + 2, 0:10 * T].rearrange("q b (i u) -> q b i u", u=5 * T)
                    m4 = a(c, M4_ + i * 2 * W, 2 * W).rearrange("q (b i u) -> q b i u", b=2, u=4 * T)
                    lm = a(c, L_ + i * (W // 2), W // 2).rearrange("q (b i u) -> q b i u", b=2, u=T)
                    v.tensor_tensor(m4, src[:, :, :, 0:4 * T],
                                    k("mask4").unsqueeze(1).unsqueeze(1).broadcast_to([128, 2, 2, 4 * T]),
                                    ALU.mult)
                    v.tensor_tensor(lm, src[:, :, :, 4 * T:5 * T],
                                    k("maskL").unsqueeze(1).unsqueeze(1).broadcast_to([128, 2, 2, T]),
                                    ALU.mult).then_inc(sem["m_ev"], 1)
                elif name == "lx":
                    dve.wait_ge(sem["x_mm"], n)
                    x = a(c, X_[0], 2 * (X_[1] - X_[0])).rearrange("q (j w) -> q j w", j=2)[:, :, 0:W]
                    level = k("levels", 2 * i * T, 2 * (i + 1) * T).rearrange("q (j t) -> q j t", j=2)
                    v.tensor_tensor(x.rearrange("q j (p t) -> q j p t", t=T),
                                    pair(bank(c, 0)).unsqueeze(1).broadcast_to([128, 2, PP, T]),
                                    level.unsqueeze(2).broadcast_to([128, 2, PP, T]), ALU.mult).then_inc(sem["x_ev"], 1)
                elif name == "lt":
                    dve.wait_ge(sem["t_mm"], n)
                    if i < len(LEVELS) - 1:
                        tt = halves(a(c, TT_, 2 * W))
                        v.tensor_tensor(tt, tt, both(c), ALU.subtract).then_inc(sem["t_ev"], 1)
                    else:
                        tt = a(c, TT_, 2 * W).rearrange("q (p u t) -> q p u t", u=2, t=T)[:, :, 1, :]
                        v.tensor_tensor(tt, tt, pair(bank(c, 1)), ALU.subtract).then_inc(sem["t_ev"], 1)
                elif name == "w":
                    dve.wait_ge(sem["w_mm"], n)
                    v.tensor_tensor(a(c, Y_, 512), a(c, Y_, 512), bank(c, 1, 512), ALU.subtract).then_inc(sem["sa"], 1)
                    dve.wait_ge(sem["sa"], 2 * n - 1)
                    v.tensor_scalar(a(c, SA_[1], 512), a(c, Y_, 512), vec("tok1"), None, ALU.mult).then_inc(sem["sa"], 1)
                elif name == "ro":
                    dve.wait_ge(sem["ro_mm"], n)
                    v.tensor_tensor(a(c, H_), a(c, H_), bank(c, 0), ALU.add).then_inc(sem["h3"], 1)
                elif name == "fo":
                    dve.wait_ge(sem["fo_mm"], n)
                    v.scalar_tensor_tensor(out=a(c, slot(6)), in0=bank(c, 0), scalar=vec("bo"), in1=a(c, H_), op0=ALU.add,
                                           op1=ALU.add).then_inc(sem["fo"], 1)

        @block.tensor
        def _(pe):
            def mm(o, l, r, start=True, stop=True):
                return nc.tensor.matmul(o, l, r, start=start, stop=stop)

            def m4(c, p, u):
                return a(c, M4_ + (4 * p + u) * T, T)

            def tt(c, p, u):
                return a(c, TT_ + (2 * p + u) * T, T)

            pairs = [(i, j) for i in range(PP) for j in range(2)]
            pe.wait_ge(sem["psum0"], 1)
            pe.wait_ge(sem["cst0"], 16)
            for name, i, c in ORDER:
                n = COUNT[name, i, c]
                if name == "tok":
                    pe.wait_ge(sem[f"x{c}"], 16)
                    xt = a(c, XT_, 2 * PP * CH).rearrange("q (j p t) -> q j p t", j=2, t=CH)
                    for j in range(2):
                        mm(bank(c, 0, W, 0, 64 * j, 64 * j + 64), k("tokA"), xt[:, j, :, 0:T], stop=False)
                        last = mm(bank(c, 0, W, 0, 64 * j, 64 * j + 64), k("tokB"), xt[:, j, :, 1:T + 1], start=False)
                    last.then_inc(sem["tok_mm"], 1)
                elif name == "mean":
                    ready = {"lt": ("tok_y", c + 1), "l1": ("h0", c + 1), "l2": ("h1", c + 1),
                             "l3": ("acc", COUNT["y", E - 1, c]), "gn": ("o_ev", c + 1), "l4": ("h3", c + 1)}[LNS[i]]
                    pe.wait_ge(sem[ready[0]], ready[1])
                    src = slot(9) if LNS[i] == "gn" else H_
                    mm(bank(c, 0), k("mean"), a(c, src)).then_inc(sem["ln_mean"], 1)
                elif name == "var":
                    pe.wait_ge(sem["ln_sq"], COUNT["mean", i, c])
                    mm(bank(c, 1), k("mean"), a(c, NORM_SLOTS[LNS[i]][1])).then_inc(sem["ln_var"], 1)
                elif name == "q":
                    if c == 0:
                        pe.wait_ge(sem["cst1"], 16)
                    pe.wait_ge(sem["ln_out"], COUNT["var", 1, c])
                    mm(bank(c, 0), k("wq"), a(c, N_))
                    mm(bank(c, 1), k("wqr"), a(c, N_)).then_inc(sem["q_mm"], 1)
                elif name == "k":
                    pe.wait_ge(sem["q_mul"], n)
                    mm(bank(c, 0), k("wk"), a(c, N_))
                    mm(bank(c, 1), k("wkr"), a(c, N_)).then_inc(sem["k_mm"], 1)
                elif name == "v":
                    pe.wait_ge(sem["k_mul"], n)
                    for hh in range(2):
                        for p, j in pairs:
                            last = mm(PS[64 * hh:64 * hh + T, 2 * c + j, 32 * p:32 * p + 32],
                                      half(c, N_, j, p * T, T, 64), k("wv", 0, 32, 64 * j, 64 * j + 64))
                    last.then_inc(sem["v_mm"], 1)
                elif name == "s":
                    if i == 0:
                        if c == 0:
                            pe.wait_ge(sem["cst_bf"], 16)
                        pe.wait_ge(sem["kx"], c + 1)
                        pe.wait_ge(sem["q_bd"], c + 1)
                        pe.wait_ge(sem["vd"], c + 1)
                    elif i % 2 == 0:
                        pe.wait_ge(sem["att"], COUNT["pvb", i - 1, c])
                    mm(bank(c, 0).rearrange("q (h t) -> q h t", t=T), identb,
                       maskb.unsqueeze(1).broadcast_to([128, NH, T]), stop=False)
                    mm(bank(c, 0), a(c, QBD_ + 128 * i, 128), a(c, KX_ + i * W), start=False).then_inc(sem["s_mm"], 1)
                elif name == "t":
                    pe.wait_ge(sem["s_exp"], n)
                    for g in range(NKV):
                        last = nc.tensor.transpose(bank(c, 1, 128, 128 * g), a(c, PB_ + 128 * g, 128), k("identf"))
                    last.then_inc(sem["pt_mm"], 1)
                elif name in ("pva", "pvb"):
                    pe.wait_ge(sem["pt_ev"], COUNT["t", i, c])
                    for g in range(NKV):
                        for j in range(2):
                            col = W + (i % 2) * NH * 9 + 18 * g
                            last = mm(PS[64 * j:64 * j + T, 2 * c, col:col + 18],
                                      a(c, PT_ + 128 * g + 64 * j, T, 0, 64 + T),
                                      a(c, VD_ + ((i * 2 + j) * NKV + g) * 18, 18, 0, 64 + T))
                    if name == "pvb":
                        last.then_inc(sem["pv_mm"], 1)
                elif name == "attT":
                    pe.wait_ge(sem["att"], COUNT["pvb", PP - 1, c])
                    for p, j in pairs:
                        last = mm(bank(c, 0, T, p * T, 64 * j, 64 * j + 64), half(c, slot(2), j, p * D, D),
                                  k("identd", 0, T, 64 * j, 64 * j + T))
                    last.then_inc(sem["attT_mm"], 1)
                elif name == "wo":
                    pe.wait_ge(sem["attT"], n)
                    mm(bank(c, 1), k("wo"), a(c, slot(4))).then_inc(sem["wo_mm"], 1)
                elif name == "gate":
                    if c == 0:
                        pe.wait_ge(sem["cst2"], 16)
                    pe.wait_ge(sem["ln_out"], COUNT["var", 2, c])
                    for p, j in pairs:
                        last = mm(to_bank(c, 0, E, j, p, T), half(c, N_, j, p * T, T, 64), k("gw", 0, E, 64 * j, 64 * j + 64))
                    last.then_inc(sem["gate_mm"], 1)
                elif name == "cwT":
                    pe.wait_ge(sem["cw"], n)
                    for p, j in pairs:
                        last = mm(to_bank(c, 1, T, j, p, 3 * E), half(c, CW_, j, 3 * p * E, 3 * E), k("identd", 0, T, 64 * j, 64 * j + T))
                    last.then_inc(sem["cwT_mm"], 1)
                elif name == "b2":
                    pe.wait_ge(sem["cwT"], n)
                    mm(bank(c, 0), k("b2"), a(c, slot(5))).then_inc(sem["b2_mm"], 1)
                elif name == "hid":
                    if i == 0:
                        pe.wait_ge(sem["b2_add"], c + 1)
                    else:
                        pe.wait_ge(sem["y_mul"], COUNT["y", i - 1, c])
                    for j in range(2):
                        last = mm(bank(c, j), k("w1", i * HID, i * HID + HID, 64 * j, 64 * j + 64), half(c, N_, j, 0, W, 64))
                    last.then_inc(sem["hid_mm"], 1)
                elif name == "y":
                    pe.wait_ge(sem["gelu"], n)
                    for j in range(2):
                        mm(bank(c, 0, W, 0, 64 * j, 64 * j + 64), k("w2", i * D, i * D + D), a(c, slot(6 + j)))
                    mm(bank(c, 1), selb[:, i * 128:i * 128 + 128], part_bf(c, 12)).then_inc(sem["y_mm"], 1)
                elif name == "rk":
                    if c == 0:
                        pe.wait_ge(sem["cst3"], 16)
                    pe.wait_ge(sem["xi"], 6 * n)
                    mm(bank(c, 0), k("Wr"), a(c, slot(3)))
                    mm(bank(c, 1), k("Wk"), a(c, slot(5))).then_inc(sem["rk_mm"], 1)
                elif name == "vw":
                    pe.wait_ge(sem["rk"], n)
                    mm(bank(c, 0), k("Wvf"), a(c, slot(6)))
                    mm(bank(c, 1), k("Aw"), a(c, slot(4))).then_inc(sem["vw_mm"], 1)
                elif name == "aw":
                    pe.wait_ge(sem["vw"], n)
                    mm(bank(c, 0), k("Aa"), a(c, slot(7)))
                    mm(bank(c, 1), k("Bw"), a(c, slot(12))).then_inc(sem["aw_mm"], 1)
                elif name == "ab":
                    pe.wait_ge(sem["aw_aa"], n)
                    mm(bank(c, 0), k("Ba"), a(c, slot(13))).then_inc(sem["ab_mm"], 1)
                elif name == "gh":
                    pe.wait_ge(sem["ab"], n)
                    pe.wait_ge(sem["aw_sg"], n)
                    for j in range(2):
                        last = mm(bank(c, j), k("Ag", 0, 128, 64 * j, 64 * j + 64), half(c, slot(8), j, 0, W, 64))
                    last.then_inc(sem["g_hid"], 1)
                elif name == "gg":
                    pe.wait_ge(sem["g_sig"], n)
                    for j in range(2):
                        last = mm(bank(c, 0, W, 0, 64 * j, 64 * j + 64), k("Bg"), a(c, slot(16 + j)))
                    last.then_inc(sem["gg_mm"], 1)
                elif name == "kk":
                    pe.wait_ge(sem["kk_sq"], n)
                    mm(bank(c, 1), k("mean"), a(c, slot(4))).then_inc(sem["kk_mm"], 1)
                elif name == "bon":
                    pe.wait_ge(sem["bon0"], n)
                    pe.wait_ge(sem["kk_cl"], n)
                    mm(bank(c, 1), k("mean"), a(c, slot(8))).then_inc(sem["bon_mm"], 1)
                elif name == "m":
                    if i == 0:
                        for ready in ("bt", "kt", "krb", "kr1", "bon"):
                            pe.wait_ge(sem[ready], COUNT["kk", 0, c])
                    else:
                        pe.wait_ge(sem["m_ev"], COUNT["m", 0, c])
                    for q in range(PP // 2):
                        p = i * PP // 2 + q
                        kt, bt = a(c, slot(7) + p * T, T), a(c, slot(5) + p * T, T)
                        for u in range(3):
                            for j in range(2):
                                kr = KR_[j] + 2 * p * T
                                l, r = [(kt, a(c, kr, 2 * T)), (bt, a(c, kr, 2 * T)), (a(c, kr, T), bt)][u]
                                col = (q % 2) * 5 * T + 2 * T * u
                                last = mm(PS[64 * j:64 * j + T, 2 * c + q // 2, col:col + (1 if u == 2 else 2) * T], l, r)
                    last.then_inc(sem["m_mm"], 1)
                elif name == "vt":
                    pe.wait_ge(sem["m_ev"], COUNT["m", 1, c])
                    for p, j in pairs:
                        last = mm(to_bank(c, 0, D, j, p, T), half(c, slot(6), j, p * T, T, 64),
                                  k("Wvt", 0, D, 64 * j, 64 * j + 64))
                    last.then_inc(sem["vt_mm"], 1)
                elif name == "lx":
                    if i == 0:
                        pe.wait_ge(sem["tt1"], COUNT["m", 1, c])
                        pe.wait_ge(sem["ltb"], COUNT["m", 1, c])
                        pe.wait_ge(sem["vt"], COUNT["vt", 0, c])
                    else:
                        pe.wait_ge(sem["t_ev"], COUNT["lt", i - 1, c])
                    for p, j in pairs:
                        last = mm(to_bank(c, 0, T, j, p, T), a(c, LT_[j] + p * T, T), tt(c, p, 0))
                    last.then_inc(sem["x_mm"], 1)
                elif name == "lt":
                    pe.wait_ge(sem["x_ev"], n)
                    for p in range(PP):
                        if i < len(LEVELS) - 1:
                            lo = (p % 4) * 2 * T
                            for j in range(2):
                                last = mm(PS[64 * j:64 * j + T, 2 * c + p // 4, lo:lo + T], tt(c, p, 1),
                                          a(c, X_[j] + p * T, T))
                            for j in range(2):
                                last = mm(PS[64 * j:64 * j + T, 2 * c + p // 4, lo + T:lo + 2 * T],
                                          a(c, X_[j] + p * T, T), tt(c, p, 1))
                        else:
                            for j in range(2):
                                last = mm(to_bank(c, 1, T, j, p, T), a(c, X_[j] + p * T, T), tt(c, p, 1))
                    last.then_inc(sem["t_mm"], 1)
                elif name == "u":
                    pe.wait_ge(sem["t_ev"], COUNT["lt", len(LEVELS) - 1, c])
                    for p, j in pairs:
                        last = mm(to_bank(c, 0, D, j, p, T), m4(c, p, 0), a(c, VT_[j] + p * D, D))
                    last.then_inc(sem["u_mm"], 1)
                elif name == "y2":
                    pe.wait_ge(sem["ttb"], n)
                    pe.wait_ge(sem["u_ev"], n)
                    for p, j in pairs:
                        last = mm(to_bank(c, 1, D, j, p, T), a(c, TB_[j] + p * T, T), a(c, U_ + p * D, D))
                    last.then_inc(sem["y_mm2"], 1)
                elif name == "z":
                    pe.wait_ge(sem["lt32"], n)
                    pe.wait_ge(sem["y_ev"], n)
                    for p, j in pairs:
                        last = mm(to_bank(c, 0, D, j, p, T), a(c, LT_[j] + p * T, T), a(c, Y_ + p * D, D))
                    last.then_inc(sem["z_mm"], 1)
                elif name == "w":
                    pe.wait_ge(sem["z_ev"], n)
                    for p, j in pairs:
                        last = mm(to_bank(c, 1, D, j, p, T), a(c, TB_[j] + p * T, T), a(c, U_ + p * D, D))
                    last.then_inc(sem["w_mm"], 1)
                elif name == "o":
                    pe.wait_ge(sem["sab"], n)
                    pe.wait_ge(sem["sa"], 2 * n)
                    for p in range(PP):
                        for u in range(2):
                            for j in range(2):
                                last = mm(bank(c, 0, T, p * T, 64 * j, 64 * j + 64),
                                          a(c, (SA_, VT_)[u][j] + p * D, D), m4(c, p, (3, 1)[u]), start=(u == 0),
                                          stop=(u == 1))
                    last.then_inc(sem["o_mm"], 1)
                elif name == "ro":
                    pe.wait_ge(sem["gn_g"], n)
                    mm(bank(c, 0), k("Wo"), a(c, slot(10))).then_inc(sem["ro_mm"], 1)
                elif name == "f":
                    if c == 0:
                        pe.wait_ge(sem["cst4"], 16)
                        pe.wait_ge(sem["r_oh"], 1)
                        pe.wait_ge(sem["rb_split"], 1)
                        pe.wait_ge(sem["wsI"], NL)
                    pe.wait_ge(sem["ln_out"], COUNT["var", 5, c])
                    for j in range(2):
                        last = mm(bank(c, j), k("Wi", 0, 128, 64 * j, 64 * j + 64), half(c, N_, j, 0, W, 64))
                    last.then_inc(sem["f_mm"], 1)
                elif name == "r":
                    if i == 0:
                        pe.wait_ge(sem["f_relu"], c + 1)
                    else:
                        pe.wait_ge(sem["r_relu"], COUNT["r", 0, c])
                    pe.wait_ge(sem[f"wg{i}_{c}"], 16 * 2 * PP)
                    src = slot(2 if i == 0 else 4)
                    for j in range(2):
                        mm(pair(bank(c, j)), rb_split[:, 1, 128 * i:128 * i + 128],
                           oneh[:, 32 * j + PP * c:32 * j + PP * c + PP].unsqueeze(2).broadcast_to([3 * (NR + 1), PP, T]),
                           stop=False)
                        for p in range(PP):
                            b = PP * j + p
                            w = WG0[:, 2 * PP * c + b, :] if i == 0 else a(c, WG1_ + 128 * b, 128)
                            mm(bank(c, j, T, p * T), w, a(c, src + j * W + p * T, T), start=False, stop=False)
                        last = mm(bank(c, j), k("Ws", 128 * i, 128 * i + 128), a(c, src + j * W), start=False)
                    last.then_inc(sem["r_mm"], 1)
                elif name == "fo":
                    pe.wait_ge(sem["r_relu"], COUNT["r", 1, c])
                    for j in range(2):
                        last = mm(bank(c, 0, W, 0, 64 * j, 64 * j + 64), k("WoT"), a(c, slot(2 + j)))
                    last.then_inc(sem["fo_mm"], 1)


def shape_constants():
    z = {}
    pos = np.arange(T, dtype=np.float32)
    inv = (1.0 / 10000.0 ** (np.arange(0, HD, 2, dtype=np.float32) / HD)).astype(np.float32)
    fr = np.outer(pos, inv).astype(np.float32)
    emb = np.concatenate([fr, fr], -1)
    cos = np.tile(np.cos(emb).T, (2 * NH, 1)).astype(np.float32)
    sin = np.tile(np.sin(emb).T, (2 * NH, 1)).astype(np.float32)
    sign = np.tile(np.where(np.arange(HD) < HD // 2, -1.0, 1.0), 2 * NH)[:, None].astype(np.float32)
    sc = np.float32(1.0 / np.sqrt(HD))
    z["cosq"], z["sinq"], z["cosk"], z["sink"] = cos * sc, sin * sign * sc, cos, sin * sign
    q = np.arange(128)
    z["headmask"] = ((q % 64) // HD)[:, None] == np.arange(NH)[None, :]
    z["identf"] = np.eye(128)
    r = (q % 64)[:, None]
    t = np.arange(T)[None, :]
    z["identd"] = r == t
    z["mean"] = ((q[:, None] // 64) == (q[None, :] // 64)) / float(D)
    z["tri"] = np.tile((np.arange(E)[None, :] < np.arange(E)[:, None]).reshape(1, -1), (128, 1))
    z["reset"] = np.tile((np.arange(W) % T != 0)[None, :], (128, 1))
    z["mask4"] = np.concatenate([r < t, r <= t, r < t, -1.0 * (r <= t)], 1)
    z["maskL"] = (r > t) & (r < T)
    z["negm1"] = -1.0 * ((r // 2 == t // 2) & (r > t))
    z["negm1T"] = -1.0 * ((r // 2 == t // 2) & (r < t))
    z["eye2"] = np.concatenate([r == t, r == t], 1)
    z["levels"] = np.concatenate([(r // (2 * b) == t // (2 * b)) & (r // b > t // b) & (r < T) & (q[:, None] // 64 == j)
                                  for b in LEVELS for j in range(2)], 1)
    z["row32"] = r >= 32
    out = {n: np.asarray(x, np.float32) for n, x in z.items()}
    causal = np.where((r < T) & (t > r), NEG, 0.0)
    sel = np.zeros((128, E, 128))
    for e in range(E):
        for j in range(2):
            for part in range(3):
                sel[64 * j + E * part + e, e, 64 * j:64 * j + 64] = 1
    return out, np.concatenate([np.eye(128), causal, sel.reshape(128, -1)], 1)


def kernel(**inputs):
    import ml_dtypes
    import concourse.bacc as _bacc
    from concourse import mybir as _mybir
    from concourse.bass_utils import run_bass_kernel_spmd as _run

    inp = {n: np.asarray(x) for n, x in inputs.items()}
    cst, bf = shape_constants()

    def bd(m):
        o = np.zeros((128, 2 * m.shape[1]), np.float32)
        o[:64, :m.shape[1]] = m
        o[64:, m.shape[1]:] = m
        return o

    def dup(m):
        return np.concatenate([m, m], 0)

    wt = inp["L0_tok_W"]
    rot = np.concatenate([(np.arange(HD) + HD // 2) % HD + h * HD for h in range(NH)])
    kvrow = np.concatenate([np.arange(HD) + (h // (NH // NKV)) * HD for h in range(NH)])
    wq, wk = inp["L0_attn_Wq"], inp["L0_attn_Wk"][kvrow]
    cst.update(
        tokA=wt[:, :128].T, tokB=wt[:, 128:].T, wq=bd(wq.T), wqr=bd(wq[rot].T), wk=bd(wk.T), wkr=bd(wk[rot].T),
        wv=dup(inp["L0_attn_Wv"].T), wo=bd(inp["L0_attn_Wo"].T), gw=dup(inp["L0_ffn_gate_w"]),
        gb=np.tile(inp["L0_ffn_gate_b"][None], (128, 1)), b1=inp["L0_ffn_b1"].T,
        w1=dup(inp["L0_ffn_W1"].transpose(1, 0, 2).reshape(D, -1)),
        w2=inp["L0_ffn_W2"].transpose(1, 0, 2).reshape(HID, -1),
        Wr=bd(inp["L1_attn_W_r"]), Wk=bd(inp["L1_attn_W_k"]), Wvf=bd(inp["L1_attn_W_v"]), Wvt=dup(inp["L1_attn_W_v"]),
        Aw=bd(inp["L1_attn_A_w"]), Bw=bd(inp["L1_attn_B_w"]), Aa=bd(inp["L1_attn_A_a"]), Ba=bd(inp["L1_attn_B_a"]),
        Ag=dup(inp["L1_attn_A_g"]), Bg=inp["L1_attn_B_g"], Wo=bd(inp["L1_attn_W_o"]),
        Wi=dup(inp["L1_ffn_Wi"].T), Ws=inp["L1_ffn_Ws"][:, 0].transpose(2, 0, 1).reshape(128, -1),
        WoT=inp["L1_ffn_Wo"].T)
    b2 = np.zeros((128, 128), np.float32)
    b2[0:E, 0:64] = inp["L0_ffn_b2"]
    b2[64:64 + E, 64:128] = inp["L0_ffn_b2"]
    rb = np.zeros((128, NL * 128), np.float32)
    for part in range(3):
        at = part * (NR + 1)
        rb[at:at + NR] = inp["L1_ffn_br"].transpose(1, 0, 2).reshape(NR, -1)
        rb[at + NR] = inp["L1_ffn_bs"][:, 0].reshape(-1)
    cst["b2"], cst["Rb"] = b2, rb
    vecs = np.zeros((128, 36), np.float32)
    cols = dict(tok_b=inp["L0_tok_b"], gamma=inp["L0_tok_gamma"], beta=inp["L0_tok_beta"], b_w=inp["L1_attn_b_w"],
                b_a=inp["L1_attn_b_a"], k_k=inp["L1_attn_k_k"], k_a=inp["L1_attn_k_a"], r_k=inp["L1_attn_r_k"],
                gn_w=inp["L1_attn_gn_w"], gn_b=inp["L1_attn_gn_b"], bo=inp["L1_ffn_bo"])
    for i in range(6):
        cols[f"mix{i}"] = inp["L1_attn_x_mix"][i]
    for n, x in cols.items():
        vecs[:, VECS.index(n)] = np.concatenate([x, x])
    vecs[:, VECS.index("bi")] = inp["L1_ffn_bi"]
    vecs[:, VECS.index("eps_ln")] = 1e-5
    vecs[:, VECS.index("eps_gn")] = D * 1e-5
    vecs[:, VECS.index("ten_ln2")] = 10.0 * np.log(2.0)
    row = np.arange(128)
    vecs[:, VECS.index("eidx")] = row % (NR + 1)
    vecs[:, VECS.index("shared")] = row % (NR + 1) == NR
    vecs[:, VECS.index("cw_mid")] = -1.0 * (row % 64 // E >= 1)
    vecs[:, VECS.index("cw_low")] = -1.0 * (row % 64 // E >= 2)
    vecs[:, VECS.index("rb_mid")] = -1.0 * (row // (NR + 1) >= 1)
    vecs[:, VECS.index("rb_low")] = -1.0 * (row // (NR + 1) >= 2)
    for j in range(2):
        for n, rows in (("feat", D), ("tok", T), ("early", 32)):
            vecs[64 * j:64 * j + rows, VECS.index(f"{n}{j}")] = 1
    cst["vecs"] = vecs
    packed = np.zeros((128, N_CONST), np.float32)
    for n, (o, w) in COL.items():
        packed[:cst[n].shape[0], o:o + w] = cst[n]
    x = inp["x"][:, :CH * STRIDE].reshape(2, C, PP, CH, STRIDE * F_IN)
    xT = np.ascontiguousarray(x.transpose(4, 1, 0, 2, 3).reshape(128, C, 2 * PP * CH))
    wr = np.zeros((128, NL, NR + 1, 128), np.float32)
    wr[:, :, :NR] = inp["L1_ffn_Wr"].transpose(3, 0, 1, 2)
    arrays = {
        "xT": xT, "consts": packed, "masks_bf": np.ascontiguousarray(bf.astype(ml_dtypes.bfloat16)),
        "route": np.ascontiguousarray(inp["L1_ffn_route_id"].reshape(1, B)), "wr": wr.reshape(128, -1),
    }
    nc = _bacc.Bacc("TRN2", target_bir_lowering=False, num_devices=1)
    args = [nc.dram_tensor(n, v.shape, _mybir.dt.from_np(v.dtype), kind="ExternalInput").ap() for n, v in arrays.items()]
    args.append(nc.dram_tensor("out", (128, C * W), _mybir.dt.float32, kind="ExternalOutput").ap())
    audio_tower(nc, *args)
    r = _run(nc, [arrays], core_ids=[0])
    o = r.results[0]["out"]
    return np.ascontiguousarray(o.reshape(2, D, B // 2, T).transpose(0, 2, 3, 1).reshape(B, T, D))
```

```python
import numpy as np
import concourse.bass as bass
from concourse import mybir
from contextlib import ExitStack

B, S_IN, F_IN = 64, 375, 16
PATCH, STRIDE, D = 16, 8, 64
T = (S_IN - PATCH) // STRIDE + 1
NH, NKV, HD = 8, 4, 8
E, HID = 8, 128
NR = 16
NL = 2
C = 4
PP = B // 2 // C
W = PP * T
LEVELS = (2, 4, 8, 16)
DECAY = -0.6065306597126334
SS_SCALE = 2.0 ** 20
NEG = -1.0e30

GROUPS = [
    [("tokA", 64), ("tokB", 64), ("mean", 128), ("vecs", 36)],
    [("wq", 128), ("wqr", 128), ("wk", 128), ("wkr", 128), ("wv", 2 * NKV * HD), ("cosq", T), ("sinq", T),
     ("cosk", T), ("sink", T), ("headmask", NH), ("identf", 128), ("wo", 128)],
    [("gw", 2 * E), ("gb", E), ("desc", E), ("b1", E), ("w1", E * HID), ("w2", E * D), ("b2", 128)],
    [("Wr", 128), ("Wk", 128), ("Wvf", 128), ("Aw", 128), ("Bw", 128), ("Aa", 128), ("Ba", 128),
     ("Ag", 128), ("Bg", 64), ("Wo", 128), ("reset", W), ("mask4", 4 * T), ("maskL", T), ("negm1", T),
     ("negm1T", T), ("eye2", 2 * T), ("levels", len(LEVELS) * 2 * T), ("row32", 1)],
    [("Wi", 128), ("Ws", NL * 128), ("WoT", 64), ("Rb", NL * 128)],
]
COL, GROUP_OF, N_CONST = {}, {}, 0
GROUP_RANGE = []
for _g, _names in enumerate(GROUPS):
    _start = N_CONST
    for _n, _w in _names:
        COL[_n] = (N_CONST, _w)
        GROUP_OF[_n] = _g
        N_CONST += _w
    GROUP_RANGE.append((_start, N_CONST))
VECS = ["tok_b", "gamma", "beta", "b_w", "b_a", "k_k", "k_a", "r_k", "gn_w", "gn_b", "bi", "bo",
        "eps_ln", "eps_gn", "zero", "ten_ln2", "mix0", "mix1", "mix2", "mix3", "mix4", "mix5", "eidx", "shared",
        "cw_mid", "cw_low", "rb_mid", "rb_low", "feat0", "feat1", "tok0", "tok1", "tok", "early0", "early1"]

H_, N_ = 0, W
def slot(i):
    return i * W
QBD_, KX_, VD_ = 5 * W, 8 * W, 16 * W
PB_ = VD_ + PP * 2 * NKV * 18
PT_ = PB_ + 512
XT_ = PT_ + 512
CH = T + 1
M4_, L_, TT_, U_, Y_ = slot(11), slot(9), slot(3), slot(19), slot(3)
KR_, X_, VT_, LT_, TB_, SA_ = ((slot(1), slot(17)), (slot(5), slot(7)), (slot(1), slot(17)), (slot(10), slot(15)),
                               (slot(5), slot(7)), (slot(5), slot(19)))
WG1_ = slot(19) + PP * D
ARENA = WG1_ + 2 * PP * 128
CW_ = slot(13) + 160

SEMS = """rb_steps r_steps g_steps cst0 cst1 cst2 cst3 cst4 cst_bf ids psum0 init oneka rb_split
r_id r_oh wsI
tok_mm tok_y h0 ln_mean ln_xc ln_sq ln_var ln_log ln_rs ln_out
q_mm q_mul q_sum q_bd k_mm k_mul k_sum kx v_mm vd s_mm s_max s_sub s_exp pt_mm pt_ev pv_mm o_rec att
attT_mm attT wo_mm h1
gate_mm g_sub g_exp cw cwT_mm c_hi c_r c_mid cwT b2_mm b2_add
hid_mm gelu y_mm cwb y_mul acc
delta xi xa xi_late rk_mm rk vw_mm vw aw_mm aw_aa aw_sg ab_mm ab g_hid g_sig gg_mm gg cs ep em kk0 kk_sq kk_mm kk_cl kk_ln kk_rs
kk bt0 bt tk kp kt kr1 krr krb bon0 bon_mm bon vt_mm vt vd_hi
m_mm m_ev lv1 tt1 ltb ttb lt32 sab x_mm x_ev t_mm t_ev u_mm u_ev y_mm2 y_ev z_mm z_ev w_mm sa o_mm o_ev
gn_a bonb gn_g ro_mm h3 f_mm f_relu r_mm r_relu fo_mm fo out_done""".split()
LNS = ["lt", "l1", "l2", "l3", "gn", "l4"]
SEMS += [f"x{c}" for c in range(C)] + [f"wg{l}_{c}" for l in range(NL) for c in range(C)]

LAG = 2


def schedule():
    order = []

    def stage(*steps):
        for name, i in steps:
            order.extend((name, i, c) for c in range(C))

    def norm(k):
        stage(("mean", k), ("var", k))

    stage(("tok", 0))
    norm(0)
    norm(1)
    stage(("q", 0), ("k", 0), ("v", 0), ("s", 0), ("e", 0))
    units = [(i, c) for i in range(PP) for c in range(C)]
    for n in range(len(units) + LAG):
        if n < len(units):
            i, c = units[n]
            order.append(("t", i, c))
            if i < PP - 1:
                order.append(("s", i + 1, c))
        if n >= LAG:
            i, c = units[n - LAG]
            order.append(("pv", i, c))
        if 1 <= n <= len(units):
            i, c = units[n - 1]
            if i < PP - 1:
                order.append(("e", i + 1, c))
    stage(("attT", 0), ("wo", 0))
    norm(2)
    stage(("gate", 0))
    order.append(("top2", 0, 0))
    stage(("hid", 0), ("cwT", 0), ("cw2", 0), ("b2", 0), ("y", 0))
    for i in range(1, E):
        stage(("hid", i), ("y", i))
    norm(3)
    for c in range(C + 1):
        if c < C:
            order += [("mixes", 0, c), ("rk", 0, c)]
        if c:
            order.append(("vw", 0, c - 1))
    stage(("aw", 0), ("ab", 0), ("gh", 0), ("gg", 0), ("kk", 0), ("bon", 0), ("kb", 0), ("m", 0), ("m", 1),
          ("vt", 0))
    for i in range(len(LEVELS)):
        stage(("lx", i), ("lt", i))
    stage(("u", 0), ("y2", 0), ("z", 0), ("w", 0), ("o", 0))
    norm(4)
    stage(("ro", 0))
    norm(5)
    stage(("f", 0), ("r", 0), ("r", 1), ("fo", 0))
    return order


ORDER = schedule()
COUNT = {}
for _name, _i, _c in ORDER:
    COUNT[_name, _i, _c] = 1 + sum(1 for key in COUNT if key[0] == _name)


def audio_tower(nc, xT, consts, masks_bf, route, wr, out):
    fp32, bf16, i32 = mybir.dt.float32, mybir.dt.bfloat16, mybir.dt.int32
    ALU, ACT, AX = mybir.AluOpType, mybir.ActivationFunctionType, mybir.AxisListType
    ctx = ExitStack()
    with ctx:
        def sb(name, shape, dt):
            return ctx.enter_context(nc.sbuf_tensor(name, shape, dt))

        sem = {n: ctx.enter_context(nc.semaphore(n)) for n in SEMS}
        K = sb("K", [128, N_CONST], fp32)
        KB = sb("KB", [128, 128 + T + E * 128], bf16)
        arena = sb("arena", [128, C, ARENA], fp32)
        WG0 = sb("WG0", [128, B, 128], fp32)
        rid = sb("rid", [1, B], i32)
        ride = sb("ride", [1, B], i32)
        ridb = sb("ridb", [3 * (NR + 1), B], i32)
        oneh = sb("oneh", [3 * (NR + 1), B], bf16)
        rb_split = sb("rb_split", [3 * (NR + 1), 2, NL * 128], bf16)
        smax = sb("smax", [128, C, NH], fp32)
        orec = sb("orec", [128, C, NH], fp32)
        oneka = sb("oneka", [128, 1], fp32)
        PS = ctx.enter_context(nc.psum_tensor("PS", [128, 2 * C, 512], fp32))

        def k(name, lo=0, hi=None, p0=0, p1=128):
            o, w = COL[name]
            return K[p0:p1, o + lo:o + (w if hi is None else hi)]

        def vec(name):
            o = COL["vecs"][0] + VECS.index(name)
            return K[:, o:o + 1]

        def a(c, off, n=W, p0=0, p1=128):
            return arena[p0:p1, c, off:off + n]

        def pair(ap, t=T):
            return ap.rearrange("q (p t) -> q p t", t=t)

        def bank(c, b, n=W, lo=0, p0=0, p1=128):
            return PS[p0:p1, 2 * c + b, lo:lo + n]

        def both(c, n=W):
            return PS[:, 2 * c:2 * c + 2, 0:n]

        def over_pairs(ap, n=PP):
            return ap.unsqueeze(1).broadcast_to([ap.shape[0], n, ap.shape[1]])

        def half(c, off, j, lo, n, rows=T):
            return arena[64 * j:64 * j + rows, c, off + lo:off + lo + n]

        def halves(ap):
            return ap.rearrange("q (b w) -> q b w", b=2)

        def to_bank(c, b, n, j, i, rows):
            return PS[64 * j:64 * j + rows, 2 * c + b, n * i:n * i + n]

        def m2(c):
            return a(c, M4_, 4 * W).rearrange("q (p u t) -> q p u t", u=4, t=T)[:, :, 2, :]

        def values_of(c, hh):
            vd = a(c, VD_, PP * 2 * NKV * 18, 64 * hh, 64 * hh + 64)
            to = vd.rearrange("q (p j g u) -> q p j g u", j=2, g=NKV, u=18)[:, :, :, :, 9 * hh:9 * hh + HD]
            ones = vd.rearrange("q (r u) -> q r u", u=18)[:, :, 9 * hh + HD]
            return to, ones, [bank(c, j, PP * NKV * HD, 0, 64 * hh, 64 * hh + 64).rearrange(
                "q (p g d) -> q p g d", g=NKV, d=HD) for j in range(2)]

        def gate(r, n=C * PP * E):
            return a(0, slot(14) + C * PP * E * r, n)

        def part_bf(c, i):
            return a(c, slot(i), W // 2).bitcast(bf16)

        rtmp = a(0, ARENA - 4 * B, 4 * B, 0, 1).rearrange("q (r b) -> q r b", b=B)
        identb, maskb, selb = KB[:, 0:128], KB[:, 128:128 + T], KB[:, 128 + T:]
        LN_EXP = "natural_log_exp_and_others"
        NORM_SLOTS = {p: (slot(2), slot(3)) for p in LNS}
        NORM_SLOTS["gn"] = (slot(10), slot(17))
        block = ctx.enter_context(nc.Block())

        @block.sync
        def _(sp):
            def load_consts(g):
                lo, hi = GROUP_RANGE[g]
                sp.dma_start(K[:, lo:hi], consts[:, lo:hi]).then_inc(sem[f"cst{g}"], 16)

            load_consts(0)
            for c in range(C):
                sp.dma_start(a(c, XT_, 2 * PP * CH), xT[:, c, :]).then_inc(sem[f"x{c}"], 16)
                if c == 0:
                    load_consts(1)
                    sp.dma_start(KB[:], masks_bf).then_inc(sem["cst_bf"], 16)
            sp.dma_start(rid[:], route[0:1, :]).then_inc(sem["ids"], 16)
            sp.dma_start(ridb[:], route[0:1, :].broadcast_to([3 * (NR + 1), B])).then_inc(sem["ids"], 16)
            for g in (2, 3, 4):
                load_consts(g)
            sp.wait_ge(sem["r_id"], 1)
            for l in range(NL):
                for c in range(C):
                    if l == 1:
                        sp.wait_ge(sem["h1"], c + 1)
                    for j in range(2):
                        for i in range(PP):
                            b = 32 * j + PP * c + i
                            e = sp.value_load(ride[0:1, b:b + 1], min_val=0, max_val=NR)
                            n = PP * j + i
                            dst = WG0[:, 2 * PP * c + n, :] if l == 0 else a(c, WG1_ + 128 * n, 128)
                            sp.dma_start(dst, wr[:, bass.ds(e * 128 + l * (NR + 1) * 128, 128)]).then_inc(
                                sem[f"wg{l}_{c}"], 16)
            for c in range(C):
                sp.wait_ge(sem["fo"], c + 1)
                sp.dma_start(out[:, c * W:(c + 1) * W], a(c, slot(6))).then_inc(sem["out_done"], 16)
            sp.wait_ge(sem["out_done"], 16 * C)

        @block.gpsimd
        def _(pool):
            g = nc.gpsimd
            for c in range(C):
                g.memset(a(c, QBD_, 3 * W), 0.0)
                g.memset(a(c, PB_, 512), 1.0)
                g.memset(a(c, VD_, PP * 2 * NKV * 18), 0.0).then_inc(sem["init"], 1)
            pool.wait_ge(sem["cst4"], 16)
            pool.wait_ge(sem["cst1"], 16)
            for l in range(NL):
                ws = k("Ws", 128 * l, 128 * l + 128)
                g.tensor_tensor(ws, ws, k("identf"), ALU.add).then_inc(sem["wsI"], 1)
            for name, i, c in ORDER:
                n = COUNT[name, i, c]
                if name == "q":
                    pool.wait_ge(sem["q_mul"], n)
                    g.tensor_tensor(a(c, slot(2)), a(c, slot(2)), a(c, slot(3)), ALU.add).then_inc(sem["q_sum"], 1)
                elif name == "k":
                    pool.wait_ge(sem["k_mul"], n)
                    g.tensor_tensor(a(c, slot(4)), a(c, slot(4)), a(c, PT_), ALU.add).then_inc(sem["k_sum"], 1)
                elif name == "s":
                    pool.wait_ge(sem["k_sum"], COUNT["k", 0, c])
                    g.tensor_tensor(a(c, KX_ + i * W).rearrange("q (h t) -> q h t", t=T),
                                    a(c, slot(4) + i * T, T).unsqueeze(1).broadcast_to([128, NH, T]),
                                    k("headmask").unsqueeze(2).broadcast_to([128, NH, T]), ALU.mult).then_inc(sem["kx"], 1)
                elif name == "y":
                    pool.wait_ge(sem["y_mul"], n)
                    if i:
                        pool.wait_ge(sem["acc"], COUNT["y", i - 1, c])
                    g.tensor_tensor(a(c, H_), a(c, H_), a(c, slot(3 + i % 2)), ALU.add).then_inc(sem["acc"], 1)
                elif name == "mixes":
                    pool.wait_ge(sem["xa"], n)
                    for u in (4, 5):
                        last = g.tensor_tensor(a(c, slot(3 + u)), a(c, slot(3 + u)), a(c, N_), ALU.add)
                    last.then_inc(sem["xi_late"], 1)
                elif name == "kb":
                    pool.wait_ge(sem["kk"], n)
                    g.tensor_tensor(a(c, slot(5)), a(c, slot(3)), a(c, slot(15)), ALU.mult).then_inc(sem["bt0"], 1)
                    pool.wait_ge(sem["bt0"], n)
                    g.tensor_tensor(a(c, slot(5)), a(c, slot(5)), a(c, slot(14)), ALU.mult).then_inc(sem["bt"], 1)
                    pool.wait_ge(sem["em"], n)
                    g.tensor_tensor(a(c, slot(12)), a(c, slot(9)), a(c, slot(13)), ALU.mult).then_inc(sem["krr"], 1)
                elif name == "m":
                    pool.wait_ge(sem["m_ev"], n)
                    p0, p1 = i * PP // 2, (i + 1) * PP // 2
                    tt = a(c, TT_, 2 * W).rearrange("q (p u t) -> q p u t", u=2, t=T)[:, p0:p1]
                    m4 = a(c, M4_, 4 * W).rearrange("q (p u t) -> q p u t", u=4, t=T)[:, p0:p1]
                    g.tensor_tensor(tt[:, :, 0, :], pair(a(c, L_))[:, p0:p1], over_pairs(k("negm1"), PP // 2), ALU.mult)
                    g.tensor_tensor(tt[:, :, 1, :], m4[:, :, 2, :], over_pairs(k("negm1T"), PP // 2),
                                    ALU.mult).then_inc(sem["lv1"], 1)
                    pool.wait_ge(sem["lv1"], n)
                    tt2 = a(c, TT_ + 2 * p0 * T, W).rearrange("q (p t) -> q p t", t=2 * T)
                    g.tensor_tensor(tt2, tt2, over_pairs(k("eye2"), PP // 2), ALU.add).then_inc(sem["tt1"], 1)
                elif name == "var" and LNS[i] == "gn":
                    pool.wait_ge(sem["gn_a"], c + 1)
                    g.tensor_tensor(a(c, slot(10)), a(c, slot(10)), a(c, slot(16)), ALU.mult).then_inc(sem["gn_g"], 1)

        @block.scalar
        def _(act):
            s = nc.scalar
            loaded = [None]

            def tables(name):
                if loaded[0] != name:
                    s.preload_act_table_set(name)
                    loaded[0] = name

            tables(LN_EXP)
            act.wait_ge(sem["cst0"], 16)
            for name, i, c in ORDER:
                n = COUNT[name, i, c]
                if name == "tok":
                    act.wait_ge(sem["tok_mm"], n)
                    s.activation(a(c, H_), bank(c, 0), ACT.Identity, bias=vec("tok_b")).then_inc(sem["tok_y"], 1)
                elif name == "mean":
                    xc, sq = NORM_SLOTS[LNS[i]]
                    act.wait_ge(sem["ln_xc"], n)
                    s.activation(a(c, sq), a(c, xc), ACT.Square).then_inc(sem["ln_sq"], 1)
                elif name == "var":
                    sq = NORM_SLOTS[LNS[i]][1]
                    tables(LN_EXP)
                    act.wait_ge(sem["ln_var"], n)
                    s.activation(a(c, sq), bank(c, 1), ACT.Ln,
                                 bias=vec("eps_gn" if LNS[i] == "gn" else "eps_ln")).then_inc(sem["ln_log"], 1)
                    act.wait_ge(sem["ln_log"], n)
                    s.activation(a(c, sq), a(c, sq), ACT.Exp, scale=-0.5).then_inc(sem["ln_rs"], 1)
                elif name == "q":
                    if c == 0:
                        act.wait_ge(sem["init"], C)
                    act.wait_ge(sem["q_sum"], n)
                    for j in range(2):
                        r0, r1 = 64 * j, 64 * j + 64
                        qb = a(c, QBD_, PP * 128, r0, r1).rearrange("q (p t) -> q p t", t=128)
                        last = s.copy(qb[:, :, 64 * j:64 * j + T], pair(a(c, slot(2), W, r0, r1)))
                    last.then_inc(sem["q_bd"], 1)
                elif name == "v":
                    act.wait_ge(sem["v_mm"], n)
                    to, ones, source = values_of(c, 1)
                    s.copy(ones, vec("tok")[64:128, :].broadcast_to([64, PP * 2 * NKV]))
                    for j in range(2):
                        last = s.activation(to[:, :, j], source[j], ACT.Copy, scale=vec("tok")[64:128, :])
                    last.then_inc(sem["vd_hi"], 1)
                elif name == "e":
                    pb = a(c, PB_, 512).rearrange("q (h t) -> q h t", t=64)[:, :, 0:T]
                    tables(LN_EXP)
                    act.wait_ge(sem["s_sub"], COUNT["s", i, c])
                    s.activation(pb, pb, ACT.Exp).then_inc(sem["s_exp"], 1)
                elif name == "t":
                    act.wait_ge(sem["pt_mm"], n)
                    s.copy(a(c, PT_, 512).rearrange("q (r t) -> q r t", t=64)[:, :, 0:T],
                           bank(c, 1, 512).rearrange("q (r t) -> q r t", t=64)[:, :, 0:T]).then_inc(sem["pt_ev"], 1)
                elif name == "attT":
                    act.wait_ge(sem["attT_mm"], n)
                    s.copy(a(c, slot(4)), bank(c, 0)).then_inc(sem["attT"], 1)
                elif name == "top2":
                    tables(LN_EXP)
                    act.wait_ge(sem["g_sub"], n)
                    s.activation(gate(0), gate(0), ACT.Exp).then_inc(sem["g_exp"], 1)
                elif name == "cwT":
                    act.wait_ge(sem["cwT_mm"], n)
                    s.copy(part_bf(c, 10), bank(c, 1)).then_inc(sem["c_hi"], 1)
                elif name == "cw2":
                    act.wait_ge(sem["c_r"], n)
                    s.copy(part_bf(c, 11), a(c, slot(5))).then_inc(sem["c_mid"], 1)
                elif name == "hid":
                    tables("gelu_and_others")
                    act.wait_ge(sem["hid_mm"], n)
                    s.activation(halves(a(c, slot(6), 2 * W)), both(c), ACT.Gelu,
                                 bias=k("b1", i, i + 1)).then_inc(sem["gelu"], 1)
                elif name == "y":
                    act.wait_ge(sem["y_mm"], n)
                    s.copy(a(c, slot(8)), bank(c, 1)).then_inc(sem["cwb"], 1)
                elif name == "mixes":
                    act.wait_ge(sem["delta"], n)
                    for u in (4, 5):
                        last = s.activation(a(c, slot(3 + u)), a(c, slot(2)), ACT.Copy, scale=vec(f"mix{u}"))
                    last.then_inc(sem["xa"], 1)
                elif name == "rk":
                    act.wait_ge(sem["rk_mm"], n)
                    s.copy(halves(a(c, slot(9), 2 * W)), both(c)).then_inc(sem["rk"], 1)
                elif name == "vw":
                    tables("sigmoid_and_others")
                    act.wait_ge(sem["vw_mm"], n)
                    s.copy(a(c, slot(11)), bank(c, 0))
                    s.activation(a(c, slot(12)), bank(c, 1), ACT.Tanh).then_inc(sem["vw"], 1)
                    act.wait_ge(sem["kk0"], n)
                    s.activation(a(c, slot(4)), a(c, slot(3)), ACT.Square).then_inc(sem["kk_sq"], 1)
                elif name == "aw":
                    tables("sigmoid_and_others")
                    act.wait_ge(sem["aw_mm"], n)
                    s.activation(a(c, slot(14)), bank(c, 1), ACT.Sigmoid, bias=vec("b_w")).then_inc(sem["aw_sg"], 1)
                elif name == "ab":
                    tables("sigmoid_and_others")
                    act.wait_ge(sem["ab_mm"], n)
                    s.activation(a(c, slot(15)), bank(c, 0), ACT.Sigmoid, bias=vec("b_a")).then_inc(sem["ab"], 1)
                elif name == "gh":
                    tables("sigmoid_and_others")
                    act.wait_ge(sem["g_hid"], n)
                    s.activation(halves(a(c, slot(16), 2 * W)), both(c), ACT.Sigmoid).then_inc(sem["g_sig"], 1)
                elif name == "gg":
                    act.wait_ge(sem["gg_mm"], n)
                    s.copy(a(c, slot(16)), bank(c, 0)).then_inc(sem["gg"], 1)
                elif name == "kk":
                    tables(LN_EXP)
                    act.wait_ge(sem["cs"], n)
                    s.activation(a(c, slot(13)), a(c, slot(12)), ACT.Exp, scale=DECAY).then_inc(sem["ep"], 1)
                    act.wait_ge(sem["kp"], n)
                    s.activation(a(c, slot(14)), a(c, slot(12)), ACT.Exp, scale=-DECAY).then_inc(sem["em"], 1)
                    act.wait_ge(sem["kk_cl"], n)
                    s.activation(a(c, slot(4)), a(c, slot(4)), ACT.Ln, scale=SS_SCALE).then_inc(sem["kk_ln"], 1)
                    act.wait_ge(sem["kk_ln"], n)
                    s.activation(a(c, slot(4)), a(c, slot(4)), ACT.Exp, scale=-0.5,
                                 bias=vec("ten_ln2")).then_inc(sem["kk_rs"], 1)
                elif name == "kb":
                    act.wait_ge(sem["krr"], n)
                    for j in range(2):
                        kr = a(c, KR_[j], 2 * W).rearrange("q (p u t) -> q p u t", u=2, t=T)
                        last = s.activation(kr[:, :, 1, :], pair(a(c, slot(12))), ACT.Copy, scale=vec(f"feat{j}"))
                    last.then_inc(sem["krb"], 1)
                elif name == "m":
                    act.wait_ge(sem["m_ev"], n)
                    p0, p1 = i * PP // 2, (i + 1) * PP // 2
                    for j in range(2):
                        last = s.activation(pair(a(c, LT_[j]))[:, p0:p1], m2(c)[:, p0:p1], ACT.Copy, scale=vec(f"tok{j}"))
                    last.then_inc(sem["ltb"], 1)
                elif name == "vt":
                    act.wait_ge(sem["vt_mm"], n)
                    for j in range(2):
                        last = s.activation(a(c, VT_[j], 512), bank(c, 0, 512), ACT.Copy, scale=vec(f"tok{j}"))
                    last.then_inc(sem["vt"], 1)
                    act.wait_ge(sem["bon"], n)
                    s.activation(a(c, slot(8)), a(c, slot(8)), ACT.Identity, bias=vec("gn_b")).then_inc(sem["bonb"], 1)
                elif name == "lt" and i == len(LEVELS) - 1:
                    act.wait_ge(sem["t_ev"], n)
                    for j in range(2):
                        last = s.activation(pair(a(c, TB_[j])), a(c, TT_, 2 * W).rearrange(
                            "q (p u t) -> q p u t", u=2, t=T)[:, :, 1, :], ACT.Copy, scale=vec(f"tok{j}"))
                    last.then_inc(sem["ttb"], 1)
                    for j in range(2):
                        last = s.activation(pair(a(c, LT_[j])), m2(c), ACT.Copy, scale=vec(f"early{j}"))
                    last.then_inc(sem["lt32"], 1)
                elif name == "u":
                    act.wait_ge(sem["u_mm"], n)
                    s.copy(a(c, U_, 512), bank(c, 0, 512)).then_inc(sem["u_ev"], 1)
                elif name == "y2":
                    act.wait_ge(sem["ttb"], n)
                    act.wait_ge(sem["y_mm2"], n)
                    s.copy(a(c, Y_, 512), bank(c, 1, 512)).then_inc(sem["y_ev"], 1)
                elif name == "z":
                    act.wait_ge(sem["z_mm"], n)
                    s.activation(a(c, U_, 512), bank(c, 0, 512), ACT.Copy, scale=k("row32")).then_inc(sem["z_ev"], 1)
                elif name == "w":
                    act.wait_ge(sem["sa"], 2 * n - 1)
                    s.activation(a(c, SA_[0], 512), a(c, Y_, 512), ACT.Copy, scale=vec("tok0")).then_inc(sem["sab"], 1)
                elif name == "o":
                    act.wait_ge(sem["o_mm"], n)
                    s.copy(a(c, slot(9)), bank(c, 0)).then_inc(sem["o_ev"], 1)
                elif name == "f":
                    act.wait_ge(sem["f_mm"], n)
                    s.activation(halves(a(c, slot(2), 2 * W)), both(c), ACT.Relu, bias=vec("bi")).then_inc(sem["f_relu"], 1)
                elif name == "r":
                    act.wait_ge(sem["r_mm"], n)
                    s.activation(halves(a(c, slot(4 if i == 0 else 2), 2 * W)), both(c), ACT.Relu).then_inc(
                        sem["r_relu"], 1)

        @block.vector
        def _(dve):
            v = nc.vector
            for b in range(2 * C):
                last = v.memset(PS[:, b, :], 1.0)
            last.then_inc(sem["psum0"], 1)
            dve.wait_ge(sem["cst0"], 16)
            v.tensor_scalar(oneka[:], vec("k_a"), -1.0, 1.0, ALU.mult, ALU.add).then_inc(sem["oneka"], 1)

            def route_ids():
                rows = 3 * (NR + 1)
                dve.wait_ge(sem["ids"], 32)
                v.tensor_scalar(rtmp[:, 0, :], rid[:], 0.0, None, ALU.is_ge).then_inc(sem["r_steps"], 1)
                v.tensor_scalar(rtmp[:, 1, :], rid[:], float(NR - 1), None, ALU.is_le).then_inc(sem["r_steps"], 1)
                v.tensor_scalar(rtmp[:, 2, :], rid[:], float(-NR), None, ALU.add).then_inc(sem["r_steps"], 1)
                v.tensor_scalar(oneh[:], ridb[:], vec("eidx")[0:rows, :], vec("shared")[0:rows, :],
                                ALU.is_equal, ALU.max).then_inc(sem["r_oh"], 1)
                dve.wait_ge(sem["r_steps"], 2)
                v.tensor_tensor(rtmp[:, 3, :], rtmp[:, 0, :], rtmp[:, 1, :], ALU.mult).then_inc(sem["r_steps"], 1)
                dve.wait_ge(sem["r_steps"], 4)
                v.tensor_tensor(rtmp[:, 0, :], rtmp[:, 3, :], rtmp[:, 2, :], ALU.mult).then_inc(sem["r_steps"], 1)
                dve.wait_ge(sem["r_steps"], 5)
                v.tensor_scalar(ride[:], rtmp[:, 0, :], float(NR), None, ALU.add).then_inc(sem["r_id"], 1)
                dve.wait_ge(sem["cst4"], 16)
                rb = k("Rb", 0, NL * 128, 0, rows)
                hi, out_ = rb_split[:, 0, :], rb_split[:, 1, :]
                v.tensor_copy(hi, rb).then_inc(sem["rb_steps"], 1)
                dve.wait_ge(sem["rb_steps"], 1)
                v.scalar_tensor_tensor(out=rb, in0=hi, scalar=vec("rb_mid")[0:rows, :], in1=rb, op0=ALU.mult,
                                       op1=ALU.add).then_inc(sem["rb_steps"], 1)
                dve.wait_ge(sem["rb_steps"], 2)
                v.tensor_copy(hi, rb).then_inc(sem["rb_steps"], 1)
                dve.wait_ge(sem["rb_steps"], 3)
                v.scalar_tensor_tensor(out=out_, in0=hi, scalar=vec("rb_low")[0:rows, :], in1=rb, op0=ALU.mult,
                                       op1=ALU.add).then_inc(sem["rb_split"], 1)

            small = PP * E
            for name, i, c in ORDER:
                n = COUNT[name, i, c]
                if name == "mean":
                    src = slot(9) if LNS[i] == "gn" else H_
                    dve.wait_ge(sem["ln_mean"], n)
                    v.tensor_tensor(a(c, NORM_SLOTS[LNS[i]][0]), a(c, src), bank(c, 0),
                                    ALU.subtract).then_inc(sem["ln_xc"], 1)
                elif name == "var":
                    xc, sq = NORM_SLOTS[LNS[i]]
                    dst = xc if LNS[i] in ("lt", "gn") else N_
                    dve.wait_ge(sem["ln_rs"], n)
                    v.tensor_tensor(a(c, dst), a(c, xc), a(c, sq), ALU.mult).then_inc(sem["ln_out"], 1)
                    if LNS[i] == "lt":
                        dve.wait_ge(sem["ln_out"], n)
                        v.tensor_scalar(a(c, H_), a(c, dst), vec("gamma"), vec("beta"), ALU.mult,
                                        ALU.add).then_inc(sem["h0"], 1)
                    if LNS[i] == "gn":
                        dve.wait_ge(sem["ln_out"], n)
                        dve.wait_ge(sem["bonb"], c + 1)
                        v.scalar_tensor_tensor(out=a(c, dst), in0=a(c, dst), scalar=vec("gn_w"), in1=a(c, slot(8)),
                                               op0=ALU.mult, op1=ALU.add).then_inc(sem["gn_a"], 1)
                    if LNS[i] == "l3":
                        d, x = pair(a(c, slot(2))), pair(a(c, N_))
                        dve.wait_ge(sem["ln_out"], n)
                        v.tensor_tensor(d[:, :, 1:T], x[:, :, 0:T - 1], x[:, :, 1:T], ALU.subtract)
                        v.tensor_scalar(d[:, :, 0:1], x[:, :, 0:1], -1.0, None, ALU.mult).then_inc(sem["delta"], 1)
                        dve.wait_ge(sem["delta"], c + 1)
                        for u in (0, 2, 3, 1):
                            last = v.scalar_tensor_tensor(out=a(c, slot(3 + u)), in0=a(c, slot(2)),
                                                          scalar=vec(f"mix{u}"), in1=a(c, N_), op0=ALU.mult, op1=ALU.add)
                            last.then_inc(sem["xi"], 1)
                elif name in ("q", "k"):
                    if c == 0:
                        dve.wait_ge(sem["cst1"], 16)
                    d0, d1 = (slot(2), slot(3)) if name == "q" else (slot(4), PT_)
                    dve.wait_ge(sem[f"{name}_mm"], n)
                    v.tensor_tensor(pair(a(c, d0)), pair(bank(c, 0)), over_pairs(k(f"cos{name}")), ALU.mult)
                    v.tensor_tensor(pair(a(c, d1)), pair(bank(c, 1)), over_pairs(k(f"sin{name}")),
                                    ALU.mult).then_inc(sem[f"{name}_mul"], 1)
                elif name == "v":
                    if c == 0:
                        dve.wait_ge(sem["init"], C)
                    dve.wait_ge(sem["v_mm"], n)
                    to, ones, source = values_of(c, 0)
                    v.tensor_copy(ones, vec("tok")[0:64, :].broadcast_to([64, PP * 2 * NKV]))
                    for j in range(2):
                        last = v.tensor_scalar(to[:, :, j], source[j], vec("tok")[0:64, :], None, ALU.mult)
                    last.then_inc(sem["vd"], 1)
                    if c == C - 1:
                        route_ids()
                elif name == "s":
                    sc = bank(c, 0).rearrange("q (h t) -> q h t", t=T)
                    dve.wait_ge(sem["s_mm"], n)
                    v.tensor_reduce(smax[:, c, :], sc, AX.X, ALU.max).then_inc(sem["s_max"], 1)
                    dve.wait_ge(sem["s_max"], n)
                    v.tensor_tensor(a(c, PB_, 512).rearrange("q (h t) -> q h t", t=64)[:, :, 0:T], sc,
                                    smax[:, c, :].unsqueeze(2).broadcast_to([128, NH, T]),
                                    ALU.subtract).then_inc(sem["s_sub"], 1)
                elif name == "pv":
                    o = bank(c, 1, 512).rearrange("q (g u) -> q g u", g=NKV)[:, :, T:T + 18].rearrange(
                        "q g (h u) -> q g h u", u=HD + 1)
                    rec = orec[:, c, :].rearrange("q (g h) -> q g h", h=2).unsqueeze(3)
                    dve.wait_ge(sem["pv_mm"], n)
                    v.reciprocal(rec, o[:, :, :, HD:HD + 1]).then_inc(sem["o_rec"], 1)
                    dve.wait_ge(sem["o_rec"], n)
                    v.tensor_tensor(a(c, slot(2) + i * D, D).rearrange("q (g h d) -> q g h d", h=2, d=HD),
                                    o[:, :, :, 0:HD], rec.broadcast_to([128, NKV, 2, HD]), ALU.mult).then_inc(sem["att"], 1)
                elif name == "wo":
                    dve.wait_ge(sem["wo_mm"], n)
                    v.tensor_tensor(a(c, H_), a(c, H_), bank(c, 1), ALU.add).then_inc(sem["h1"], 1)
                elif name == "top2":
                    dve.wait_ge(sem["cst2"], 16)
                    dve.wait_ge(sem["gate_mm"], C)
                    steps = [0]

                    def step(instruction):
                        steps[0] += 1
                        instruction.then_inc(sem["g_steps"], 1)
                        dve.wait_ge(sem["g_steps"], steps[0])

                    def rows(r):
                        return gate(r).rearrange("q (r e) -> q r e", e=E)

                    def chunks(ap):
                        return ap.rearrange("q (c p e) -> q c p e", c=C, e=E)

                    def wide(ap):
                        return ap.unsqueeze(2).broadcast_to([128, C * PP, E])

                    prob, equal, first, rest = rows(0), rows(1), rows(2), rows(3)
                    top = gate(4, C * PP)
                    desc = k("desc").unsqueeze(1).broadcast_to([128, C * PP, E])
                    logits = PS.rearrange("q (c b) n -> q c b n", b=2)[:, :, 0, 0:small].rearrange(
                        "q c (p e) -> q c p e", e=E)
                    step(v.tensor_tensor(chunks(gate(0)), logits,
                                         k("gb").unsqueeze(1).unsqueeze(1).broadcast_to([128, C, PP, E]), ALU.add))
                    step(v.tensor_reduce(top, prob, AX.X, ALU.max))
                    v.tensor_tensor(prob, prob, wide(top), ALU.subtract).then_inc(sem["g_sub"], 1)
                    dve.wait_ge(sem["g_exp"], 1)
                    step(v.tensor_reduce(top, prob, AX.X, ALU.add))
                    step(v.reciprocal(top, top))
                    step(v.tensor_tensor(prob, prob, wide(top), ALU.mult))
                    for source, taken in ((prob, first), (rest, equal)):
                        step(v.tensor_reduce(top, source, AX.X, ALU.max))
                        step(v.tensor_tensor(equal, source, wide(top), ALU.is_equal))
                        step(v.tensor_tensor(equal, equal, desc, ALU.mult))
                        step(v.tensor_reduce(top, equal, AX.X, ALU.max))
                        step(v.tensor_tensor(taken, equal, wide(top), ALU.is_equal))
                        if taken is first:
                            step(v.scalar_tensor_tensor(out=rest, in0=first, scalar=-2.0, in1=prob, op0=ALU.mult,
                                                        op1=ALU.add))
                    step(v.tensor_tensor(equal, equal, first, ALU.add))
                    for cc in range(C):
                        def thrice(r):
                            return gate(r)[:, cc * small:(cc + 1) * small].rearrange(
                                "q (p e) -> q p e", e=E).unsqueeze(2).broadcast_to([128, PP, 3, E])
                        v.tensor_tensor(a(cc, CW_, 3 * small).rearrange("q (p r e) -> q p r e", r=3, e=E), thrice(1),
                                        thrice(0), ALU.mult).then_inc(sem["cw"], 1)
                elif name == "cwT":
                    dve.wait_ge(sem["c_hi"], n)
                    v.scalar_tensor_tensor(out=a(c, slot(5)), in0=part_bf(c, 10), scalar=vec("cw_mid"), in1=bank(c, 1),
                                           op0=ALU.mult, op1=ALU.add).then_inc(sem["c_r"], 1)
                elif name == "cw2":
                    dve.wait_ge(sem["c_mid"], n)
                    v.scalar_tensor_tensor(out=part_bf(c, 12), in0=part_bf(c, 11), scalar=vec("cw_low"),
                                           in1=a(c, slot(5)), op0=ALU.mult, op1=ALU.add).then_inc(sem["cwT"], 1)
                elif name == "b2":
                    dve.wait_ge(sem["b2_mm"], n)
                    v.tensor_tensor(a(c, H_), a(c, H_), bank(c, 0), ALU.add).then_inc(sem["b2_add"], 1)
                elif name == "y":
                    dve.wait_ge(sem["cwb"], n)
                    if i >= 2:
                        dve.wait_ge(sem["acc"], COUNT["y", i - 2, c])
                    v.tensor_tensor(a(c, slot(3 + i % 2)), bank(c, 0), a(c, slot(8)), ALU.mult).then_inc(sem["y_mul"], 1)
                elif name == "rk":
                    if c == 0:
                        dve.wait_ge(sem["cst3"], 16)
                        dve.wait_ge(sem["oneka"], 1)
                    dve.wait_ge(sem["rk"], n)
                    v.tensor_scalar(a(c, slot(3)), a(c, slot(10)), vec("k_k"), None, ALU.mult).then_inc(sem["kk0"], 1)
                elif name == "aw":
                    dve.wait_ge(sem["aw_mm"], n)
                    v.tensor_copy(a(c, slot(13)), bank(c, 0)).then_inc(sem["aw_aa"], 1)
                    dve.wait_ge(sem["aw_sg"], n)
                    v.tensor_tensor_scan(a(c, slot(12)), k("reset"), a(c, slot(14)), 0.0, ALU.mult,
                                         ALU.add).then_inc(sem["cs"], 1)
                elif name == "gh":
                    dve.wait_ge(sem["ab"], n)
                    dve.wait_ge(sem["cs"], n)
                    v.tensor_scalar(a(c, slot(14)), a(c, slot(15)), vec("k_a"), oneka[:], ALU.mult,
                                    ALU.add).then_inc(sem["tk"], 1)
                    dve.wait_ge(sem["tk"], n)
                    v.tensor_tensor(a(c, slot(10)), a(c, slot(10)), a(c, slot(14)), ALU.mult).then_inc(sem["kp"], 1)
                elif name == "gg":
                    dve.wait_ge(sem["g_hid"], n)
                    dve.wait_ge(sem["kp"], n)
                    v.scalar_tensor_tensor(out=a(c, slot(8)), in0=a(c, slot(9)), scalar=vec("r_k"), in1=a(c, slot(10)),
                                           op0=ALU.mult, op1=ALU.mult).then_inc(sem["bon0"], 1)
                elif name == "kk":
                    dve.wait_ge(sem["kk_mm"], n)
                    v.tensor_scalar(a(c, slot(4)), bank(c, 1), float(D), 1e-24, ALU.mult,
                                    ALU.max).then_inc(sem["kk_cl"], 1)
                elif name == "kb":
                    dve.wait_ge(sem["em"], n)
                    v.tensor_tensor(a(c, slot(7)), a(c, slot(10)), a(c, slot(14)), ALU.mult).then_inc(sem["kt"], 1)
                    dve.wait_ge(sem["kk_rs"], n)
                    v.tensor_tensor(a(c, slot(3)), a(c, slot(3)), a(c, slot(4)), ALU.mult).then_inc(sem["kk"], 1)
                    dve.wait_ge(sem["kk"], n)
                    for j in range(2):
                        kr = a(c, KR_[j], 2 * W).rearrange("q (p u t) -> q p u t", u=2, t=T)
                        v.scalar_tensor_tensor(out=kr[:, :, 0, 1:T], in0=pair(a(c, slot(3)))[:, :, 1:T],
                                               scalar=vec(f"feat{j}"), in1=pair(a(c, slot(13)))[:, :, 0:T - 1],
                                               op0=ALU.mult, op1=ALU.mult)
                        last = v.tensor_scalar(kr[:, :, 0, 0:1], pair(a(c, slot(3)))[:, :, 0:1], vec(f"feat{j}"), None,
                                               ALU.mult)
                    last.then_inc(sem["kr1"], 1)
                elif name == "bon":
                    dve.wait_ge(sem["bon_mm"], n)
                    v.scalar_tensor_tensor(out=a(c, slot(8)), in0=bank(c, 1), scalar=float(D), in1=a(c, slot(11)),
                                           op0=ALU.mult, op1=ALU.mult).then_inc(sem["bon"], 1)
                elif name == "m":
                    dve.wait_ge(sem["m_mm"], n)
                    src = PS[:, 2 * c:2 * c + 2, 0:10 * T].rearrange("q b (i u) -> q b i u", u=5 * T)
                    m4 = a(c, M4_ + i * 2 * W, 2 * W).rearrange("q (b i u) -> q b i u", b=2, u=4 * T)
                    lm = a(c, L_ + i * (W // 2), W // 2).rearrange("q (b i u) -> q b i u", b=2, u=T)
                    v.tensor_tensor(m4, src[:, :, :, 0:4 * T],
                                    k("mask4").unsqueeze(1).unsqueeze(1).broadcast_to([128, 2, 2, 4 * T]),
                                    ALU.mult)
                    v.tensor_tensor(lm, src[:, :, :, 4 * T:5 * T],
                                    k("maskL").unsqueeze(1).unsqueeze(1).broadcast_to([128, 2, 2, T]),
                                    ALU.mult).then_inc(sem["m_ev"], 1)
                elif name == "lx":
                    dve.wait_ge(sem["x_mm"], n)
                    x = a(c, X_[0], 2 * (X_[1] - X_[0])).rearrange("q (j w) -> q j w", j=2)[:, :, 0:W]
                    level = k("levels", 2 * i * T, 2 * (i + 1) * T).rearrange("q (j t) -> q j t", j=2)
                    v.tensor_tensor(x.rearrange("q j (p t) -> q j p t", t=T),
                                    pair(bank(c, 0)).unsqueeze(1).broadcast_to([128, 2, PP, T]),
                                    level.unsqueeze(2).broadcast_to([128, 2, PP, T]), ALU.mult).then_inc(sem["x_ev"], 1)
                elif name == "lt":
                    dve.wait_ge(sem["t_mm"], n)
                    if i < len(LEVELS) - 1:
                        tt = halves(a(c, TT_, 2 * W))
                        v.tensor_tensor(tt, tt, both(c), ALU.subtract).then_inc(sem["t_ev"], 1)
                    else:
                        tt = a(c, TT_, 2 * W).rearrange("q (p u t) -> q p u t", u=2, t=T)[:, :, 1, :]
                        v.tensor_tensor(tt, tt, pair(bank(c, 1)), ALU.subtract).then_inc(sem["t_ev"], 1)
                elif name == "w":
                    dve.wait_ge(sem["w_mm"], n)
                    v.tensor_tensor(a(c, Y_, 512), a(c, Y_, 512), bank(c, 1, 512), ALU.subtract).then_inc(sem["sa"], 1)
                    dve.wait_ge(sem["sa"], 2 * n - 1)
                    v.tensor_scalar(a(c, SA_[1], 512), a(c, Y_, 512), vec("tok1"), None, ALU.mult).then_inc(sem["sa"], 1)
                elif name == "ro":
                    dve.wait_ge(sem["ro_mm"], n)
                    v.tensor_tensor(a(c, H_), a(c, H_), bank(c, 0), ALU.add).then_inc(sem["h3"], 1)
                elif name == "fo":
                    dve.wait_ge(sem["fo_mm"], n)
                    v.scalar_tensor_tensor(out=a(c, slot(6)), in0=bank(c, 0), scalar=vec("bo"), in1=a(c, H_), op0=ALU.add,
                                           op1=ALU.add).then_inc(sem["fo"], 1)

        @block.tensor
        def _(pe):
            def mm(o, l, r, start=True, stop=True):
                return nc.tensor.matmul(o, l, r, start=start, stop=stop)

            def m4(c, p, u):
                return a(c, M4_ + (4 * p + u) * T, T)

            def tt(c, p, u):
                return a(c, TT_ + (2 * p + u) * T, T)

            pairs = [(i, j) for i in range(PP) for j in range(2)]
            pe.wait_ge(sem["psum0"], 1)
            pe.wait_ge(sem["cst0"], 16)
            for name, i, c in ORDER:
                n = COUNT[name, i, c]
                if name == "tok":
                    pe.wait_ge(sem[f"x{c}"], 16)
                    xt = a(c, XT_, 2 * PP * CH).rearrange("q (j p t) -> q j p t", j=2, t=CH)
                    for j in range(2):
                        mm(bank(c, 0, W, 0, 64 * j, 64 * j + 64), k("tokA"), xt[:, j, :, 0:T], stop=False)
                        last = mm(bank(c, 0, W, 0, 64 * j, 64 * j + 64), k("tokB"), xt[:, j, :, 1:T + 1], start=False)
                    last.then_inc(sem["tok_mm"], 1)
                elif name == "mean":
                    ready = {"lt": ("tok_y", c + 1), "l1": ("h0", c + 1), "l2": ("h1", c + 1),
                             "l3": ("acc", COUNT["y", E - 1, c]), "gn": ("o_ev", c + 1), "l4": ("h3", c + 1)}[LNS[i]]
                    pe.wait_ge(sem[ready[0]], ready[1])
                    src = slot(9) if LNS[i] == "gn" else H_
                    mm(bank(c, 0), k("mean"), a(c, src)).then_inc(sem["ln_mean"], 1)
                elif name == "var":
                    pe.wait_ge(sem["ln_sq"], COUNT["mean", i, c])
                    mm(bank(c, 1), k("mean"), a(c, NORM_SLOTS[LNS[i]][1])).then_inc(sem["ln_var"], 1)
                elif name == "q":
                    if c == 0:
                        pe.wait_ge(sem["cst1"], 16)
                    pe.wait_ge(sem["ln_out"], COUNT["var", 1, c])
                    mm(bank(c, 0), k("wq"), a(c, N_))
                    mm(bank(c, 1), k("wqr"), a(c, N_)).then_inc(sem["q_mm"], 1)
                elif name == "k":
                    pe.wait_ge(sem["q_mul"], n)
                    mm(bank(c, 0), k("wk"), a(c, N_))
                    mm(bank(c, 1), k("wkr"), a(c, N_)).then_inc(sem["k_mm"], 1)
                elif name == "v":
                    pe.wait_ge(sem["k_mul"], n)
                    for hh in range(2):
                        for p, j in pairs:
                            last = mm(PS[64 * hh:64 * hh + T, 2 * c + j, 32 * p:32 * p + 32],
                                      a(c, N_ + p * T, T), k("wv", 32 * j, 32 * j + 32))
                    last.then_inc(sem["v_mm"], 1)
                elif name == "s":
                    pe.wait_ge(sem["kx"], n)
                    if i == 0:
                        if c == 0:
                            pe.wait_ge(sem["cst_bf"], 16)
                        pe.wait_ge(sem["vd_hi"], c + 1)
                        pe.wait_ge(sem["q_bd"], c + 1)
                        pe.wait_ge(sem["vd"], c + 1)
                    else:
                        pe.wait_ge(sem["s_sub"], COUNT["s", i - 1, c])
                    mm(bank(c, 0).rearrange("q (h t) -> q h t", t=T), identb,
                       maskb.unsqueeze(1).broadcast_to([128, NH, T]), stop=False)
                    mm(bank(c, 0), a(c, QBD_ + 128 * i, 128), a(c, KX_ + i * W), start=False).then_inc(sem["s_mm"], 1)
                elif name == "t":
                    pe.wait_ge(sem["s_exp"], COUNT["e", i, c])
                    if i:
                        pe.wait_ge(sem["att"], COUNT["pv", i - 1, c])
                    for g in range(NKV):
                        last = nc.tensor.transpose(bank(c, 1, 128, 128 * g), a(c, PB_ + 128 * g, 128), k("identf"))
                    last.then_inc(sem["pt_mm"], 1)
                elif name == "pv":
                    pe.wait_ge(sem["pt_ev"], COUNT["t", i, c])
                    for g in range(NKV):
                        for j in range(2):
                            last = mm(bank(c, 1, 18, 128 * g + T, 64 * j, 64 * j + T),
                                      a(c, PT_ + 128 * g + 64 * j, T, 0, 64 + T),
                                      a(c, VD_ + ((i * 2 + j) * NKV + g) * 18, 18, 0, 64 + T))
                    last.then_inc(sem["pv_mm"], 1)
                elif name == "attT":
                    pe.wait_ge(sem["att"], COUNT["pv", PP - 1, c])
                    for p, j in pairs:
                        last = mm(bank(c, 0, T, p * T, 64 * j, 64 * j + 64), a(c, slot(2) + p * D, D),
                                  k("identf", 64 * j, 64 * j + T))
                    last.then_inc(sem["attT_mm"], 1)
                elif name == "wo":
                    pe.wait_ge(sem["attT"], n)
                    mm(bank(c, 1), k("wo"), a(c, slot(4))).then_inc(sem["wo_mm"], 1)
                elif name == "gate":
                    if c == 0:
                        pe.wait_ge(sem["cst2"], 16)
                    pe.wait_ge(sem["ln_out"], COUNT["var", 2, c])
                    for p, j in pairs:
                        last = mm(to_bank(c, 0, E, j, p, T), a(c, N_ + p * T, T), k("gw", j * E, j * E + E))
                    last.then_inc(sem["gate_mm"], 1)
                elif name == "cwT":
                    pe.wait_ge(sem["cw"], n)
                    pe.wait_ge(sem["gelu"], COUNT["hid", 0, c])
                    for p, j in pairs:
                        last = mm(to_bank(c, 1, T, j, p, 3 * E), a(c, CW_ + 3 * p * E, 3 * E), k("identf", 64 * j, 64 * j + T))
                    last.then_inc(sem["cwT_mm"], 1)
                elif name == "b2":
                    pe.wait_ge(sem["c_r"], n)
                    mm(bank(c, 0), k("b2"), a(c, slot(5))).then_inc(sem["b2_mm"], 1)
                elif name == "hid":
                    if i == 0:
                        pe.wait_ge(sem["g_steps"], 1)
                    else:
                        pe.wait_ge(sem["y_mul"], COUNT["y", i - 1, c])
                    for j in range(2):
                        last = mm(bank(c, j), k("w1", i * HID, i * HID + HID, 64 * j, 64 * j + 64), half(c, N_, j, 0, W, 64))
                    last.then_inc(sem["hid_mm"], 1)
                elif name == "y":
                    if i == 0:
                        pe.wait_ge(sem["cwT"], n)
                        pe.wait_ge(sem["b2_add"], n)
                    pe.wait_ge(sem["gelu"], n)
                    for j in range(2):
                        mm(bank(c, 0, W, 0, 64 * j, 64 * j + 64), k("w2", i * D, i * D + D), a(c, slot(6 + j)))
                    mm(bank(c, 1), selb[:, i * 128:i * 128 + 128], part_bf(c, 12)).then_inc(sem["y_mm"], 1)
                elif name == "rk":
                    if c == 0:
                        pe.wait_ge(sem["cst3"], 16)
                    pe.wait_ge(sem["xi"], 4 * n)
                    mm(bank(c, 0), k("Wr"), a(c, slot(3)))
                    mm(bank(c, 1), k("Wk"), a(c, slot(5))).then_inc(sem["rk_mm"], 1)
                elif name == "vw":
                    pe.wait_ge(sem["rk"], n)
                    mm(bank(c, 0), k("Wvf"), a(c, slot(6)))
                    mm(bank(c, 1), k("Aw"), a(c, slot(4))).then_inc(sem["vw_mm"], 1)
                elif name == "aw":
                    pe.wait_ge(sem["xi_late"], n)
                    pe.wait_ge(sem["vw"], n)
                    mm(bank(c, 0), k("Aa"), a(c, slot(7)))
                    mm(bank(c, 1), k("Bw"), a(c, slot(12))).then_inc(sem["aw_mm"], 1)
                elif name == "ab":
                    pe.wait_ge(sem["aw_aa"], n)
                    mm(bank(c, 0), k("Ba"), a(c, slot(13))).then_inc(sem["ab_mm"], 1)
                elif name == "gh":
                    pe.wait_ge(sem["ab"], n)
                    pe.wait_ge(sem["aw_sg"], n)
                    for j in range(2):
                        last = mm(bank(c, j), k("Ag", 0, 128, 64 * j, 64 * j + 64), half(c, slot(8), j, 0, W, 64))
                    last.then_inc(sem["g_hid"], 1)
                elif name == "gg":
                    pe.wait_ge(sem["g_sig"], n)
                    for j in range(2):
                        last = mm(bank(c, 0, W, 0, 64 * j, 64 * j + 64), k("Bg"), a(c, slot(16 + j)))
                    last.then_inc(sem["gg_mm"], 1)
                elif name == "kk":
                    pe.wait_ge(sem["kk_sq"], n)
                    mm(bank(c, 1), k("mean"), a(c, slot(4))).then_inc(sem["kk_mm"], 1)
                elif name == "bon":
                    pe.wait_ge(sem["bon0"], n)
                    pe.wait_ge(sem["kk_cl"], n)
                    mm(bank(c, 1), k("mean"), a(c, slot(8))).then_inc(sem["bon_mm"], 1)
                elif name == "m":
                    if i == 0:
                        for ready in ("bt", "kt", "krb", "kr1", "bon"):
                            pe.wait_ge(sem[ready], COUNT["kk", 0, c])
                    else:
                        pe.wait_ge(sem["m_ev"], COUNT["m", 0, c])
                    for q in range(PP // 2):
                        p = i * PP // 2 + q
                        kt, bt = a(c, slot(7) + p * T, T), a(c, slot(5) + p * T, T)
                        for u in range(3):
                            for j in range(2):
                                kr = KR_[j] + 2 * p * T
                                l, r = [(kt, a(c, kr, 2 * T)), (bt, a(c, kr, 2 * T)), (a(c, kr, T), bt)][u]
                                col = (q % 2) * 5 * T + 2 * T * u
                                last = mm(PS[64 * j:64 * j + T, 2 * c + q // 2, col:col + (1 if u == 2 else 2) * T], l, r)
                    last.then_inc(sem["m_mm"], 1)
                elif name == "vt":
                    pe.wait_ge(sem["m_ev"], COUNT["m", 1, c])
                    for p, j in pairs:
                        last = mm(to_bank(c, 0, D, j, p, T), a(c, slot(6) + p * T, T), k("Wvf", 64 * j, 64 * j + 64))
                    last.then_inc(sem["vt_mm"], 1)
                elif name == "lx":
                    if i == 0:
                        pe.wait_ge(sem["tt1"], COUNT["m", 1, c])
                        pe.wait_ge(sem["ltb"], COUNT["m", 1, c])
                        pe.wait_ge(sem["vt"], COUNT["vt", 0, c])
                    else:
                        pe.wait_ge(sem["t_ev"], COUNT["lt", i - 1, c])
                    for p, j in pairs:
                        last = mm(to_bank(c, 0, T, j, p, T), a(c, LT_[j] + p * T, T), tt(c, p, 0))
                    last.then_inc(sem["x_mm"], 1)
                elif name == "lt":
                    pe.wait_ge(sem["x_ev"], n)
                    for p in range(PP):
                        if i < len(LEVELS) - 1:
                            lo = (p % 4) * 2 * T
                            for j in range(2):
                                last = mm(PS[64 * j:64 * j + T, 2 * c + p // 4, lo:lo + T], tt(c, p, 1),
                                          a(c, X_[j] + p * T, T))
                            for j in range(2):
                                last = mm(PS[64 * j:64 * j + T, 2 * c + p // 4, lo + T:lo + 2 * T],
                                          a(c, X_[j] + p * T, T), tt(c, p, 1))
                        else:
                            for j in range(2):
                                last = mm(to_bank(c, 1, T, j, p, T), a(c, X_[j] + p * T, T), tt(c, p, 1))
                    last.then_inc(sem["t_mm"], 1)
                elif name == "u":
                    pe.wait_ge(sem["t_ev"], COUNT["lt", len(LEVELS) - 1, c])
                    for p, j in pairs:
                        last = mm(to_bank(c, 0, D, j, p, T), m4(c, p, 0), a(c, VT_[j] + p * D, D))
                    last.then_inc(sem["u_mm"], 1)
                elif name == "y2":
                    pe.wait_ge(sem["ttb"], n)
                    pe.wait_ge(sem["u_ev"], n)
                    for p, j in pairs:
                        last = mm(to_bank(c, 1, D, j, p, T), a(c, TB_[j] + p * T, T), a(c, U_ + p * D, D))
                    last.then_inc(sem["y_mm2"], 1)
                elif name == "z":
                    pe.wait_ge(sem["lt32"], n)
                    pe.wait_ge(sem["y_ev"], n)
                    for p, j in pairs:
                        last = mm(to_bank(c, 0, D, j, p, T), a(c, LT_[j] + p * T, T), a(c, Y_ + p * D, D))
                    last.then_inc(sem["z_mm"], 1)
                elif name == "w":
                    pe.wait_ge(sem["z_ev"], n)
                    for p, j in pairs:
                        last = mm(to_bank(c, 1, D, j, p, T), a(c, TB_[j] + p * T, T), a(c, U_ + p * D, D))
                    last.then_inc(sem["w_mm"], 1)
                elif name == "o":
                    pe.wait_ge(sem["sab"], n)
                    pe.wait_ge(sem["sa"], 2 * n)
                    for p in range(PP):
                        for u in range(2):
                            for j in range(2):
                                last = mm(bank(c, 0, T, p * T, 64 * j, 64 * j + 64),
                                          a(c, (SA_, VT_)[u][j] + p * D, D), m4(c, p, (3, 1)[u]), start=(u == 0),
                                          stop=(u == 1))
                    last.then_inc(sem["o_mm"], 1)
                elif name == "ro":
                    pe.wait_ge(sem["gn_g"], n)
                    mm(bank(c, 0), k("Wo"), a(c, slot(10))).then_inc(sem["ro_mm"], 1)
                elif name == "f":
                    if c == 0:
                        pe.wait_ge(sem["cst4"], 16)
                        pe.wait_ge(sem["r_oh"], 1)
                        pe.wait_ge(sem["rb_split"], 1)
                        pe.wait_ge(sem["wsI"], NL)
                    pe.wait_ge(sem["ln_out"], COUNT["var", 5, c])
                    for j in range(2):
                        last = mm(bank(c, j), k("Wi", 0, 128, 64 * j, 64 * j + 64), half(c, N_, j, 0, W, 64))
                    last.then_inc(sem["f_mm"], 1)
                elif name == "r":
                    if i == 0:
                        pe.wait_ge(sem["f_relu"], c + 1)
                    else:
                        pe.wait_ge(sem["r_relu"], COUNT["r", 0, c])
                    pe.wait_ge(sem[f"wg{i}_{c}"], 16 * 2 * PP)
                    src = slot(2 if i == 0 else 4)
                    for j in range(2):
                        mm(pair(bank(c, j)), rb_split[:, 1, 128 * i:128 * i + 128],
                           oneh[:, 32 * j + PP * c:32 * j + PP * c + PP].unsqueeze(2).broadcast_to([3 * (NR + 1), PP, T]),
                           stop=False)
                        for p in range(PP):
                            b = PP * j + p
                            w = WG0[:, 2 * PP * c + b, :] if i == 0 else a(c, WG1_ + 128 * b, 128)
                            mm(bank(c, j, T, p * T), w, a(c, src + j * W + p * T, T), start=False, stop=False)
                        last = mm(bank(c, j), k("Ws", 128 * i, 128 * i + 128), a(c, src + j * W), start=False)
                    last.then_inc(sem["r_mm"], 1)
                elif name == "fo":
                    pe.wait_ge(sem["r_relu"], COUNT["r", 1, c])
                    for j in range(2):
                        last = mm(bank(c, 0, W, 0, 64 * j, 64 * j + 64), k("WoT"), a(c, slot(2 + j)))
                    last.then_inc(sem["fo_mm"], 1)


def shape_constants():
    z = {}
    pos = np.arange(T, dtype=np.float32)
    inv = (1.0 / 10000.0 ** (np.arange(0, HD, 2, dtype=np.float32) / HD)).astype(np.float32)
    fr = np.outer(pos, inv).astype(np.float32)
    emb = np.concatenate([fr, fr], -1)
    cos = np.tile(np.cos(emb).T, (2 * NH, 1)).astype(np.float32)
    sin = np.tile(np.sin(emb).T, (2 * NH, 1)).astype(np.float32)
    sign = np.tile(np.where(np.arange(HD) < HD // 2, -1.0, 1.0), 2 * NH)[:, None].astype(np.float32)
    sc = np.float32(1.0 / np.sqrt(HD))
    z["cosq"], z["sinq"], z["cosk"], z["sink"] = cos * sc, sin * sign * sc, cos, sin * sign
    q = np.arange(128)
    z["headmask"] = ((q % 64) // HD)[:, None] == np.arange(NH)[None, :]
    z["identf"] = np.eye(128)
    r = (q % 64)[:, None]
    t = np.arange(T)[None, :]
    z["mean"] = ((q[:, None] // 64) == (q[None, :] // 64)) / float(D)
    z["desc"] = np.tile(float(E) - np.arange(E)[None, :], (128, 1))
    z["reset"] = np.tile((np.arange(W) % T != 0)[None, :], (128, 1))
    z["mask4"] = np.concatenate([r < t, r <= t, r < t, -1.0 * (r <= t)], 1)
    z["maskL"] = (r > t) & (r < T)
    z["negm1"] = -1.0 * ((r // 2 == t // 2) & (r > t))
    z["negm1T"] = -1.0 * ((r // 2 == t // 2) & (r < t))
    z["eye2"] = np.concatenate([r == t, r == t], 1)
    z["levels"] = np.concatenate([(r // (2 * b) == t // (2 * b)) & (r // b > t // b) & (r < T) & (q[:, None] // 64 == j)
                                  for b in LEVELS for j in range(2)], 1)
    z["row32"] = r >= 32
    out = {n: np.asarray(x, np.float32) for n, x in z.items()}
    causal = np.where((r < T) & (t > r), NEG, 0.0)
    sel = np.zeros((128, E, 128))
    for e in range(E):
        for j in range(2):
            for part in range(3):
                sel[64 * j + E * part + e, e, 64 * j:64 * j + 64] = 1
    return out, np.concatenate([np.eye(128), causal, sel.reshape(128, -1)], 1)


def kernel(**inputs):
    import ml_dtypes
    import concourse.bacc as _bacc
    from concourse import mybir as _mybir
    from concourse.bass_utils import run_bass_kernel_spmd as _run

    inp = {n: np.asarray(x) for n, x in inputs.items()}
    cst, bf = shape_constants()

    def bd(m):
        o = np.zeros((128, 2 * m.shape[1]), np.float32)
        o[:64, :m.shape[1]] = m
        o[64:, m.shape[1]:] = m
        return o

    def dup(m):
        return np.concatenate([m, m], 0)

    wt = inp["L0_tok_W"]
    rot = np.concatenate([(np.arange(HD) + HD // 2) % HD + h * HD for h in range(NH)])
    kvrow = np.concatenate([np.arange(HD) + (h // (NH // NKV)) * HD for h in range(NH)])
    wq, wk = inp["L0_attn_Wq"], inp["L0_attn_Wk"][kvrow]
    cst.update(
        tokA=wt[:, :128].T, tokB=wt[:, 128:].T, wq=bd(wq.T), wqr=bd(wq[rot].T), wk=bd(wk.T), wkr=bd(wk[rot].T),
        wv=bd(inp["L0_attn_Wv"].T), wo=bd(inp["L0_attn_Wo"].T), gw=bd(inp["L0_ffn_gate_w"]),
        gb=np.tile(inp["L0_ffn_gate_b"][None], (128, 1)), b1=inp["L0_ffn_b1"].T,
        w1=dup(inp["L0_ffn_W1"].transpose(1, 0, 2).reshape(D, -1)),
        w2=inp["L0_ffn_W2"].transpose(1, 0, 2).reshape(HID, -1),
        Wr=bd(inp["L1_attn_W_r"]), Wk=bd(inp["L1_attn_W_k"]), Wvf=bd(inp["L1_attn_W_v"]),
        Aw=bd(inp["L1_attn_A_w"]), Bw=bd(inp["L1_attn_B_w"]), Aa=bd(inp["L1_attn_A_a"]), Ba=bd(inp["L1_attn_B_a"]),
        Ag=dup(inp["L1_attn_A_g"]), Bg=inp["L1_attn_B_g"], Wo=bd(inp["L1_attn_W_o"]),
        Wi=dup(inp["L1_ffn_Wi"].T), Ws=inp["L1_ffn_Ws"][:, 0].transpose(2, 0, 1).reshape(128, -1),
        WoT=inp["L1_ffn_Wo"].T)
    b2 = np.zeros((128, 128), np.float32)
    b2[0:E, 0:64] = inp["L0_ffn_b2"]
    b2[64:64 + E, 64:128] = inp["L0_ffn_b2"]
    rb = np.zeros((128, NL * 128), np.float32)
    for part in range(3):
        at = part * (NR + 1)
        rb[at:at + NR] = inp["L1_ffn_br"].transpose(1, 0, 2).reshape(NR, -1)
        rb[at + NR] = inp["L1_ffn_bs"][:, 0].reshape(-1)
    cst["b2"], cst["Rb"] = b2, rb
    vecs = np.zeros((128, 36), np.float32)
    cols = dict(tok_b=inp["L0_tok_b"], gamma=inp["L0_tok_gamma"], beta=inp["L0_tok_beta"], b_w=inp["L1_attn_b_w"],
                b_a=inp["L1_attn_b_a"], k_k=inp["L1_attn_k_k"], k_a=inp["L1_attn_k_a"], r_k=inp["L1_attn_r_k"],
                gn_w=inp["L1_attn_gn_w"], gn_b=inp["L1_attn_gn_b"], bo=inp["L1_ffn_bo"])
    for i in range(6):
        cols[f"mix{i}"] = inp["L1_attn_x_mix"][i]
    for n, x in cols.items():
        vecs[:, VECS.index(n)] = np.concatenate([x, x])
    vecs[:, VECS.index("bi")] = inp["L1_ffn_bi"]
    vecs[:, VECS.index("eps_ln")] = 1e-5
    vecs[:, VECS.index("eps_gn")] = D * 1e-5
    vecs[:, VECS.index("ten_ln2")] = 10.0 * np.log(2.0)
    row = np.arange(128)
    vecs[:, VECS.index("eidx")] = row % (NR + 1)
    vecs[:, VECS.index("shared")] = row % (NR + 1) == NR
    vecs[:, VECS.index("cw_mid")] = -1.0 * (row % 64 // E >= 1)
    vecs[:, VECS.index("cw_low")] = -1.0 * (row % 64 // E >= 2)
    vecs[:, VECS.index("rb_mid")] = -1.0 * (row // (NR + 1) >= 1)
    vecs[:, VECS.index("rb_low")] = -1.0 * (row // (NR + 1) >= 2)
    for j in range(2):
        for n, rows in (("feat", D), ("tok", T), ("early", 32)):
            vecs[64 * j:64 * j + rows, VECS.index(f"{n}{j}")] = 1
    vecs[:, VECS.index("tok")] = row % 64 < T
    cst["vecs"] = vecs
    packed = np.zeros((128, N_CONST), np.float32)
    for n, (o, w) in COL.items():
        packed[:cst[n].shape[0], o:o + w] = cst[n]
    x = inp["x"][:, :CH * STRIDE].reshape(2, C, PP, CH, STRIDE * F_IN)
    xT = np.ascontiguousarray(x.transpose(4, 1, 0, 2, 3).reshape(128, C, 2 * PP * CH))
    wr = np.zeros((128, NL, NR + 1, 128), np.float32)
    wr[:, :, :NR] = inp["L1_ffn_Wr"].transpose(3, 0, 1, 2)
    arrays = {
        "xT": xT, "consts": packed, "masks_bf": np.ascontiguousarray(bf.astype(ml_dtypes.bfloat16)),
        "route": np.ascontiguousarray(inp["L1_ffn_route_id"].reshape(1, B)), "wr": wr.reshape(128, -1),
    }
    nc = _bacc.Bacc("TRN2", target_bir_lowering=False, num_devices=1)
    args = [nc.dram_tensor(n, v.shape, _mybir.dt.from_np(v.dtype), kind="ExternalInput").ap() for n, v in arrays.items()]
    args.append(nc.dram_tensor("out", (128, C * W), _mybir.dt.float32, kind="ExternalOutput").ap())
    audio_tower(nc, *args)
    r = _run(nc, [arrays], core_ids=[0])
    o = r.results[0]["out"]
    return np.ascontiguousarray(o.reshape(2, D, B // 2, T).transpose(0, 2, 3, 1).reshape(B, T, D))
```
